# Optimizing a Trainium2 kernel written in Bass

```python
import numpy as np
import jax
import jax.numpy as jnp

def _softmax(x, axis=-1):
    return jax.nn.softmax(x, axis=axis)

def _gelu(x):
    return jax.nn.gelu(x, approximate=True)

def _silu(x):
    return jax.nn.silu(x)

def _sigmoid(x):
    return jax.nn.sigmoid(x)

def _layernorm(x, axis=-1, eps=1e-05):
    m = jnp.mean(x, axis=axis, keepdims=True)
    v = jnp.var(x, axis=axis, keepdims=True)
    return (x - m) / jnp.sqrt(v + eps)

def _scatter_add(tgt, idx, src, axis=0):
    return tgt.at[idx].add(src)

def _segment_sum(src, seg, n):
    return jax.ops.segment_sum(src, seg, n)
kernel_name = 'mk_gnn_resnorm_d4_gnn_r32_c166bd'

def setup_inputs(seed: int=0):
    np.random.seed(seed)
    _w = jnp.asarray

    def _rec_inputs():
        import jax
        import jax.numpy as jnp
        _gk = jax.random.key(seed)
        x = -0.0001006 + 1 * jax.random.normal(jax.random.fold_in(_gk, 1), (3125, 96), jnp.float32)
        _s = jax.random.randint(jax.random.fold_in(_gk, 2), (50000,), 0, 3125, jnp.int32)
        _d = jax.random.randint(jax.random.fold_in(_gk, 3), (50000,), 0, 3125, jnp.int32)
        _loop = jnp.arange(3125, dtype=jnp.int32)
        src = jnp.concatenate([_s, _d, _loop])
        dst = jnp.concatenate([_d, _s, _loop])
        _o = jnp.argsort(dst, stable=True)
        src = src[_o]
        dst = dst[_o]
        edge_attr_32 = 0.000196303 + 1.00016 * jax.random.normal(jax.random.fold_in(_gk, 12), (103125, 32), jnp.float32)
        return (x, src, dst, edge_attr_32)
    x, src, dst, edge_attr_32 = _rec_inputs()

    def _L0_gnn_setup():
        import jax, jax.numpy as jnp
        import numpy as np
        N_NODES = 50000
        N_EDGES = 25000
        DIM = 96
        HEADS = 4
        LAYERS = 3
        NEG_SLOPE = 0.2

        def _gat_layer(x, src, dst, W, a_src, a_dst, b):
            N = x.shape[0]
            H, C = a_src.shape
            h = (x @ W).reshape(N, H, C)
            alpha_s = jnp.einsum('nhc,hc->nh', h, a_src)
            alpha_d = jnp.einsum('nhc,hc->nh', h, a_dst)
            e = jax.nn.leaky_relu(alpha_s[src] + alpha_d[dst], NEG_SLOPE)
            m = jax.ops.segment_max(e, dst, num_segments=N)
            m = jnp.where(jnp.isfinite(m), m, 0.0)
            ex = jnp.exp(e - m[dst])
            den = jax.ops.segment_sum(ex, dst, num_segments=N)
            alpha = ex / (den[dst] + 1e-16)
            msg = h[src] * alpha[:, :, None]
            out = jax.ops.segment_sum(msg, dst, num_segments=N)
            return out.reshape(N, H * C) + b
        key = jax.random.key(seed)
        ks = jax.random.split(key, 6)
        C = DIM // HEADS
        x = jax.random.normal(ks[0], (N_NODES, DIM), dtype=jnp.float32)
        edge_index = jax.random.randint(ks[1], (2, N_EDGES), 0, N_NODES, dtype=jnp.int32)
        W = jax.random.normal(ks[2], (LAYERS, DIM, DIM), dtype=jnp.float32) * (1.0 / np.sqrt(DIM))
        att_src = jax.random.normal(ks[3], (LAYERS, HEADS, C), dtype=jnp.float32) * (1.0 / np.sqrt(C))
        att_dst = jax.random.normal(ks[4], (LAYERS, HEADS, C), dtype=jnp.float32) * (1.0 / np.sqrt(C))
        bias = jnp.zeros((LAYERS, DIM), dtype=jnp.float32)
        return {'x': x, 'edge_index': edge_index, 'W': W, 'att_src': att_src, 'att_dst': att_dst, 'bias': bias}
    _L0_gnn_all = _L0_gnn_setup()
    _L0_gnn_in = {k: v for k, v in _L0_gnn_all.items() if k in ('W', 'att_src', 'att_dst', 'bias')}
    del _L0_gnn_all

    def _L1_gnn_setup():
        import jax, jax.numpy as jnp
        import numpy as np
        N, E, D = (50000, 25000, 96)
        BN_EPS = 1e-05
        key = jax.random.key(seed)
        ks = jax.random.split(key, 10)
        feature = jax.random.normal(ks[0], (N, D), dtype=jnp.float32)
        src = jax.random.randint(ks[1], (E,), 0, N, dtype=jnp.int32)
        dst = jax.random.randint(ks[2], (E,), 0, N, dtype=jnp.int32)
        W1 = jax.random.normal(ks[3], (D, D), dtype=jnp.float32) / np.sqrt(D)
        b1 = jnp.zeros((D,), dtype=jnp.float32)
        W2 = jax.random.normal(ks[4], (D, D), dtype=jnp.float32) / np.sqrt(D)
        b2 = jnp.zeros((D,), dtype=jnp.float32)
        gamma = jnp.ones((D,), dtype=jnp.float32)
        beta = jnp.zeros((D,), dtype=jnp.float32)
        eps = jnp.zeros((1,), dtype=jnp.float32)
        return {'feature': feature, 'src': src, 'dst': dst, 'W1': W1, 'b1': b1, 'W2': W2, 'b2': b2, 'gamma': gamma, 'beta': beta, 'eps': eps}
    _L1_gnn_all = _L1_gnn_setup()
    _L1_gnn_in = {k: v for k, v in _L1_gnn_all.items() if k in ('W1', 'b1', 'W2', 'b2', 'gamma', 'beta', 'eps')}
    del _L1_gnn_all

    def _L2_gnn_setup():
        import jax, jax.numpy as jnp
        import numpy as np
        N_NODES = 50000
        N_EDGES = 25000
        D_MODEL = 96
        HEADS = 4
        key = jax.random.key(seed)
        ks = jax.random.split(key, 6)
        scale = 1.0 / np.sqrt(D_MODEL)
        return {'embeds': jax.random.normal(ks[0], (N_NODES, D_MODEL), dtype=jnp.float32), 'qW': jax.random.normal(ks[1], (D_MODEL, D_MODEL), dtype=jnp.float32) * scale, 'kW': jax.random.normal(ks[2], (D_MODEL, D_MODEL), dtype=jnp.float32) * scale, 'vW': jax.random.normal(ks[3], (D_MODEL, D_MODEL), dtype=jnp.float32) * scale, 'rows': jax.random.randint(ks[4], (N_EDGES,), 0, N_NODES, dtype=jnp.int32), 'cols': jax.random.randint(ks[5], (N_EDGES,), 0, N_NODES, dtype=jnp.int32)}
    _L2_gnn_all = _L2_gnn_setup()
    _L2_gnn_in = {k: v for k, v in _L2_gnn_all.items() if k in ('qW', 'kW', 'vW')}
    del _L2_gnn_all

    def _L3_gnn_setup():
        import jax, jax.numpy as jnp
        import numpy as np
        N_NODES = 50000
        N_EDGES = 25000
        IN_DIM = 96
        OUT_DIM = 96
        EDGE_DIM = 32
        BN_EPS = 1e-05
        key = jax.random.key(seed)
        ks = jax.random.split(key, 12)
        x = jax.random.normal(ks[0], (N_NODES, IN_DIM), dtype=jnp.float32)
        edge_index = jax.random.randint(ks[1], (2, N_EDGES), 0, N_NODES, dtype=jnp.int64)
        edge_attr = jax.random.normal(ks[2], (N_EDGES, EDGE_DIM), dtype=jnp.float32)
        We = jax.random.normal(ks[3], (EDGE_DIM, IN_DIM), dtype=jnp.float32) / np.sqrt(EDGE_DIM)
        be = jnp.zeros((IN_DIM,), dtype=jnp.float32)
        W1 = jax.random.normal(ks[4], (IN_DIM, OUT_DIM), dtype=jnp.float32) / np.sqrt(IN_DIM)
        b1 = jnp.zeros((OUT_DIM,), dtype=jnp.float32)
        W2 = jax.random.normal(ks[5], (OUT_DIM, OUT_DIM), dtype=jnp.float32) / np.sqrt(OUT_DIM)
        b2 = jnp.zeros((OUT_DIM,), dtype=jnp.float32)
        gamma = jnp.ones((OUT_DIM,), dtype=jnp.float32)
        beta = jnp.zeros((OUT_DIM,), dtype=jnp.float32)
        return {'x': x, 'edge_index': edge_index, 'edge_attr': edge_attr, 'We': We, 'be': be, 'W1': W1, 'b1': b1, 'W2': W2, 'b2': b2, 'gamma': gamma, 'beta': beta}
    _L3_gnn_all = _L3_gnn_setup()
    _L3_gnn_in = {k: v for k, v in _L3_gnn_all.items() if k in ('We', 'be', 'W1', 'b1', 'W2', 'b2', 'gamma', 'beta')}
    del _L3_gnn_all
    return {'x': x, 'src': src, 'dst': dst, 'edge_attr_32': edge_attr_32, 'L0_gnn_W': _L0_gnn_in['W'], 'L0_gnn_att_src': _L0_gnn_in['att_src'], 'L0_gnn_att_dst': _L0_gnn_in['att_dst'], 'L0_gnn_bias': _L0_gnn_in['bias'], 'L1_gnn_W1': _L1_gnn_in['W1'], 'L1_gnn_b1': _L1_gnn_in['b1'], 'L1_gnn_W2': _L1_gnn_in['W2'], 'L1_gnn_b2': _L1_gnn_in['b2'], 'L1_gnn_gamma': _L1_gnn_in['gamma'], 'L1_gnn_beta': _L1_gnn_in['beta'], 'L1_gnn_eps': _L1_gnn_in['eps'], 'L2_gnn_qW': _L2_gnn_in['qW'], 'L2_gnn_kW': _L2_gnn_in['kW'], 'L2_gnn_vW': _L2_gnn_in['vW'], 'L3_gnn_We': _L3_gnn_in['We'], 'L3_gnn_be': _L3_gnn_in['be'], 'L3_gnn_W1': _L3_gnn_in['W1'], 'L3_gnn_b1': _L3_gnn_in['b1'], 'L3_gnn_W2': _L3_gnn_in['W2'], 'L3_gnn_b2': _L3_gnn_in['b2'], 'L3_gnn_gamma': _L3_gnn_in['gamma'], 'L3_gnn_beta': _L3_gnn_in['beta']}

def reference(x, src, dst, edge_attr_32, L0_gnn_W, L0_gnn_att_src, L0_gnn_att_dst, L0_gnn_bias, L1_gnn_W1, L1_gnn_b1, L1_gnn_W2, L1_gnn_b2, L1_gnn_gamma, L1_gnn_beta, L1_gnn_eps, L2_gnn_qW, L2_gnn_kW, L2_gnn_vW, L3_gnn_We, L3_gnn_be, L3_gnn_W1, L3_gnn_b1, L3_gnn_W2, L3_gnn_b2, L3_gnn_gamma, L3_gnn_beta):
    import jax
    import jax.numpy as jnp

    def _L0_gnn_ref(x, edge_index, W, att_src, att_dst, bias):
        import jax, jax.numpy as jnp
        import numpy as np
        N_NODES = 50000
        N_EDGES = 25000
        DIM = 96
        HEADS = 4
        LAYERS = 3
        NEG_SLOPE = 0.2

        def _gat_layer(x, src, dst, W, a_src, a_dst, b):
            N = x.shape[0]
            H, C = a_src.shape
            h = (x @ W).reshape(N, H, C)
            alpha_s = jnp.einsum('nhc,hc->nh', h, a_src)
            alpha_d = jnp.einsum('nhc,hc->nh', h, a_dst)
            e = jax.nn.leaky_relu(alpha_s[src] + alpha_d[dst], NEG_SLOPE)
            m = jax.ops.segment_max(e, dst, num_segments=N)
            m = jnp.where(jnp.isfinite(m), m, 0.0)
            ex = jnp.exp(e - m[dst])
            den = jax.ops.segment_sum(ex, dst, num_segments=N)
            alpha = ex / (den[dst] + 1e-16)
            msg = h[src] * alpha[:, :, None]
            out = jax.ops.segment_sum(msg, dst, num_segments=N)
            return out.reshape(N, H * C) + b
        src = edge_index[0]
        dst = edge_index[1]
        for l in range(W.shape[0]):
            x = jax.nn.relu(_gat_layer(x, src, dst, W[l], att_src[l], att_dst[l], bias[l]))
        return x

    def _L1_gnn_ref(feature, src, dst, W1, b1, W2, b2, gamma, beta, eps):
        import jax, jax.numpy as jnp
        import numpy as np
        N, E, D = (50000, 25000, 96)
        BN_EPS = 1e-05
        n_nodes = feature.shape[0]
        pooled = jax.ops.segment_sum(feature[src], dst, num_segments=n_nodes)
        pooled = pooled + (1.0 + eps[0]) * feature
        h = jax.nn.relu(pooled @ W1 + b1) @ W2 + b2
        mean = jnp.mean(h, axis=0)
        var = jnp.var(h, axis=0)
        h = (h - mean) * jax.lax.rsqrt(var + BN_EPS) * gamma + beta
        return jax.nn.relu(h)

    def _L2_gnn_ref(embeds, qW, kW, vW, rows, cols):
        import jax, jax.numpy as jnp
        import numpy as np
        N_NODES = 50000
        N_EDGES = 25000
        D_MODEL = 96
        HEADS = 4
        nvar, d = embeds.shape
        dh = d // HEADS
        e = rows.shape[0]
        q = (embeds[rows] @ qW).reshape(e, HEADS, dh)
        k = (embeds[cols] @ kW).reshape(e, HEADS, dh)
        v = (embeds[cols] @ vW).reshape(e, HEADS, dh)
        scores = jnp.clip(jnp.einsum('ehd,ehd->eh', q, k), -10.0, 10.0)
        exp_s = jnp.exp(scores)
        norms = jax.ops.segment_sum(exp_s, rows, num_segments=nvar)[rows]
        w = exp_s / (norms + 1e-08)
        res = jax.ops.segment_sum(w[:, :, None] * v, rows, num_segments=nvar).reshape(nvar, d)
        return embeds + res

    def _L3_gnn_ref(x, edge_index, edge_attr, We, be, W1, b1, W2, b2, gamma, beta):
        import jax, jax.numpy as jnp
        import numpy as np
        N_NODES = 50000
        N_EDGES = 25000
        IN_DIM = 96
        OUT_DIM = 96
        EDGE_DIM = 32
        BN_EPS = 1e-05
        src = edge_index[0]
        dst = edge_index[1]
        msg = jax.nn.relu(x[src] + edge_attr @ We + be)
        aggr = jax.ops.segment_sum(msg, dst, num_segments=x.shape[0])
        h = x + aggr
        h = jax.nn.relu(h @ W1 + b1) @ W2 + b2
        mean = jnp.mean(h, axis=0)
        var = jnp.mean(jnp.square(h - mean), axis=0)
        h = (h - mean) * jax.lax.rsqrt(var + BN_EPS) * gamma + beta
        return jax.nn.relu(h)
    edge_index = jnp.stack([src, dst])
    x = _layernorm(x + _L0_gnn_ref(x, edge_index, L0_gnn_W, L0_gnn_att_src, L0_gnn_att_dst, L0_gnn_bias), axis=-1)
    x = _layernorm(x + _L1_gnn_ref(x, src, dst, L1_gnn_W1, L1_gnn_b1, L1_gnn_W2, L1_gnn_b2, L1_gnn_gamma, L1_gnn_beta, L1_gnn_eps), axis=-1)
    x = _layernorm(x + _L2_gnn_ref(x, L2_gnn_qW, L2_gnn_kW, L2_gnn_vW, src, dst), axis=-1)
    x = _layernorm(x + _L3_gnn_ref(x, edge_index, edge_attr_32, L3_gnn_We, L3_gnn_be, L3_gnn_W1, L3_gnn_b1, L3_gnn_W2, L3_gnn_b2, L3_gnn_gamma, L3_gnn_beta), axis=-1)
    return x

_drawn_inputs = setup_inputs


def setup_inputs(seed=0):
    import zlib

    import numpy as np

    out = dict(_drawn_inputs(seed))
    spreads = {'L0_gnn_bias': (0.0, 0.1),
     'L1_gnn_b1': (0.0, 0.742),
     'L1_gnn_b2': (0.0, 0.8),
     'L1_gnn_gamma': (1.0, 0.2),
     'L1_gnn_beta': (0.0, 0.1),
     'L3_gnn_be': (0.0, 0.1),
     'L3_gnn_b1': (0.0, 0.8),
     'L3_gnn_b2': (0.0, 0.8),
     'L3_gnn_gamma': (1.0, 0.2),
     'L3_gnn_beta': (0.0, 0.1)}
    factors = {'L0_gnn_att_dst': 8.0}
    for name, (base, spread) in spreads.items():
        noise = np.random.default_rng([zlib.crc32(name.encode()), seed]).standard_normal(out[name].shape)
        drawn = base * np.exp(spread * noise) if base else spread * noise
        out[name] = jnp.asarray(drawn.astype(out[name].dtype))
    for name, factor in factors.items():
        out[name] = (out[name] * factor).astype(out[name].dtype)
    return out
```

```python
import concourse.bass as bass
from concourse import mybir
from contextlib import ExitStack

N, D, E, ED, HEADS, LAYERS = 3125, 96, 103125, 32, 4, 3
DH = D // HEADS
P = 128
NT = -(-N // P)
NP = NT * P
NFULL = N // P
NREST = N - NFULL * P
ET = -(-E // P)
EREST = E - (P - 1) * ET
G = 13
NG = ET // G
BT = 5
NB = NT // BT
BW = BT * P
HW = BW // 2
VW = 32
UNITS = NT * HEADS
W_BUFS = 6
KA = 4
LN_EPS = BN_EPS = 1e-5
SLOPE = 0.2

f32, bf16, i32 = mybir.dt.float32, mybir.dt.bfloat16, mybir.dt.int32
ALU = mybir.AluOpType
ACT = mybir.ActivationFunctionType
AX = mybir.AxisListType


def bcast_rows(ap, n):
    return ap.unsqueeze(0).to_broadcast([n, ap.shape[0]])


class Chain:

    def __init__(self, eng, sem, base=0):
        self.eng, self.sem, self.base, self.n = eng, sem, base, 0

    def __call__(self, instruction):
        instruction.then_inc(self.sem, 1)
        self.n += 1
        self.eng.wait_ge(self.sem, self.base + self.n)


def wait(eng, sem, value):
    if not isinstance(value, int) or value > 0:
        eng.wait_ge(sem, value)


def held(eng, turn, sem, value):
    if not isinstance(value, int) or value > 0:
        eng.wait_ge(sem, value)
        eng.sem_inc(turn, 1)


def turns(eng, n, body):
    body(0)
    with eng.Fori(1, n) as i:
        body(i)


def program(nc, a, out):
    ctx = ExitStack()
    with ctx:
        sb = lambda n, s, d=f32: ctx.enter_context(nc.sbuf_tensor(n, s, d))

        counts = nc.dram_tensor("counts", [NP * NP + P, 1], f32)
        xtab = nc.dram_tensor("xtab", [NP, D], f32)
        aggr = [nc.dram_tensor(f"aggr{k}", [NP + P, D], f32) for k in range(KA)]
        counts_rows = counts[0:NP * NP, :].rearrange("(r c) o -> r (c o)", c=NP)

        x = sb("x", [P, NT, D])
        ident = sb("ident", [P, P])
        dst_f = sb("dst_f", [P, ET])
        src_i = sb("src_i", [P, ET], i32)
        dst_slot = sb("dst_slot", [P, ET], i32)

        build_counts(nc, a, x, ident, dst_f, src_i, dst_slot, counts)

        with ExitStack() as c2:
            y = c2.enter_context(nc.sbuf_tensor("y", [P, NT, D], f32))
            xT = c2.enter_context(nc.sbuf_tensor("xT", [D, NP], f32))
            with ExitStack() as c3:
                hx = c3.enter_context(nc.sbuf_tensor("hx", [P, NT, HEADS, VW], f32))
                att = c3.enter_context(nc.sbuf_tensor("att", [P, NT, 2 * HEADS], f32))
                shift = c3.enter_context(nc.sbuf_tensor("shift", [P, HEADS], f32))
                for layer in range(LAYERS):
                    cur = x if layer == 0 else y
                    gat_project(nc, a, layer, cur, ident, xT, hx, att, shift)
                    gat_attend(nc, a, layer, ident, hx, att, shift, counts_rows, y)
            layer_norm(nc, "n0", x, y)
            transpose_and_project(nc, "t1", x, ident, xT)
            gin_pool(nc, a, x, xT, counts_rows)
            mlp_norm(nc, a, "L1_gnn", ident, xT, y)
            layer_norm(nc, "n1", x, y)
            with ExitStack() as c3:
                hx = c3.enter_context(nc.sbuf_tensor("hx2", [P, NT, HEADS, VW], f32))
                dot_attend(nc, a, x, ident, xT, hx, counts_rows, y)
            layer_norm(nc, "n2", x, y)
            edge_messages(nc, a, x, ident, dst_f, src_i, dst_slot, xtab, aggr)
            gather_sums(nc, x, y, ident, xT, aggr)
            mlp_norm(nc, a, "L3_gnn", ident, xT, y)
            layer_norm(nc, "n3", x, y)
        store(nc, x, out)


def build_counts(nc, a, x, ident, dst_f, src_i, dst_slot, counts):
    ctx = ExitStack()
    with ctx:
        ctx.enter_context(nc.cleanup_on_exit())
        sb = lambda n, s, d=f32: ctx.enter_context(nc.sbuf_tensor(n, s, d))
        sem = lambda n: nc.alloc_semaphore(n)
        ZW = NP
        NZ = NP * NP // P // ZW
        zeros = sb("zeros", [P, ZW])
        dst_i = sb("dst_i", [P, ET], i32)
        cell = sb("cell", [P, ET])
        keys = sb("keys", [P, 2, 2, G])
        cell_slot = sb("cell_slot", [P, 2, G], i32)
        cell_add = sb("cell_add", [P, 2, G])
        nlow = sb("nlow", [P, G])
        first = sb("first", [P, G])
        moved = sb("moved", [P, G])
        spare_i = sb("spare_i", [P, 2], i32)
        spare = sb("spare", [P, 2])
        earlier = sb("earlier", [P, P], bf16)
        same = sb("same", [P, G, P], bf16)
        rows = [ctx.enter_context(nc.psum_tensor(f"rows{w}", [P, 4 * 512], f32)) for w in range(2)]

        zeros_set, padded, loaded, x_padded, x_loaded = (sem(n) for n in ("zeros_set", "padded", "loaded", "x_padded", "x_loaded"))
        const_made, cells_made, keys_set, slots_ready = (sem(n) for n in ("const_made", "cells_made", "keys_set", "slots_ready"))
        rows_ready = [sem(f"rows_ready{w}") for w in range(2)]
        rows_free = [sem(f"rows_free{w}") for w in range(2)]
        converted, dve_steps, added, turn = (sem(n) for n in ("converted", "dve_steps", "added", "turn"))
        zeroed = sem("zeroed")
        ZEROED = 16 * (NZ + 1)

        with nc.Block() as block:
            @block.sync
            def _(sp):
                sp.wait_ge(zeros_set, 1)
                v = counts[0:NP * NP, :].rearrange("(p f) o -> p (f o)", p=P)
                for j in range(NZ):
                    sp.dma_start(v[:, j * ZW:(j + 1) * ZW], zeros[:]).then_inc(zeroed, 16)
                sp.dma_start(counts[NP * NP:NP * NP + P, :], zeros[:, 0:1]).then_inc(zeroed, 16)
                sp.wait_ge(x_padded, 1)
                sp.dma_start(x[:, 0:NFULL, :], a["x"][0:NFULL * P, :].rearrange("(t p) d -> p t d", p=P)).then_inc(x_loaded, 16)
                sp.dma_start(x[0:NREST, NFULL, :], a["x"][NFULL * P:N, :]).then_inc(x_loaded, 16)
                sp.wait_ge(x_loaded, 32)

            @block.scalar
            def _(act):
                act.wait_ge(padded, 2)
                for ap, t in ((a["src"], src_i), (a["dst"], dst_i)):
                    for lo, hi in ((0, 112), (112, P - 1)):
                        act.dma_start(t[lo:hi, :], ap[lo * ET:hi * ET].rearrange("(p t) -> p t", t=ET)).then_inc(loaded, 16)
                    act.dma_start(t[P - 1:P, 0:EREST], ap[(P - 1) * ET:E].rearrange("(p t) -> p t", p=1)).then_inc(loaded, 16)
                act.wait_ge(cells_made, 1)

                def copy_keys(g, half):
                    nc.scalar.activation(keys[:, half, 0, :], cell[:, bass.ds(g * G, G)], ACT.Copy)
                    nc.scalar.activation(keys[:, half, 1, :], dst_f[:, bass.ds(g * G, G)], ACT.Copy).then_inc(keys_set, 1)

                for half in range(2):
                    copy_keys(half, half)
                with act.Fori(1, NG // 2) as i:
                    for half in range(2):
                        act.wait_ge(rows_ready[1], 2 * i + half - 1)
                        act.sem_inc(turn, 1)
                        copy_keys(2 * i + half, half)

            @block.gpsimd
            def _(pool):
                nc.gpsimd.memset(ident[:], 0.0)
                nc.gpsimd.memset(earlier[:], 1.0).then_inc(const_made, 1)
                pool.wait_ge(const_made, 1)
                nc.gpsimd.affine_select(out=ident[:], in_=ident[:], compare_op=ALU.not_equal, fill=1.0, base=0, pattern=[[-1, P]], channel_multiplier=1)
                nc.gpsimd.affine_select(out=earlier[:], in_=earlier[:], compare_op=ALU.is_gt, fill=0.0, base=0, pattern=[[-1, P]], channel_multiplier=1)
                nc.gpsimd.iota(spare_i[:, 0:1], pattern=[[0, 1]], base=NP * NP, channel_multiplier=1)
                nc.gpsimd.iota(spare_i[:, 1:2], pattern=[[0, 1]], base=NP, channel_multiplier=1).then_inc(const_made, 1)
                pool.wait_ge(zeroed, ZEROED)
                with pool.Fori(0, NG // 2) as i:
                    for half in range(2):
                        pool.wait_ge(slots_ready, 2 * i + half + 1)
                        pool.sem_inc(turn, 1)
                        for j in range(G):
                            nc.gpsimd.indirect_dma_start(counts[:, :], bass.IndirectOffsetOnAxis(ap=cell_slot[:, half, j:j + 1], axis=0),
                                                         cell_add[:, half, j:j + 1], None, compute_op=ALU.add).then_inc(added, 16)
                            pool.wait_ge(added, i * (32 * G) + 16 * (half * G + j + 1))
                            pool.sem_inc(turn, 1)

            @block.vector
            def _(dve):
                nc.vector.memset(zeros[:], 0.0).then_inc(zeros_set, 1)
                for w in range(2):
                    dve.sem_inc(rows_free[w], 1)
                for t in (src_i, dst_i):
                    nc.vector.memset(t[96:P, :], NP - 1).then_inc(padded, 1)
                nc.vector.memset(x[:, NFULL, :], 0.0).then_inc(x_padded, 1)
                dve.wait_ge(loaded, 96)
                dve.wait_ge(const_made, 2)
                nc.vector.tensor_copy(spare[:], spare_i[:])
                nc.vector.tensor_copy(dst_f[:], dst_i[:])
                nc.vector.tensor_copy(cell[:], src_i[:]).then_inc(converted, 1)
                dve.wait_ge(converted, 1)
                nc.vector.scalar_tensor_tensor(cell[:], cell[:], float(NP), dst_f[:], ALU.mult, ALU.add).then_inc(cells_made, 1)
                dve.wait_ge(cells_made, 1)
                STEPS = 13

                def body(i):
                    for half in range(2):
                        g = 2 * i + half
                        group = bass.ds(g * G, G)
                        step = Chain(dve, dve_steps, i * (2 * STEPS) + half * STEPS)
                        for w, table in ((0, cell), (1, dst_f)):
                            dve.wait_ge(rows_ready[w], g + 1)
                            nc.vector.tensor_tensor(same[:], rows[w][:, 0:G * P].rearrange("p (t c) -> p t c", c=P),
                                                    table[:, group].unsqueeze(2).to_broadcast([P, G, P]), ALU.is_equal).then_inc(rows_free[w], 1)
                            dve.wait_ge(rows_free[w], g + 2)
                            if w == 0:
                                wait(dve, added, i * (32 * G) + 16 * G * (half - 1))
                                step(nc.vector.reduce_sum(cell_add[:, half, :], same[:], axis=AX.X))
                            step(nc.vector.tensor_tensor(same[:], same[:], earlier[:].unsqueeze(1).to_broadcast([P, G, P]), ALU.mult))
                            step(nc.vector.reduce_sum(nlow[:], same[:], axis=AX.X))
                            step(nc.vector.tensor_scalar(first[:], nlow[:], 0.0, None, ALU.is_equal))
                            step(nc.vector.tensor_scalar(moved[:], table[:, group], spare[:, w:w + 1], None, ALU.subtract))
                            step(nc.vector.tensor_tensor(moved[:], moved[:], first[:], ALU.mult))
                            slot = cell_slot[:, half, :] if w == 0 else dst_slot[:, group]
                            step(nc.vector.tensor_scalar(slot, moved[:], spare[:, w:w + 1], None, ALU.add))
                            if w == 0:
                                dve.sem_inc(slots_ready, 1)
                        assert step.n == STEPS

                turns(dve, NG // 2, body)

            @block.tensor
            def _(pe):
                pe.wait_ge(const_made, 2)
                with pe.Fori(0, NG // 2) as i:
                    for half in range(2):
                        g = 2 * i + half
                        pe.wait_ge(keys_set, g + 1)
                        for w in range(2):
                            pe.wait_ge(rows_free[w], g + 1)
                            for j in range(G):
                                last = nc.tensor.transpose(rows[w][:, j * P:(j + 1) * P],
                                                           keys[:, half, w, j:j + 1].to_broadcast([P, P]), ident[:])
                            last.then_inc(rows_ready[w], 1)


def transpose_and_project(nc, tag, cur, ident, xT, project=None):
    ctx = ExitStack()
    with ctx:
        ctx.enter_context(nc.cleanup_on_exit())
        sb = lambda n, s, d=f32: ctx.enter_context(nc.sbuf_tensor(tag + n, s, d))
        sem = lambda n: nc.alloc_semaphore(tag + n)
        groups = [(t, min(4, NT - t)) for t in range(0, NT, 4)]
        psT = ctx.enter_context(nc.psum_tensor(tag + "psT", [D, 2, 512], f32))
        psH = ctx.enter_context(nc.psum_tensor(tag + "psH", [P, 2, 512], f32))
        turned, evacuated, projected, kept = (sem(n) for n in ("turned", "evacuated", "projected", "kept"))
        with nc.Block() as block:
            more = project(ctx, block, sem, sb) if project else None

            @block.tensor
            def _(pe):
                for n, (t, k) in enumerate(groups):
                    if n >= 2:
                        pe.wait_ge(evacuated, n - 1)
                    for j in range(k):
                        last = nc.tensor.transpose(psT[:, n % 2, j * P:(j + 1) * P], cur[:, t + j, :], ident[:])
                    last.then_inc(turned, 1)
                if more:
                    weights, width, ready, keep = more
                    ready(pe)
                    pe.wait_ge(evacuated, len(groups))
                    for n, (t, k) in enumerate(groups):
                        if n >= 2:
                            pe.wait_ge(kept, n - 1)
                        for j in range(k):
                            last = nc.tensor.matmul(psH[:, n % 2, j * width:(j + 1) * width], xT[:, (t + j) * P:(t + j + 1) * P],
                                                    weights, start=True, stop=True)
                        last.then_inc(projected, 1)

            @block.scalar
            def _(act):
                for n, (t, k) in enumerate(groups):
                    act.wait_ge(turned, n + 1)
                    nc.scalar.activation(xT[:, t * P:(t + k) * P], psT[:, n % 2, 0:k * P], ACT.Copy).then_inc(evacuated, 1)

            if more:
                @block.vector
                def _(dve):
                    weights, width, ready, keep = more
                    keep.start(dve)
                    for n, (t, k) in enumerate(groups):
                        dve.wait_ge(projected, n + 1)
                        keep.group(psH[:, n % 2, 0:k * width].rearrange("p (t w) -> p t w", w=width), t, k).then_inc(kept, 1)
                    dve.wait_ge(kept, len(groups))
                    keep.end(dve)


class Keep:
    def __init__(self, start, group, end):
        self.start, self.group, self.end = start, group, end


def gat_project(nc, a, layer, cur, ident, xT, hx, att, shift):
    WE = D + 2 * HEADS

    def project(ctx, block, sem, sb):
        wext = sb("wext", [D, WE])
        arow = sb("arow", [D, 2, D])
        prod = sb("prod", [D, 2, D])
        neg = sb("neg", [P, HEADS])
        w_loaded, steps, weights_made, neg_made, shifted = (sem(n) for n in ("w_loaded", "steps", "weights_made", "neg_made", "shifted"))

        @block.sync
        def _(sp):
            sp.dma_start(wext[:, 0:D], a["L0_gnn_W"][layer]).then_inc(w_loaded, 16)
            for k, name in enumerate(("L0_gnn_att_src", "L0_gnn_att_dst")):
                sp.dma_start(arow[:, k, :], bcast_rows(a[name][layer].rearrange("h c -> (h c)"), D)).then_inc(w_loaded, 16)

        @block.gpsimd
        def _(pool):
            pool.wait_ge(neg_made, 1)
            nc.gpsimd.partition_all_reduce(shift[:], neg[:], P, bass.bass_isa.ReduceOp.max).then_inc(shifted, 1)
            pool.wait_ge(shifted, 1)

        def start(dve):
            dve.wait_ge(w_loaded, 48)
            step = Chain(dve, steps)
            for k in range(2):
                step(nc.vector.tensor_tensor(prod[:, k, :], wext[:, 0:D], arow[:, k, :], ALU.mult))
                nc.vector.reduce_sum(wext[:, D + k * HEADS:D + (k + 1) * HEADS], prod[:, k, :].rearrange("p (h c) -> p h c", c=DH),
                                     axis=AX.X).then_inc(weights_made, 1)
            nc.vector.memset(hx[:, :, :, DH + 1:VW], 0.0)
            step(nc.vector.memset(hx[:, :, :, DH:DH + 1], 1.0))

        def group(ps, t, k):
            for j in range(k):
                nc.vector.tensor_copy(hx[:, t + j, :, 0:DH], ps[:, j, 0:D].rearrange("p (h c) -> p h c", c=DH))
            return nc.vector.tensor_copy(att[:, t:t + k, :], ps[:, :, D:WE])

        def end(dve):
            nc.vector.tensor_reduce(neg[:], att[:, :, 0:HEADS].rearrange("p t h -> p h t"), AX.X, ALU.min).then_inc(steps, 1)
            dve.wait_ge(steps, 4)
            nc.vector.tensor_scalar(neg[:], neg[:], -1.0, None, ALU.mult).then_inc(neg_made, 1)

        return wext[:], WE, lambda pe: pe.wait_ge(weights_made, 2), Keep(start, group, end)

    transpose_and_project(nc, f"gp{layer}", cur, ident, xT, project)


def gat_attend(nc, a, layer, ident, hx, att, shift, counts_rows, y):
    ctx = ExitStack()
    tag = f"ga{layer}"
    with ctx:
        sb = lambda n, s, d=f32: ctx.enter_context(nc.sbuf_tensor(tag + n, s, d))
        sem = lambda n: nc.alloc_semaphore(tag + n)
        cnt = sb("cnt", [P, NT, BW])
        mask = sb("mask", [P, NT, BW], bf16)
        srcl = sb("srcl", [P, NT, 3, HEADS])
        top = sb("top", [P, HEADS, BW])
        tcol = sb("tcol", [P, 2, BT, HEADS])
        uv_col = sb("uv_col", [P, 2, BT, HEADS])
        uv = sb("uv", [P, 2, HEADS, BW])
        work = sb("work", [P, W_BUFS, BW])
        o_sb = sb("o_sb", [P, BW])
        rden = sb("rden", [P, BT, HEADS])
        bias = sb("bias", [P, D])
        psO = ctx.enter_context(nc.psum_tensor(tag + "psO", [P, 2, 512], f32))
        psT = ctx.enter_context(nc.psum_tensor(tag + "psT", [P, BT, 512], f32))

        cnt_loaded = [sem(f"cnt_loaded{k}") for k in range(BT)]
        bias_loaded, mask_ready, max_done, turn = (sem(n) for n in ("bias_loaded", "mask_ready", "max_done", "turn"))
        top_turned, col_steps, col_ready, row_ready, row_kept = (sem(n) for n in ("top_turned", "col_steps", "col_ready", "row_ready", "row_kept"))
        lin_ready, logit_ready, exp_ready, prob_ready, prob_used = (sem(n) for n in ("lin_ready", "logit_ready", "exp_ready", "prob_ready", "prob_used"))
        o_kept, o_turned, out_steps = (sem(n) for n in ("o_kept", "o_turned", "out_steps"))
        src_made = sem("src_made")

        with nc.Block() as block:
            @block.sync
            def _(sp):
                sp.dma_start(bias[:], bcast_rows(a["L0_gnn_bias"][layer], P)).then_inc(bias_loaded, 16)
                with sp.Fori(0, NB) as j:
                    for k in range(BT):
                        sp.wait_ge(prob_ready, j * UNITS + (k + 1) * BT * HEADS)
                        sp.dma_start(cnt[:, k * BT:(k + 1) * BT, :],
                                     counts_rows[k * BW:(k + 1) * BW, bass.ds(j * BW, BW)].rearrange("(t p) c -> p t c", p=P)
                                     ).then_inc(cnt_loaded[k], 16)

            @block.gpsimd
            def _(pool):
                with pool.Fori(0, NB) as j:
                    for s in range(NT):
                        if s % BT == 0:
                            pool.wait_ge(cnt_loaded[s // BT], 16 * j + 16)
                        pool.wait_ge(max_done, j * UNITS + (s + 1) * HEADS)
                        pool.sem_inc(turn, 1)
                        nc.gpsimd.tensor_scalar(mask[:, s, :], cnt[:, s, :], 1.0, None, ALU.min).then_inc(mask_ready, 1)

            @block.vector
            def _(dve):
                dve.sem_inc(prob_ready, UNITS)
                dve.sem_inc(max_done, UNITS)
                nc.vector.tensor_tensor(srcl[:, :, 0, :], att[:, :, 0:HEADS], shift[:].unsqueeze(1).to_broadcast([P, NT, HEADS]), ALU.add)
                nc.vector.tensor_copy(srcl[:, :, 1, :], att[:, :, 0:HEADS])
                nc.vector.tensor_scalar(srcl[:, :, 2, :], att[:, :, 0:HEADS], SLOPE, None, ALU.mult).then_inc(src_made, 1)
                dve.wait_ge(src_made, 1)
                dve.wait_ge(bias_loaded, 16)
                with dve.Fori(0, NB) as j:
                    for s in range(NT):
                        dve.wait_ge(mask_ready, j * NT + s + 1)
                        for h in range(HEADS):
                            if s == 0:
                                nc.vector.tensor_scalar(top[:, h, :], mask[:, s, :], srcl[:, s, 0, h:h + 1], None, ALU.mult).then_inc(max_done, 1)
                            else:
                                dve.wait_ge(max_done, j * UNITS + UNITS + (s - 1) * HEADS + h + 1)
                                nc.vector.scalar_tensor_tensor(top[:, h, :], mask[:, s, :], srcl[:, s, 0, h:h + 1], top[:, h, :],
                                                               ALU.mult, ALU.max).then_inc(max_done, 1)
                    dst = att[:, bass.ds(j * BT, BT), HEADS:2 * HEADS]
                    step = Chain(dve, col_steps, j * 7)
                    dve.wait_ge(top_turned, j + 1)
                    step(nc.vector.reduce_max(tcol[:, 0, :, :], psT[:, :, :].rearrange("p q (h c) -> p q h c", c=P), axis=AX.X))
                    step(nc.vector.tensor_tensor(tcol[:, 0], tcol[:, 0], shift[:].unsqueeze(1).to_broadcast([P, BT, HEADS]), ALU.subtract))
                    step(nc.vector.tensor_tensor(tcol[:, 0], tcol[:, 0], dst, ALU.add))
                    step(nc.vector.tensor_scalar(tcol[:, 1], tcol[:, 0], SLOPE, None, ALU.mult))
                    step(nc.vector.tensor_tensor(tcol[:, 0], tcol[:, 0], tcol[:, 1], ALU.max))
                    step(nc.vector.tensor_tensor(uv_col[:, 0], dst, tcol[:, 0], ALU.subtract))
                    step(nc.vector.tensor_scalar(tcol[:, 1], dst, SLOPE, None, ALU.mult))
                    assert step.n == 7
                    nc.vector.tensor_tensor(uv_col[:, 1], tcol[:, 1], tcol[:, 0], ALU.subtract).then_inc(col_ready, 1)

                    for m in range(UNITS + 2):
                        if m < UNITS:
                            s, h = divmod(m, HEADS)
                            dve.wait_ge(lin_ready, j * UNITS + m + 1)
                            w = work[:, m % W_BUFS, :]
                            nc.vector.scalar_tensor_tensor(w, uv[:, 0, h, :], srcl[:, s, 1, h:h + 1], w, ALU.add, ALU.max).then_inc(logit_ready, 1)
                        if m >= 2:
                            n = m - 2
                            s, h = divmod(n, HEADS)
                            dve.wait_ge(exp_ready, j * UNITS + n + 1)
                            w = work[:, n % W_BUFS, :]
                            nc.vector.tensor_tensor(w, w, cnt[:, s, :], ALU.mult).then_inc(prob_ready, 1)

                    dve.wait_ge(o_turned, j + 1)
                    step = Chain(dve, out_steps, j * 5)
                    o = psT[:, :, :].rearrange("p q c -> p (q c)")[:, 0:BW].rearrange("p (q h c) -> p q h c", h=HEADS, c=VW)
                    yb = y[:, bass.ds(j * BT, BT), :]
                    step(nc.vector.tensor_scalar(rden[:], o[:, :, :, DH], 1e-16, None, ALU.add))
                    step(nc.vector.reciprocal(rden[:], rden[:]))
                    for h in range(HEADS):
                        last = nc.vector.tensor_tensor(yb[:, :, h * DH:(h + 1) * DH], o[:, :, h, 0:DH],
                                                       rden[:, :, h:h + 1].to_broadcast([P, BT, DH]), ALU.mult)
                    step(last)
                    step(nc.vector.tensor_tensor(yb, yb, bias[:].unsqueeze(1).to_broadcast([P, BT, D]), ALU.add))
                    step(nc.vector.tensor_scalar(yb, yb, 0.0, None, ALU.max))

            @block.scalar
            def _(act):
                act.wait_ge(src_made, 1)
                with act.Fori(0, NB) as j:
                    for u in range(2):
                        for q in range(BT):
                            act.wait_ge(row_ready, j * (2 * BT) + u * BT + q + 1)
                            nc.scalar.activation(uv[:, u, :, q * P:(q + 1) * P], psT[:, q, :].rearrange("p (h c) -> p h c", c=P),
                                                 ACT.Copy).then_inc(row_kept, 1)
                    act.wait_ge(row_kept, j * (2 * BT) + 2 * BT)
                    for m in range(UNITS + 2):
                        if m < UNITS:
                            s, h = divmod(m, HEADS)
                            act.wait_ge(prob_used, j * UNITS + m + 1)
                            nc.scalar.activation(work[:, m % W_BUFS, :], uv[:, 1, h, :], ACT.Identity, bias=srcl[:, s, 2, h:h + 1]).then_inc(lin_ready, 1)
                        if m >= 2:
                            n = m - 2
                            act.wait_ge(logit_ready, j * UNITS + n + 1)
                            w = work[:, n % W_BUFS, :]
                            nc.scalar.activation(w, w, ACT.Exp).then_inc(exp_ready, 1)
                    act.wait_ge(prob_used, j * UNITS + UNITS + W_BUFS)
                    nc.scalar.activation(o_sb[:].rearrange("p (a c) -> p a c", a=2), psO[:, :, 0:HW], ACT.Copy).then_inc(o_kept, 1)

            @block.tensor
            def _(pe):
                pe.sem_inc(prob_used, W_BUFS)
                with pe.Fori(0, NB) as j:
                    pe.wait_ge(max_done, j * UNITS + 2 * UNITS)
                    for q in range(BT):
                        for h in range(HEADS):
                            last = nc.tensor.transpose(psT[:, q, h * P:(h + 1) * P], top[:, h, q * P:(q + 1) * P], ident[:])
                    last.then_inc(top_turned, 1)
                    pe.wait_ge(col_ready, j + 1)
                    for u in range(2):
                        for q in range(BT):
                            if u == 1:
                                pe.wait_ge(row_kept, j * (2 * BT) + q + 1)
                            for h in range(HEADS):
                                last = nc.tensor.transpose(psT[:, q, h * P:(h + 1) * P], uv_col[:, u, q, h:h + 1].to_broadcast([P, P]), ident[:])
                            last.then_inc(row_ready, 1)
                    for m in range(UNITS):
                        s, h = divmod(m, HEADS)
                        pe.wait_ge(prob_ready, j * UNITS + UNITS + m + 1)
                        for f in range(2):
                            last = nc.tensor.matmul(psO[h * VW:(h + 1) * VW, f, 0:HW], hx[:, s, h, :], work[:, m % W_BUFS, f * HW:(f + 1) * HW],
                                                    start=(s == 0), stop=(s == NT - 1), skip_group_check=True, tile_position=(0, h * VW))
                        last.then_inc(prob_used, 1)
                    pe.wait_ge(o_kept, j + 1)
                    for q in range(BT):
                        last = nc.tensor.transpose(psT[:, :, :].rearrange("p q c -> p (q c)")[:, q * P:(q + 1) * P], o_sb[:, q * P:(q + 1) * P], ident[:])
                    last.then_inc(o_turned, 1)


def layer_norm(nc, tag, x, y):
    ctx = ExitStack()
    with ctx:
        ctx.enter_context(nc.cleanup_on_exit())
        sb = lambda n, s, d=f32: ctx.enter_context(nc.sbuf_tensor(tag + n, s, d))
        sem = lambda n: nc.alloc_semaphore(tag + n)
        mean, var = sb("mean", [P, NT]), sb("var", [P, NT])
        steps, var_ready, std_ready = (sem(n) for n in ("steps", "var_ready", "std_ready"))
        with nc.Block() as block:
            @block.vector
            def _(dve):
                step = Chain(dve, steps)
                over = lambda t: t[:].unsqueeze(2).to_broadcast([P, NT, D])
                step(nc.vector.tensor_tensor(x[:], x[:], y[:], ALU.add))
                step(nc.vector.reduce_sum(mean[:], x[:], axis=AX.X))
                step(nc.vector.tensor_scalar(mean[:], mean[:], 1.0 / D, None, ALU.mult))
                step(nc.vector.tensor_tensor(x[:], x[:], over(mean), ALU.subtract))
                step(nc.vector.tensor_tensor(y[:], x[:], x[:], ALU.mult))
                step(nc.vector.reduce_sum(var[:], y[:], axis=AX.X))
                nc.vector.tensor_scalar(var[:], var[:], 1.0 / D, LN_EPS, ALU.mult, ALU.add).then_inc(var_ready, 1)
                dve.wait_ge(std_ready, 1)
                step(nc.vector.reciprocal(var[:], var[:]))
                step(nc.vector.tensor_tensor(x[:], x[:], over(var), ALU.mult))

            @block.scalar
            def _(act):
                act.wait_ge(var_ready, 1)
                nc.scalar.activation(var[:], var[:], ACT.Sqrt).then_inc(std_ready, 1)


def gin_pool(nc, a, x, xT, counts_rows):
    ctx = ExitStack()
    with ctx:
        ctx.enter_context(nc.cleanup_on_exit())
        sb = lambda n, s, d=f32: ctx.enter_context(nc.sbuf_tensor("gin" + n, s, d))
        sem = lambda n: nc.alloc_semaphore("gin" + n)
        cnt = sb("cnt", [P, NT, BW])
        eps = sb("eps", [D, 1])
        ps = ctx.enter_context(nc.psum_tensor("ginps", [D, 2, 2, 512], f32))
        cnt_loaded = [sem(f"cnt_loaded{k}") for k in range(BT)]
        eps_loaded, eps_made, used, kept = (sem(n) for n in ("eps_loaded", "eps_made", "used", "kept"))
        with nc.Block() as block:
            @block.sync
            def _(sp):
                sp.dma_start(eps[:], bcast_rows(a["L1_gnn_eps"], D)).then_inc(eps_loaded, 16)
                with sp.Fori(0, NB) as j:
                    for k in range(BT):
                        sp.wait_ge(used, j * BT + k + 1)
                        sp.dma_start(cnt[:, k * BT:(k + 1) * BT, :],
                                     counts_rows[k * BW:(k + 1) * BW, bass.ds(j * BW, BW)].rearrange("(t p) c -> p t c", p=P)
                                     ).then_inc(cnt_loaded[k], 16)

            @block.tensor
            def _(pe):
                pe.sem_inc(used, BT)
                with pe.Fori(0, NB) as j:
                    pe.wait_ge(kept, j + 1)
                    for s in range(NT):
                        if s % BT == 0:
                            pe.wait_ge(cnt_loaded[s // BT], 16 * j + 16)
                        for f in range(2):
                            last = nc.tensor.matmul(ps[:, 0, f, 0:HW], x[:, s, :], cnt[:, s, f * HW:(f + 1) * HW], start=(s == 0), stop=(s == NT - 1))
                        if s % BT == BT - 1:
                            last.then_inc(used, 1)

            @block.vector
            def _(dve):
                dve.sem_inc(kept, 1)
                dve.wait_ge(eps_loaded, 16)
                nc.vector.tensor_scalar(eps[:], eps[:], 1.0, None, ALU.add).then_inc(eps_made, 1)
                dve.wait_ge(eps_made, 1)
                with dve.Fori(0, NB) as j:
                    dve.wait_ge(used, j * BT + 2 * BT)
                    block_T = xT[:, bass.ds(j * BW, BW)].rearrange("p (f c) -> p f c", f=2)
                    nc.vector.scalar_tensor_tensor(block_T, block_T, eps[:, 0:1], ps[:, 0, :, 0:HW], ALU.mult, ALU.add).then_inc(kept, 1)


def mlp_norm(nc, a, layer, ident, xT, y):
    ctx = ExitStack()
    with ctx:
        ctx.enter_context(nc.cleanup_on_exit())
        sb = lambda n, s, d=f32: ctx.enter_context(nc.sbuf_tensor(layer + n, s, d))
        sem = lambda n: nc.alloc_semaphore(layer + n)
        w = sb("w", [D, 2, D])
        vec = sb("vec", [D, 4])
        z1, z2 = sb("z1", [D, NP]), sb("z2", [D, NP])
        stat = sb("stat", [D, 4])
        ps = [ctx.enter_context(nc.psum_tensor(f"{layer}ps{k}", [D, 2, 512], f32)) for k in range(2)]
        psY = ctx.enter_context(nc.psum_tensor(layer + "psY", [P, 2, 512], f32))
        loaded, steps, var_ready, std_ready, scaled, turned, kept = (sem(n) for n in ("loaded", "steps", "var_ready", "std_ready", "scaled", "turned", "kept"))
        multiplied = [sem(f"multiplied{k}") for k in range(2)]
        acted = [sem(f"acted{k}") for k in range(2)]
        normed = sem("normed")
        chunks = [(c, min(512, NP - c)) for c in range(0, NP, 512)]
        groups = [(t, min(4, NT - t)) for t in range(0, NT, 4)]
        with nc.Block() as block:
            @block.sync
            def _(sp):
                for k in range(2):
                    sp.dma_start(w[:, k, :], a[f"{layer}_W{k + 1}"]).then_inc(loaded, 16)
                for k, name in enumerate(("b1", "b2", "gamma", "beta")):
                    sp.dma_start(vec[:, k:k + 1], a[f"{layer}_{name}"].unsqueeze(1)).then_inc(loaded, 16)

            @block.tensor
            def _(pe):
                pe.wait_ge(loaded, 96)
                for k, src in ((0, xT), (1, z1)):
                    for n, (c, m) in enumerate(chunks):
                        if k == 1:
                            pe.wait_ge(acted[0], n + 1)
                        if n >= 2:
                            pe.wait_ge(acted[k], n - 1)
                        nc.tensor.matmul(ps[k][:, n % 2, 0:m], w[:, k, :], src[:, c:c + m], start=True, stop=True).then_inc(multiplied[k], 1)
                pe.wait_ge(normed, 1)
                for n, (t, k) in enumerate(groups):
                    if n >= 2:
                        pe.wait_ge(kept, n - 1)
                    for j in range(k):
                        last = nc.tensor.transpose(psY[:, n % 2, j * D:(j + 1) * D], z1[:, (t + j) * P:(t + j + 1) * P], ident[0:D, 0:D])
                    last.then_inc(turned, 1)

            @block.scalar
            def _(act):
                act.wait_ge(loaded, 96)
                for k, dst, func in ((0, z1, ACT.Relu), (1, z2, ACT.Identity)):
                    for n, (c, m) in enumerate(chunks):
                        act.wait_ge(multiplied[k], n + 1)
                        nc.scalar.activation(dst[:, c:c + m], ps[k][:, n % 2, 0:m], func, bias=vec[:, k:k + 1]).then_inc(acted[k], 1)
                act.wait_ge(var_ready, 1)
                nc.scalar.activation(stat[:, 2:3], stat[:, 1:2], ACT.Sqrt).then_inc(std_ready, 1)
                act.wait_ge(scaled, 1)
                nc.scalar.activation(z1[:], z2[:], ACT.Relu, bias=vec[:, 3:4], scale=stat[:, 3:4]).then_inc(normed, 1)

            @block.vector
            def _(dve):
                step = Chain(dve, steps)
                dve.wait_ge(acted[1], len(chunks))
                step(nc.vector.reduce_sum(stat[:, 0:1], z2[:, 0:N], axis=AX.X))
                step(nc.vector.tensor_scalar(stat[:, 0:1], stat[:, 0:1], 1.0 / N, None, ALU.mult))
                step(nc.vector.tensor_scalar(z2[:], z2[:], stat[:, 0:1], None, ALU.subtract))
                step(nc.vector.tensor_tensor(z1[:, 0:N], z2[:, 0:N], z2[:, 0:N], ALU.mult))
                step(nc.vector.reduce_sum(stat[:, 1:2], z1[:, 0:N], axis=AX.X))
                nc.vector.tensor_scalar(stat[:, 1:2], stat[:, 1:2], 1.0 / N, BN_EPS, ALU.mult, ALU.add).then_inc(var_ready, 1)
                dve.wait_ge(std_ready, 1)
                step(nc.vector.reciprocal(stat[:, 2:3], stat[:, 2:3]))
                nc.vector.tensor_tensor(stat[:, 3:4], stat[:, 2:3], vec[:, 2:3], ALU.mult).then_inc(scaled, 1)
                for n, (t, k) in enumerate(groups):
                    dve.wait_ge(turned, n + 1)
                    nc.vector.tensor_copy(y[:, t:t + k, :].rearrange("p t d -> p (t d)"), psY[:, n % 2, 0:k * D]).then_inc(kept, 1)


def value_project(nc, a, x, ident, xT, hx):
    def project(ctx, block, sem, sb):
        wv = sb("wv", [D, D])
        w_loaded, steps = sem("w_loaded"), sem("steps")

        @block.sync
        def _(sp):
            sp.dma_start(wv[:], a["L2_gnn_vW"]).then_inc(w_loaded, 16)

        def start(dve):
            nc.vector.memset(hx[:, :, :, DH + 1:VW], 0.0).then_inc(steps, 1)
            dve.wait_ge(steps, 1)
            nc.vector.memset(hx[:, :, :, DH:DH + 1], 1.0)

        def group(ps, t, k):
            for j in range(k):
                last = nc.vector.tensor_copy(hx[:, t + j, :, 0:DH], ps[:, j, :].rearrange("p (h c) -> p h c", c=DH))
            return last

        return wv[:], D, lambda pe: pe.wait_ge(w_loaded, 16), Keep(start, group, lambda dve: None)

    transpose_and_project(nc, "vp", x, ident, xT, project)


def dot_attend(nc, a, x, ident, xT, hx, counts_rows, y):
    value_project(nc, a, x, ident, xT, hx)
    ctx = ExitStack()
    with ctx:
        ctx.enter_context(nc.cleanup_on_exit())
        sb = lambda n, s, d=f32: ctx.enter_context(nc.sbuf_tensor("dot" + n, s, d))
        sem = lambda n: nc.alloc_semaphore("dot" + n)
        RING = 3
        wq, wk = sb("wq", [D, HEADS, VW]), sb("wk", [D, HEADS, VW])
        kT = sb("kT", [P, NP])
        qb = sb("qb", [P, BW])
        raw = sb("raw", [P, RING, BT, BW])
        cnt = sb("cnt", [P, 2, BW])
        work = sb("work", [P, W_BUFS, BW])
        o_sb = sb("o_sb", [P, BW])
        rden = sb("rden", [P, BT, HEADS])
        psS = ctx.enter_context(nc.psum_tensor("dotpsS", [P, 2, 2, 512], f32))
        psO = ctx.enter_context(nc.psum_tensor("dotpsO", [P, 2, 512], f32))
        psC = ctx.enter_context(nc.psum_tensor("dotpsC", [P, 2, 512], f32))
        raw_loaded = [sem(f"raw_loaded{k}") for k in range(RING)]
        w_cleared, w_loaded, k_ready, k_kept = (sem(n) for n in ("w_cleared", "w_loaded", "k_ready", "k_kept"))
        q_ready, q_kept, c_turned, c_kept = (sem(n) for n in ("q_ready", "q_kept", "c_turned", "c_kept"))
        s_ready, clipped, exp_ready, prob_ready, prob_used = (sem(n) for n in ("s_ready", "clipped", "exp_ready", "prob_ready", "prob_used"))
        o_kept, o_turned, out_steps, turn = (sem(n) for n in ("o_kept", "o_turned", "out_steps", "turn"))
        kchunks = [(c, min(512, NP - c)) for c in range(0, NP, 512)]
        flatC = psC[:, :, :].rearrange("p a c -> p (a c)")
        with nc.Block() as block:
            @block.sync
            def _(sp):
                sp.wait_ge(w_cleared, 1)
                for w, name in ((wq, "L2_gnn_qW"), (wk, "L2_gnn_kW")):
                    sp.dma_start(w[:, :, 0:DH], a[name].rearrange("k (h c) -> k h c", c=DH)).then_inc(w_loaded, 16)
                for j in range(NB):
                    for k in range(BT):
                        n = j * BT + k
                        if n >= RING:
                            sp.wait_ge(c_turned, (n - RING + 1) * BT)
                        sp.dma_start(raw[:, n % RING, :, :],
                                     counts_rows[j * BW:(j + 1) * BW, k * BW:(k + 1) * BW].rearrange("(t p) c -> p t c", p=P)
                                     ).then_inc(raw_loaded[n % RING], 16)

            @block.tensor
            def _(pe):
                pe.wait_ge(w_loaded, 32)
                for n, (c, m) in enumerate(kchunks):
                    if n >= 2:
                        pe.wait_ge(k_kept, n - 1)
                    nc.tensor.matmul(psS[:, 0, n % 2, 0:m], wk[:].rearrange("p h c -> p (h c)"), xT[:, c:c + m], start=True, stop=True).then_inc(k_ready, 1)
                pe.wait_ge(k_kept, len(kchunks))
                for j in range(NB):
                    if j:
                        pe.wait_ge(out_steps, 5 * j)
                    for f in range(2):
                        last = nc.tensor.matmul(psC[:, f, 0:HW], wq[:].rearrange("p h c -> p (h c)"), xT[:, j * BW + f * HW:j * BW + (f + 1) * HW], start=True, stop=True)
                    last.then_inc(q_ready, 1)
                    pe.wait_ge(q_kept, j + 1)

                    def turn_counts(s):
                        t = j * NT + s
                        n = t // BT
                        pe.wait_ge(raw_loaded[n % RING], 16 * (n // RING + 1))
                        if s:
                            pe.wait_ge(c_kept, t)
                        for q in range(BT):
                            last = nc.tensor.transpose(flatC[:, q * P:(q + 1) * P], raw[:, n % RING, q, (s % BT) * P:(s % BT + 1) * P], ident[:])
                        last.then_inc(c_turned, 1)

                    turn_counts(0)
                    LAG = 3
                    for m in range(UNITS + LAG):
                        if m < UNITS:
                            s, h = divmod(m, HEADS)
                            n = j * UNITS + m
                            if n >= 2:
                                pe.wait_ge(clipped, n - 1)
                            for f in range(2):
                                last = nc.tensor.matmul(psS[:, m % 2, f, 0:HW], kT[h * VW:(h + 1) * VW, s * P:(s + 1) * P],
                                                        qb[h * VW:(h + 1) * VW, f * HW:(f + 1) * HW], start=True, stop=True, tile_position=(h * VW, 0))
                            last.then_inc(s_ready, 1)
                            if h == HEADS - 1 and s + 1 < NT:
                                turn_counts(s + 1)
                        if m >= LAG:
                            k = m - LAG
                            s, h = divmod(k, HEADS)
                            pe.wait_ge(prob_ready, j * UNITS + k + 1)
                            for f in range(2):
                                last = nc.tensor.matmul(psO[h * VW:(h + 1) * VW, f, 0:HW], hx[:, s, h, :], work[:, k % W_BUFS, f * HW:(f + 1) * HW],
                                                        start=(s == 0), stop=(s == NT - 1), skip_group_check=True, tile_position=(0, h * VW))
                            last.then_inc(prob_used, 1)
                    pe.wait_ge(o_kept, j + 1)
                    for q in range(BT):
                        last = nc.tensor.transpose(flatC[:, q * P:(q + 1) * P], o_sb[:, q * P:(q + 1) * P], ident[:])
                    last.then_inc(o_turned, 1)

            @block.scalar
            def _(act):
                for n, (c, m) in enumerate(kchunks):
                    act.wait_ge(k_ready, n + 1)
                    nc.scalar.activation(kT[:, c:c + m], psS[:, 0, n % 2, 0:m], ACT.Copy).then_inc(k_kept, 1)
                for j in range(NB):
                    act.wait_ge(q_ready, j + 1)
                    nc.scalar.activation(qb[:].rearrange("p (f c) -> p f c", f=2), psC[:, :, 0:HW], ACT.Copy).then_inc(q_kept, 1)
                    for m in range(UNITS):
                        s, h = divmod(m, HEADS)
                        n = j * UNITS + m
                        if h == 0:
                            t = j * NT + s
                            act.wait_ge(c_turned, t + 1)
                            if t >= 2:
                                act.wait_ge(prob_ready, (t - 1) * HEADS)
                            nc.scalar.activation(cnt[:, t % 2, :], flatC[:, 0:BW], ACT.Copy).then_inc(c_kept, 1)
                        act.wait_ge(clipped, n + 1)
                        w = work[:, m % W_BUFS, :]
                        nc.scalar.activation(w, w, ACT.Exp).then_inc(exp_ready, 1)
                    act.wait_ge(prob_used, (j + 1) * UNITS)
                    nc.scalar.activation(o_sb[:].rearrange("p (f c) -> p f c", f=2), psO[:, :, 0:HW], ACT.Copy).then_inc(o_kept, 1)

            @block.vector
            def _(dve):
                nc.vector.memset(wq[:], 0.0)
                nc.vector.memset(psS[:], 0.0)
                nc.vector.memset(wk[:], 0.0).then_inc(w_cleared, 1)
                dve.wait_ge(w_cleared, 1)
                LAG = 1
                for j in range(NB):
                    for m in range(UNITS + LAG):
                        if m < UNITS:
                            n = j * UNITS + m
                            dve.wait_ge(s_ready, n + 1)
                            free = n - W_BUFS + 1 if m >= W_BUFS else j * UNITS
                            if free > 0:
                                dve.wait_ge(prob_used, free)
                            nc.vector.tensor_scalar(work[:, m % W_BUFS, :].rearrange("p (f c) -> p f c", f=2), psS[:, m % 2, :, 0:HW],
                                                    -10.0, 10.0, ALU.max, ALU.min).then_inc(clipped, 1)
                        if m >= LAG:
                            k = m - LAG
                            s = k // HEADS
                            t = j * NT + s
                            dve.wait_ge(exp_ready, j * UNITS + k + 1)
                            w = work[:, k % W_BUFS, :]
                            nc.vector.tensor_tensor(w, w, cnt[:, t % 2, :], ALU.mult).then_inc(prob_ready, 1)
                    dve.wait_ge(o_turned, j + 1)
                    step = Chain(dve, out_steps, j * 5)
                    o = flatC[:, 0:BW].rearrange("p (q h c) -> p q h c", h=HEADS, c=VW)
                    yb = y[:, j * BT:(j + 1) * BT, :]
                    step(nc.vector.tensor_scalar(rden[:], o[:, :, :, DH], 1e-8, None, ALU.add))
                    step(nc.vector.reciprocal(rden[:], rden[:]))
                    for h in range(HEADS):
                        last = nc.vector.tensor_tensor(yb[:, :, h * DH:(h + 1) * DH], o[:, :, h, 0:DH],
                                                       rden[:, :, h:h + 1].to_broadcast([P, BT, DH]), ALU.mult)
                    step(last)
                    step(nc.vector.tensor_tensor(yb, yb, x[:, j * BT:(j + 1) * BT, :], ALU.add))
                    dve.sem_inc(out_steps, 1)


def edge_messages(nc, a, x, ident, dst_f, src_i, dst_slot, xtab, aggr):
    ctx = ExitStack()
    with ctx:
        ctx.enter_context(nc.cleanup_on_exit())
        sb = lambda n, s, d=f32: ctx.enter_context(nc.sbuf_tensor("em" + n, s, d))
        sem = lambda n: nc.alloc_semaphore("em" + n)
        CH = [(0, 4), (4, 4), (8, 4), (12, 1)]
        NC = len(CH)
        xe = sb("xe", [P, NT, D])
        be = sb("be", [P, D])
        zeros = sb("zeros", [P, NT + 1, D])
        we = sb("we", [P, 4, D])
        feat = sb("feat", [P, 2, G, ED])
        featT = sb("featT", [P, 2, P])
        src_st = sb("src_st", [P, 2, G], i32)
        dst_stage = sb("dst_stage", [P, 2, G], i32)
        key_st = sb("key_st", [P, 2, G])
        xg = sb("xg", [P, 2, G, D])
        msg = sb("msg", [P, 2, 4, D])
        same = sb("same", [P, 2, 4, P])
        sums = sb("sums", [P, 2, G, D])
        ps_f = ctx.enter_context(nc.psum_tensor("emps_f", [P, 2, 512], f32))
        ps_k = ctx.enter_context(nc.psum_tensor("emps_k", [P, 2, 512], f32))
        ps_m = ctx.enter_context(nc.psum_tensor("emps_m", [P, 2, 512], f32))
        ps_s = ctx.enter_context(nc.psum_tensor("emps_s", [P, 2, 512], f32))
        be_loaded, xe_made, x_stored, we_cleared, we_loaded, z_set, z_stored = (
            sem(n) for n in ("be_loaded", "xe_made", "x_stored", "we_cleared", "we_loaded", "z_set", "z_stored"))
        feat_loaded = [sem(f"feat_loaded{h}") for h in range(2)]
        gathered = [sem(f"gathered{h}") for h in range(2)]
        added = [sem(f"added{k}") for k in range(KA)]
        feat_turned, feat_kept, key_turned, same_ready, pre_ready, pre_read, msg_ready, sum_ready, sum_kept, turn = (
            sem(n) for n in ("feat_turned", "feat_kept", "key_turned", "same_ready", "pre_ready", "pre_read", "msg_ready", "sum_ready", "sum_kept", "turn"))
        raw_ready, src_staged, dst_staged, key_staged = (sem(n) for n in ("raw_ready", "src_staged", "dst_staged", "key_staged"))
        per = [len(range(k, 2 * G, KA)) for k in range(KA)]
        FULL = EREST // G
        PART = EREST - FULL * G

        LASTI = NG // 2 - 1
        FULL_TURNS = EREST // G // 2
        assert FULL_TURNS * 2 == EREST // G

        def landed(i, half, j, k):
            return i * per[k] + len(range(k, half * G + j, KA))

        def before_last(i, half, k):
            return 16 * (i * per[k] + (len(range(k, G, KA)) - per[k] if half == 0 else 0))

        with nc.Block() as block:
            @block.sync
            def _(sp):
                sp.dma_start(be[:], bcast_rows(a["L3_gnn_be"], P)).then_inc(be_loaded, 16)
                sp.wait_ge(we_cleared, 1)
                for g in range(4):
                    sp.dma_start(we[g * ED:(g + 1) * ED, g, :], a["L3_gnn_We"]).then_inc(we_loaded, 16)
                sp.wait_ge(z_set, 1)
                for k in range(KA):
                    sp.dma_start(aggr[k][:, :].rearrange("(t p) d -> p t d", p=P), zeros[:]).then_inc(z_stored, 16)
                sp.wait_ge(xe_made, 1)
                sp.dma_start(xtab[:, :].rearrange("(t p) d -> p t d", p=P), xe[:]).then_inc(x_stored, 16)
                flat = a["edge_attr_32"].rearrange("e k -> (e k)")
                most = flat[0:(P - 1) * ET * ED].rearrange("(p f) -> p f", f=ET * ED)
                rest = flat[(P - 1) * ET * ED:E * ED].rearrange("(p f) -> p f", p=1)

                def load(i, half, last_group, n):
                    sp.wait_ge(feat_turned, i * (2 * NC) + (half + 1) * NC)
                    dst = feat[:, half, :, :].rearrange("p t k -> p (t k)")
                    for lo, hi in ((0, 112), (112, P - 1)):
                        sp.dma_start(dst[lo:hi, :], most[lo:hi, bass.ds((2 * i + half) * (G * ED), G * ED)]).then_inc(feat_loaded[half], 16)
                    sp.dma_start(dst[P - 1:P, 0:n * ED], rest[:, bass.ds(last_group * (G * ED), n * ED)]).then_inc(feat_loaded[half], 16)

                with sp.Fori(0, FULL_TURNS) as i:
                    for half in range(2):
                        load(i, half, 2 * i + half, G)
                for i in range(FULL_TURNS, NG // 2):
                    for half in range(2):
                        g = 2 * i + half
                        n = min(G, EREST - g * G)
                        load(i, half, g if n > 0 else 0, n if n > 0 else G)

            @block.gpsimd
            def _(pool):
                def gather(i, half, j, staging=src_st):
                    nc.gpsimd.indirect_dma_start(xg[:, half, j, :], None, xtab[:, :],
                                                 bass.IndirectOffsetOnAxis(ap=src_st[:, half, j:j + 1], axis=0)).then_inc(gathered[half], 16)

                def body(i, last=False):
                    for half in range(2):
                        g = 2 * i + half
                        ahead = not (last and half == 1)
                        if ahead:
                            held(pool, turn, src_staged, g + 2)
                            held(pool, turn, raw_ready, 4 * g)
                        held(pool, turn, dst_staged, g + 1)
                        for c, (lo, n) in enumerate(CH):
                            for j in range(lo, lo + n):
                                if ahead:
                                    gather(i, 1 - half, j)
                                if j == lo:
                                    held(pool, turn, sum_kept, NC * g + c + 1)
                                k = (half * G + j) % KA
                                held(pool, turn, added[k], 16 * landed(i, half, j, k))
                                nc.gpsimd.indirect_dma_start(aggr[k][:, :], bass.IndirectOffsetOnAxis(ap=dst_stage[:, half, j:j + 1], axis=0),
                                                             sums[:, half, j, :], None, compute_op=ALU.add).then_inc(added[k], 16)

                pool.wait_ge(x_stored, 16)
                pool.wait_ge(z_stored, 16 * KA)
                pool.wait_ge(src_staged, 1)
                for j in range(G):
                    gather(0, 0, j)
                body(0)
                with pool.Fori(1, LASTI) as i:
                    body(i)
                body(LASTI, last=True)
                for k in range(KA):
                    pool.wait_ge(added[k], 16 * per[k] * (NG // 2))

            @block.scalar
            def _(act):
                def body(i):
                    for half in range(2):
                        for c, (lo, n) in enumerate(CH):
                            u, v = c % 2, 2 * NC * i + half * NC + c
                            act.wait_ge(feat_turned, v + 2 * NC + 1)
                            wait(act, pre_ready, v - 1)
                            nc.scalar.activation(featT[0:n * ED, u, :], ps_f[0:n * ED, u, 0:P], ACT.Copy).then_inc(feat_kept, 1)
                            act.wait_ge(raw_ready, v + 1)
                            nc.scalar.activation(msg[:, u, 0:n, :], msg[:, u, 0:n, :], ACT.Relu).then_inc(msg_ready, 1)
                            if c == 0:
                                for k in range(KA):
                                    wait(act, added[k], before_last(i, half, k))
                            act.wait_ge(sum_ready, v + 1)
                            nc.scalar.activation(sums[:, half, lo:lo + n, :].rearrange("p t d -> p (t d)"), ps_s[:, u, 0:n * D], ACT.Copy).then_inc(sum_kept, 1)

                turns(act, NG // 2, body)

            @block.vector
            def _(dve):
                dve.sem_inc(feat_turned, 2 * NC)
                nc.vector.memset(zeros[:], 0.0).then_inc(z_set, 1)
                nc.vector.memset(we[:], 0.0).then_inc(we_cleared, 1)
                dve.wait_ge(be_loaded, 16)
                nc.vector.tensor_tensor(xe[:], x[:], be[:].unsqueeze(1).to_broadcast([P, NT, D]), ALU.add).then_inc(xe_made, 1)
                for half in range(2):
                    nc.vector.tensor_copy(src_st[:, half, :], src_i[:, half * G:(half + 1) * G]).then_inc(src_staged, 1)

                def body(i, last=False):
                    for half in range(2):
                        g = 2 * i + half
                        group = bass.ds(g * G, G)
                        held(dve, turn, key_turned, NC * (g - 1) if not isinstance(g, int) or g > 1 else 0)
                        nc.vector.tensor_copy(key_st[:, half, :], dst_f[:, group]).then_inc(key_staged, 1)
                        for k in range(KA):
                            held(dve, turn, added[k], before_last(i, half, k))
                        nc.vector.tensor_copy(dst_stage[:, half, :], dst_slot[:, group]).then_inc(dst_staged, 1)
                        dve.wait_ge(key_staged, g + 1)
                        for c, (lo, n) in enumerate(CH):
                            u, v = c % 2, 2 * NC * i + half * NC + c
                            dve.wait_ge(key_turned, v + 1)
                            wait(dve, sum_ready, v - 1)
                            nc.vector.tensor_tensor(same[:, u, 0:n, :], ps_k[:, u, 0:n * P].rearrange("p (t c) -> p t c", c=P),
                                                    key_st[:, half, lo:lo + n].unsqueeze(2).to_broadcast([P, n, P]), ALU.is_equal).then_inc(same_ready, 1)
                            if c == 0:
                                dve.wait_ge(gathered[half], (16 * G) * i + 16 * G)
                            dve.wait_ge(pre_ready, v + 1)
                            nc.vector.tensor_tensor(msg[:, u, 0:n, :], ps_m[:, u, 0:n * D].rearrange("p (t d) -> p t d", d=D),
                                                    xg[:, half, lo:lo + n, :], ALU.add).then_inc(raw_ready, 1)
                        if not last:
                            nc.vector.tensor_copy(src_st[:, half, :], src_i[:, bass.ds((g + 2) * G, G)]).then_inc(src_staged, 1)

                body(0)
                with dve.Fori(1, LASTI) as i:
                    body(i)
                body(LASTI, last=True)

            @block.tensor
            def _(pe):
                pe.wait_ge(we_loaded, 64)

                def body(i):
                    for half in range(2):
                        g = 2 * i + half
                        for c, (lo, n) in enumerate(CH):
                            u, v = c % 2, 2 * NC * i + half * NC + c
                            if c == 0:
                                pe.wait_ge(feat_loaded[half], 48 * i + 48)
                                pe.wait_ge(key_staged, g + 1)
                            wait(pe, feat_kept, v - 1)
                            nc.tensor.transpose(ps_f[0:n * ED, u, 0:P], feat[:, half, lo:lo + n, :].rearrange("p t k -> p (t k)"), ident[:]).then_inc(feat_turned, 1)
                            wait(pe, same_ready, v - 1)
                            for j in range(n):
                                last = nc.tensor.transpose(ps_k[:, u, j * P:(j + 1) * P], key_st[:, half, lo + j:lo + j + 1].to_broadcast([P, P]), ident[:])
                            last.then_inc(key_turned, 1)
                            pe.wait_ge(feat_kept, v + 1)
                            wait(pe, raw_ready, v - 1)
                            nc.tensor.matmul(ps_m[:, u, 0:n * D], featT[0:n * ED, u, :], we[0:n * ED, 0:n, :].rearrange("p t d -> p (t d)"),
                                             start=True, stop=True).then_inc(pre_ready, 1)
                            pe.wait_ge(same_ready, v + 1)
                            pe.wait_ge(msg_ready, v + 1)
                            wait(pe, sum_kept, v - 1)
                            for j in range(n):
                                last = nc.tensor.matmul(ps_s[:, u, j * D:(j + 1) * D], same[:, u, j, :], msg[:, u, j, :], start=True, stop=True)
                            last.then_inc(sum_ready, 1)

                turns(pe, NG // 2, body)


def gather_sums(nc, x, y, ident, xT, aggr):
    ctx = ExitStack()
    with ctx:
        ctx.enter_context(nc.cleanup_on_exit())
        part = ctx.enter_context(nc.sbuf_tensor("part", [P, KA, NT, D], f32))
        loaded, steps = (nc.alloc_semaphore(n) for n in ("parts_loaded", "part_steps"))
        with nc.Block() as block:
            @block.sync
            def _(sp):
                for k in range(KA):
                    sp.dma_start(part[:, k, :, :], aggr[k][0:NP, :].rearrange("(t p) d -> p t d", p=P)).then_inc(loaded, 16)

            @block.vector
            def _(dve):
                dve.wait_ge(loaded, 16 * KA)
                step = Chain(dve, steps)
                step(nc.vector.tensor_tensor(y[:], x[:], part[:, 0], ALU.add))
                for k in range(1, KA):
                    step(nc.vector.tensor_tensor(y[:], y[:], part[:, k], ALU.add))
    transpose_and_project(nc, "gs", y, ident, xT)


def store(nc, x, out):
    with nc.semaphore("stored") as stored, nc.Block() as block:
        @block.sync
        def _(sp):
            sp.dma_start(out[0:NFULL * P, :].rearrange("(t p) d -> p t d", p=P), x[:, 0:NFULL, :]).then_inc(stored, 16)
            sp.dma_start(out[NFULL * P:N, :], x[0:NREST, NFULL, :]).then_inc(stored, 16)
            sp.wait_ge(stored, 32)


_INS = ['x', 'src', 'dst', 'edge_attr_32', 'L0_gnn_W', 'L0_gnn_att_src', 'L0_gnn_att_dst', 'L0_gnn_bias',
        'L1_gnn_W1', 'L1_gnn_b1', 'L1_gnn_W2', 'L1_gnn_b2', 'L1_gnn_gamma', 'L1_gnn_beta', 'L1_gnn_eps',
        'L2_gnn_qW', 'L2_gnn_kW', 'L2_gnn_vW', 'L3_gnn_We', 'L3_gnn_be', 'L3_gnn_W1', 'L3_gnn_b1',
        'L3_gnn_W2', 'L3_gnn_b2', 'L3_gnn_gamma', 'L3_gnn_beta']


def kernel(**inputs):
    import numpy as _np
    import concourse.bacc as _bacc
    from concourse import mybir as _mybir
    from concourse.bass_utils import run_bass_kernel_spmd as _run

    nc = _bacc.Bacc("TRN2", target_bir_lowering=False, num_devices=1)
    arrays, args = {}, {}
    for name in _INS:
        a = _np.ascontiguousarray(inputs[name])
        arrays[f"in_{name}_dram"] = a
        args[name] = nc.dram_tensor(f"in_{name}_dram", a.shape, _mybir.dt.from_np(a.dtype), kind="ExternalInput").ap()
    out = nc.dram_tensor("out_dram", (N, D), _mybir.dt.float32, kind="ExternalOutput").ap()
    program(nc, args, out)
    r = _run(nc, [arrays], core_ids=[0])
    return r.results[0]["out_dram"]
```

```python
import concourse.bass as bass
from concourse import mybir
from contextlib import ExitStack

N, D, E, ED, HEADS, LAYERS = 3125, 96, 103125, 32, 4, 3
DH = D // HEADS
P = 128
NT = -(-N // P)
NP = NT * P
NFULL = N // P
NREST = N - NFULL * P
ET = -(-E // P)
EREST = E - (P - 1) * ET
G = 13
NG = ET // G
BT = 5
NB = NT // BT
BW = BT * P
HW = BW // 2
VW = 32
VC = DH + 1
UNITS = NT * HEADS
W_BUFS = 6
KA = 4
LN_EPS = BN_EPS = 1e-5
SLOPE = 0.2
BIG = 1e30

f32, bf16, i32 = mybir.dt.float32, mybir.dt.bfloat16, mybir.dt.int32
ALU = mybir.AluOpType
ACT = mybir.ActivationFunctionType
AX = mybir.AxisListType


def bcast_rows(ap, n):
    return ap.unsqueeze(0).to_broadcast([n, ap.shape[0]])


class Chain:

    def __init__(self, eng, sem, base=0):
        self.eng, self.sem, self.base, self.n = eng, sem, base, 0

    def __call__(self, instruction):
        instruction.then_inc(self.sem, 1)
        self.n += 1
        self.eng.wait_ge(self.sem, self.base + self.n)


def wait(eng, sem, value):
    if not isinstance(value, int) or value > 0:
        eng.wait_ge(sem, value)


def held(eng, turn, sem, value):
    if not isinstance(value, int) or value > 0:
        eng.wait_ge(sem, value)
        eng.sem_inc(turn, 1)


def turns(eng, n, body):
    body(0)
    with eng.Fori(1, n) as i:
        body(i)


def program(nc, a, out):
    ctx = ExitStack()
    with ctx:
        sb = lambda n, s, d=f32: ctx.enter_context(nc.sbuf_tensor(n, s, d))

        counts = [nc.dram_tensor(f"counts{w}", [NP * NP + P, 1], f32) for w in range(2)]
        xtab = nc.dram_tensor("xtab", [NP, D], f32)
        aggr = [nc.dram_tensor(f"aggr{k}", [NP + P, D], f32) for k in range(KA)]
        edge_rows = nc.dram_tensor("edge_rows", [NP, NP], bf16)
        halves_rows = [c[0:NP * NP, :].rearrange("(r c) o -> r (c o)", c=NP) for c in counts]
        counts_rows = halves_rows[0]

        tables = {"dst_f": nc.dram_tensor("dst_f_kept", [P, ET], f32), "src_i": nc.dram_tensor("src_i_kept", [P, ET], i32),
                  "dst_slot": nc.dram_tensor("dst_slot_kept", [P, ET], i32)}

        x = sb("x", [P, NT, D])
        ident = sb("ident", [P, P])
        build_counts(nc, a, x, ident, counts, tables)
        make_edge_rows(nc, ident, halves_rows, edge_rows)

        y = sb("y", [P, NT, D])
        with ExitStack() as c2:
            sb2 = lambda n, s, d=f32: c2.enter_context(nc.sbuf_tensor(n, s, d))
            hx = sb2("hx", [P, NT, HEADS, VW])
            att = sb2("att", [P, NT, 2 * HEADS])
            shift = sb2("shift", [P, HEADS])
            src_row = sb2("src_row", [P, HEADS, NP])
            for layer in range(LAYERS):
                with ExitStack() as c3:
                    xT = c3.enter_context(nc.sbuf_tensor(f"xT{layer}", [D, NP], f32))
                    wext = c3.enter_context(nc.sbuf_tensor(f"wext{layer}", [D, D + 2 * HEADS], f32))
                    gat_project(nc, a, layer, x if layer == 0 else y, ident, xT, hx, wext, att, shift)
                    source_rows(nc, f"sr{layer}", ident, xT, wext, shift, src_row)
                gat_attend(nc, a, layer, ident, hx, att, shift, src_row, counts_rows, edge_rows, y)
        layer_norm(nc, "n0", x, y)

        xT = sb("xT", [D, NP])
        transpose_and_project(nc, "t1", x, ident, xT)
        gin_pool(nc, a, x, xT, counts_rows)
        mlp_norm(nc, a, "L1_gnn", ident, xT, y)
        layer_norm(nc, "n1", x, y)
        with ExitStack() as c2:
            hx = c2.enter_context(nc.sbuf_tensor("hx2", [P, NT, HEADS, VW], f32))
            dot_attend(nc, a, x, ident, xT, hx, counts_rows, y)
        layer_norm(nc, "n2", x, y)
        edge_messages(nc, a, x, ident, tables, xtab, aggr)
        gather_sums(nc, x, y, ident, xT, aggr)
        mlp_norm(nc, a, "L3_gnn", ident, xT, y)
        layer_norm(nc, "n3", x, y)
        store(nc, x, out)


def build_counts(nc, a, x, ident, counts, tables):
    ctx = ExitStack()
    with ctx:
        ctx.enter_context(nc.cleanup_on_exit())
        sb = lambda n, s, d=f32: ctx.enter_context(nc.sbuf_tensor(n, s, d))
        sem = lambda n: nc.alloc_semaphore(n)
        ZW = NP
        NZ = NP * NP // P // ZW
        zeros = sb("zeros", [P, ZW])
        dst_f = sb("dst_f", [P, ET])
        src_i = sb("src_i", [P, ET], i32)
        dst_slot = sb("dst_slot", [P, ET], i32)
        dst_i = sb("dst_i", [P, ET], i32)
        cell = sb("cell", [P, ET])
        keys = sb("keys", [P, 2, 2, G])
        cell_slot = sb("cell_slot", [P, 2, G], i32)
        cell_add = sb("cell_add", [P, 2, G])
        nlow = sb("nlow", [P, G])
        first = sb("first", [P, G])
        moved = sb("moved", [P, G])
        spare_i = sb("spare_i", [P, 2], i32)
        spare = sb("spare", [P, 2])
        earlier = sb("earlier", [P, P], bf16)
        same = sb("same", [P, G, P], bf16)
        rows = [ctx.enter_context(nc.psum_tensor(f"rows{w}", [P, 4 * 512], f32)) for w in range(2)]

        zeros_set, padded, loaded, x_padded, x_loaded = (sem(n) for n in ("zeros_set", "padded", "loaded", "x_padded", "x_loaded"))
        const_made, cells_made, keys_set, slots_ready = (sem(n) for n in ("const_made", "cells_made", "keys_set", "slots_ready"))
        rows_ready = [sem(f"rows_ready{w}") for w in range(2)]
        rows_free = [sem(f"rows_free{w}") for w in range(2)]
        converted, dve_steps, turn = (sem(n) for n in ("converted", "dve_steps", "turn"))
        added = [sem(f"added{w}") for w in range(2)]
        zeroed, tables_kept = sem("zeroed"), sem("tables_kept")
        STEPS = 13
        ZEROED = 2 * 16 * (NZ + 1)

        with nc.Block() as block:
            @block.sync
            def _(sp):
                sp.wait_ge(zeros_set, 1)
                for part in counts:
                    v = part[0:NP * NP, :].rearrange("(p f) o -> p (f o)", p=P)
                    for j in range(NZ):
                        sp.dma_start(v[:, j * ZW:(j + 1) * ZW], zeros[:]).then_inc(zeroed, 16)
                    sp.dma_start(part[NP * NP:NP * NP + P, :], zeros[:, 0:1]).then_inc(zeroed, 16)
                sp.wait_ge(x_padded, 1)
                sp.dma_start(x[:, 0:NFULL, :], a["x"][0:NFULL * P, :].rearrange("(t p) d -> p t d", p=P)).then_inc(x_loaded, 16)
                sp.dma_start(x[0:NREST, NFULL, :], a["x"][NFULL * P:N, :]).then_inc(x_loaded, 16)
                sp.wait_ge(x_loaded, 32)
                sp.wait_ge(dve_steps, STEPS * NG)
                for name, t in (("dst_f", dst_f), ("src_i", src_i), ("dst_slot", dst_slot)):
                    sp.dma_start(tables[name][:, :], t[:]).then_inc(tables_kept, 16)
                sp.wait_ge(tables_kept, 48)

            @block.scalar
            def _(act):
                act.wait_ge(padded, 2)
                for ap, t in ((a["src"], src_i), (a["dst"], dst_i)):
                    for lo, hi in ((0, 112), (112, P - 1)):
                        act.dma_start(t[lo:hi, :], ap[lo * ET:hi * ET].rearrange("(p t) -> p t", t=ET)).then_inc(loaded, 16)
                    act.dma_start(t[P - 1:P, 0:EREST], ap[(P - 1) * ET:E].rearrange("(p t) -> p t", p=1)).then_inc(loaded, 16)
                act.wait_ge(cells_made, 1)

                def copy_keys(g, half):
                    nc.scalar.activation(keys[:, half, 0, :], cell[:, bass.ds(g * G, G)], ACT.Copy)
                    nc.scalar.activation(keys[:, half, 1, :], dst_f[:, bass.ds(g * G, G)], ACT.Copy).then_inc(keys_set, 1)

                for half in range(2):
                    copy_keys(half, half)
                with act.Fori(1, NG // 2) as i:
                    for half in range(2):
                        act.wait_ge(rows_ready[1], 2 * i + half - 1)
                        act.sem_inc(turn, 1)
                        copy_keys(2 * i + half, half)

            @block.gpsimd
            def _(pool):
                nc.gpsimd.memset(ident[:], 0.0)
                nc.gpsimd.memset(earlier[:], 1.0).then_inc(const_made, 1)
                pool.wait_ge(const_made, 1)
                nc.gpsimd.affine_select(out=ident[:], in_=ident[:], compare_op=ALU.not_equal, fill=1.0, base=0, pattern=[[-1, P]], channel_multiplier=1)
                nc.gpsimd.affine_select(out=earlier[:], in_=earlier[:], compare_op=ALU.is_gt, fill=0.0, base=0, pattern=[[-1, P]], channel_multiplier=1)
                nc.gpsimd.iota(spare_i[:, 0:1], pattern=[[0, 1]], base=NP * NP, channel_multiplier=1)
                nc.gpsimd.iota(spare_i[:, 1:2], pattern=[[0, 1]], base=NP, channel_multiplier=1).then_inc(const_made, 1)
                pool.wait_ge(zeroed, ZEROED)

                def body(i):
                    for u in range(2 * G):
                        half, j = divmod(u, G)
                        if j == 0:
                            held(pool, turn, slots_ready, 2 * i + half + 1)
                        held(pool, turn, added[u % 2], i * (16 * G) + 16 * (u // 2))
                        nc.gpsimd.indirect_dma_start(counts[u % 2][:, :], bass.IndirectOffsetOnAxis(ap=cell_slot[:, half, j:j + 1], axis=0),
                                                     cell_add[:, half, j:j + 1], None, compute_op=ALU.add).then_inc(added[u % 2], 16)

                turns(pool, NG // 2, body)
                for w in range(2):
                    pool.wait_ge(added[w], 16 * (ET // 2))

            @block.vector
            def _(dve):
                nc.vector.memset(zeros[:], 0.0).then_inc(zeros_set, 1)
                for w in range(2):
                    dve.sem_inc(rows_free[w], 1)
                for t in (src_i, dst_i):
                    nc.vector.memset(t[96:P, :], NP - 1).then_inc(padded, 1)
                nc.vector.memset(x[:, NFULL, :], 0.0).then_inc(x_padded, 1)
                dve.wait_ge(loaded, 96)
                dve.wait_ge(const_made, 2)
                nc.vector.tensor_copy(spare[:], spare_i[:])
                nc.vector.tensor_copy(dst_f[:], dst_i[:])
                nc.vector.tensor_copy(cell[:], src_i[:]).then_inc(converted, 1)
                dve.wait_ge(converted, 1)
                nc.vector.scalar_tensor_tensor(cell[:], cell[:], float(NP), dst_f[:], ALU.mult, ALU.add).then_inc(cells_made, 1)
                dve.wait_ge(cells_made, 1)

                def body(i):
                    for half in range(2):
                        g = 2 * i + half
                        group = bass.ds(g * G, G)
                        step = Chain(dve, dve_steps, i * (2 * STEPS) + half * STEPS)
                        for w, table in ((0, cell), (1, dst_f)):
                            dve.wait_ge(rows_ready[w], g + 1)
                            nc.vector.tensor_tensor(same[:], rows[w][:, 0:G * P].rearrange("p (t c) -> p t c", c=P),
                                                    table[:, group].unsqueeze(2).to_broadcast([P, G, P]), ALU.is_equal).then_inc(rows_free[w], 1)
                            dve.wait_ge(rows_free[w], g + 2)
                            if w == 0:
                                for part in range(2):
                                    wait(dve, added[part], i * (16 * G) - 16 * ((1 - half) * (G + part) // 2))
                                step(nc.vector.reduce_sum(cell_add[:, half, :], same[:], axis=AX.X))
                            step(nc.vector.tensor_tensor(same[:], same[:], earlier[:].unsqueeze(1).to_broadcast([P, G, P]), ALU.mult))
                            step(nc.vector.reduce_sum(nlow[:], same[:], axis=AX.X))
                            step(nc.vector.tensor_scalar(first[:], nlow[:], 0.0, None, ALU.is_equal))
                            step(nc.vector.tensor_scalar(moved[:], table[:, group], spare[:, w:w + 1], None, ALU.subtract))
                            step(nc.vector.tensor_tensor(moved[:], moved[:], first[:], ALU.mult))
                            slot = cell_slot[:, half, :] if w == 0 else dst_slot[:, group]
                            step(nc.vector.tensor_scalar(slot, moved[:], spare[:, w:w + 1], None, ALU.add))
                            if w == 0:
                                dve.sem_inc(slots_ready, 1)
                        assert step.n == STEPS

                turns(dve, NG // 2, body)

            @block.tensor
            def _(pe):
                pe.wait_ge(const_made, 2)
                with pe.Fori(0, NG // 2) as i:
                    for half in range(2):
                        g = 2 * i + half
                        pe.wait_ge(keys_set, g + 1)
                        for w in range(2):
                            pe.wait_ge(rows_free[w], g + 1)
                            for j in range(G):
                                last = nc.tensor.transpose(rows[w][:, j * P:(j + 1) * P],
                                                           keys[:, half, w, j:j + 1].to_broadcast([P, P]), ident[:])
                            last.then_inc(rows_ready[w], 1)


def transpose_and_project(nc, tag, cur, ident, xT, project=None):
    ctx = ExitStack()
    with ctx:
        ctx.enter_context(nc.cleanup_on_exit())
        sb = lambda n, s, d=f32: ctx.enter_context(nc.sbuf_tensor(tag + n, s, d))
        sem = lambda n: nc.alloc_semaphore(tag + n)
        groups = [(t, min(4, NT - t)) for t in range(0, NT, 4)]
        psT = ctx.enter_context(nc.psum_tensor(tag + "psT", [D, 2, 512], f32))
        psH = ctx.enter_context(nc.psum_tensor(tag + "psH", [P, 2, 512], f32))
        turned, evacuated, projected, kept = (sem(n) for n in ("turned", "evacuated", "projected", "kept"))
        with nc.Block() as block:
            more = project(ctx, block, sem, sb) if project else None

            @block.tensor
            def _(pe):
                for n, (t, k) in enumerate(groups):
                    if n >= 2:
                        pe.wait_ge(evacuated, n - 1)
                    for j in range(k):
                        last = nc.tensor.transpose(psT[:, n % 2, j * P:(j + 1) * P], cur[:, t + j, :], ident[:])
                    last.then_inc(turned, 1)
                if more:
                    weights, width, ready, keep = more
                    ready(pe)
                    pe.wait_ge(evacuated, len(groups))
                    for n, (t, k) in enumerate(groups):
                        if n >= 2:
                            pe.wait_ge(kept, n - 1)
                        for j in range(k):
                            last = nc.tensor.matmul(psH[:, n % 2, j * width:(j + 1) * width], xT[:, (t + j) * P:(t + j + 1) * P],
                                                    weights, start=True, stop=True)
                        last.then_inc(projected, 1)

            @block.scalar
            def _(act):
                for n, (t, k) in enumerate(groups):
                    act.wait_ge(turned, n + 1)
                    nc.scalar.activation(xT[:, t * P:(t + k) * P], psT[:, n % 2, 0:k * P], ACT.Copy).then_inc(evacuated, 1)

            if more:
                @block.vector
                def _(dve):
                    weights, width, ready, keep = more
                    keep.start(dve)
                    for n, (t, k) in enumerate(groups):
                        dve.wait_ge(projected, n + 1)
                        keep.group(psH[:, n % 2, 0:k * width].rearrange("p (t w) -> p t w", w=width), t, k).then_inc(kept, 1)
                    dve.wait_ge(kept, len(groups))
                    keep.end(dve)


class Keep:
    def __init__(self, start, group, end):
        self.start, self.group, self.end = start, group, end


def gat_project(nc, a, layer, cur, ident, xT, hx, wext, att, shift):
    WE = D + 2 * HEADS

    def project(ctx, block, sem, sb):
        arow = sb("arow", [D, 2, D])
        prod = sb("prod", [D, 2, D])
        neg = sb("neg", [P, HEADS])
        w_loaded, steps, weights_made, neg_made, shifted = (sem(n) for n in ("w_loaded", "steps", "weights_made", "neg_made", "shifted"))

        @block.sync
        def _(sp):
            sp.dma_start(wext[:, 0:D], a["L0_gnn_W"][layer]).then_inc(w_loaded, 16)
            for k, name in enumerate(("L0_gnn_att_src", "L0_gnn_att_dst")):
                sp.dma_start(arow[:, k, :], bcast_rows(a[name][layer].rearrange("h c -> (h c)"), D)).then_inc(w_loaded, 16)

        @block.gpsimd
        def _(pool):
            pool.wait_ge(neg_made, 1)
            nc.gpsimd.partition_all_reduce(shift[:], neg[:], P, bass.bass_isa.ReduceOp.max).then_inc(shifted, 1)
            pool.wait_ge(shifted, 1)

        def start(dve):
            dve.wait_ge(w_loaded, 48)
            step = Chain(dve, steps)
            for k in range(2):
                step(nc.vector.tensor_tensor(prod[:, k, :], wext[:, 0:D], arow[:, k, :], ALU.mult))
                nc.vector.reduce_sum(wext[:, D + k * HEADS:D + (k + 1) * HEADS], prod[:, k, :].rearrange("p (h c) -> p h c", c=DH),
                                     axis=AX.X).then_inc(weights_made, 1)
            nc.vector.memset(hx[:, :, :, VC:VW], 0.0)
            step(nc.vector.memset(hx[:, :, :, DH:VC], 1.0))

        def group(ps, t, k):
            for j in range(k):
                nc.vector.tensor_copy(hx[:, t + j, :, 0:DH], ps[:, j, 0:D].rearrange("p (h c) -> p h c", c=DH))
            return nc.vector.tensor_copy(att[:, t:t + k, :], ps[:, :, D:WE])

        def end(dve):
            nc.vector.tensor_reduce(neg[:], att[:, :, 0:HEADS].rearrange("p t h -> p h t"), AX.X, ALU.min).then_inc(steps, 1)
            dve.wait_ge(steps, 4)
            nc.vector.tensor_scalar(neg[:], neg[:], -1.0, None, ALU.mult).then_inc(neg_made, 1)

        return wext[:], WE, lambda pe: pe.wait_ge(weights_made, 2), Keep(start, group, end)

    transpose_and_project(nc, f"gp{layer}", cur, ident, xT, project)


def make_edge_rows(nc, ident, halves_rows, edge_rows):
    ctx = ExitStack()
    with ctx:
        ctx.enter_context(nc.cleanup_on_exit())
        sb = lambda n, s, d=f32: ctx.enter_context(nc.sbuf_tensor("er" + n, s, d))
        sem = lambda n: nc.alloc_semaphore("er" + n)
        RING = 3
        cnt = sb("cnt", [P, RING, NT, P])
        more = sb("more", [P, RING, NT, P])
        sign = sb("sign", [P, 2, NP], bf16)
        ps = ctx.enter_context(nc.psum_tensor("erps", [P, 3, 1024], f32))
        cnt_loaded = [sem(f"cnt_loaded{k}") for k in range(RING)]
        sum_stored = [sem(f"sum_stored{k}") for k in range(RING)]
        stored = [sem(f"stored{k}") for k in range(2)]
        summed, turned, signed = sem("summed"), sem("turned"), sem("signed")
        cols = [rows.rearrange("(s p) c -> p s c", p=P) for rows in halves_rows]
        with nc.Block() as block:
            @block.sync
            def _(sp):
                for i in range(NT):
                    if i >= RING:
                        sp.wait_ge(turned, NB * (i - RING + 1))
                        sp.wait_ge(sum_stored[i % RING], 16 * (i // RING))
                    sp.dma_start(cnt[:, i % RING], cols[0][:, :, i * P:(i + 1) * P]).then_inc(cnt_loaded[i % RING], 16)
                    sp.dma_start(more[:, i % RING], cols[1][:, :, i * P:(i + 1) * P]).then_inc(cnt_loaded[i % RING], 16)

            @block.tensor
            def _(pe):
                for i in range(NT):
                    pe.wait_ge(summed, i + 1)
                    for k in range(NB):
                        u = i * NB + k
                        if u >= 3:
                            pe.wait_ge(signed, u - 2)
                        for q in range(BT):
                            last = nc.tensor.transpose(ps[:, u % 3, q * P:(q + 1) * P], cnt[:, i % RING, k * BT + q, :], ident[:])
                        last.then_inc(turned, 1)

            @block.vector
            def _(dve):
                def add_parts(i):
                    dve.wait_ge(cnt_loaded[i % RING], 32 * (i // RING + 1))
                    nc.vector.tensor_tensor(cnt[:, i % RING], cnt[:, i % RING], more[:, i % RING], ALU.add).then_inc(summed, 1)

                add_parts(0)
                for i in range(NT):
                    if i + 1 < NT:
                        add_parts(i + 1)
                    if i >= 2:
                        dve.wait_ge(stored[i % 2], 16 * (i // 2))
                    for k in range(NB):
                        dve.wait_ge(turned, i * NB + k + 1)
                        nc.vector.tensor_scalar(sign[:, i % 2, k * BW:(k + 1) * BW], ps[:, (i * NB + k) % 3, 0:BW], 1.0, None, ALU.min).then_inc(signed, 1)

            @block.scalar
            def _(act):
                for i in range(NT):
                    act.wait_ge(summed, i + 1)
                    act.dma_start(cols[0][:, :, i * P:(i + 1) * P], cnt[:, i % RING]).then_inc(sum_stored[i % RING], 16)
                    act.wait_ge(signed, NB * (i + 1))
                    act.dma_start(edge_rows[i * P:(i + 1) * P, :], sign[:, i % 2, :]).then_inc(stored[i % 2], 16)
                for k in range(2):
                    act.wait_ge(stored[k], 16 * len(range(k, NT, 2)))
                for k in range(RING):
                    act.wait_ge(sum_stored[k], 16 * len(range(k, NT, RING)))


def source_rows(nc, tag, ident, xT, wext, shift, src_row):
    ctx = ExitStack()
    with ctx:
        ctx.enter_context(nc.cleanup_on_exit())
        sem = lambda n: nc.alloc_semaphore(tag + n)
        ps = ctx.enter_context(nc.psum_tensor(tag + "ps", [P, 4, 512], f32))
        scaled = ctx.enter_context(nc.sbuf_tensor(tag + "scaled", [P, HEADS], f32))
        row_ready, row_kept, shift_scaled = sem("row_ready"), sem("row_kept"), sem("shift_scaled")
        chunks = [(h, c, min(512, NP - c)) for h in range(HEADS) for c in range(0, NP, 512)]
        with nc.Block() as block:
            @block.tensor
            def _(pe):
                for n, (h, c, m) in enumerate(chunks):
                    if n >= 4:
                        pe.wait_ge(row_kept, n - 3)
                    nc.tensor.matmul(ps[:, n % 4, 0:m], wext[:, D + h:D + h + 1].to_broadcast([D, P]), xT[:, c:c + m], start=True, stop=True).then_inc(row_ready, 1)

            @block.scalar
            def _(act):
                nc.scalar.activation(scaled[:], shift[:], ACT.Copy, scale=1.0 - SLOPE).then_inc(shift_scaled, 1)
                act.wait_ge(shift_scaled, 1)
                for n, (h, c, m) in enumerate(chunks):
                    act.wait_ge(row_ready, n + 1)
                    nc.scalar.activation(src_row[:, h, c:c + m], ps[:, n % 4, 0:m], ACT.Identity, bias=scaled[:, h:h + 1], scale=1.0 - SLOPE).then_inc(row_kept, 1)


def gat_attend(nc, a, layer, ident, hx, att, shift, src_row, counts_rows, edge_rows, y):
    ctx = ExitStack()
    tag = f"ga{layer}"
    with ctx:
        ctx.enter_context(nc.cleanup_on_exit())
        sb = lambda n, s, d=f32: ctx.enter_context(nc.sbuf_tensor(tag + n, s, d))
        sem = lambda n: nc.alloc_semaphore(tag + n)
        GROUPS = HEADS * NB
        DVE_TILES, ACT_TILES, POOL_TILES = (0,), (1, 2), (3, 4)
        P_BUFS = 5
        HALF = NP // 2
        logit = sb("logit", [P, 2, BT, BW])
        prob = sb("prob", [P, P_BUFS, BW])
        cnt = sb("cnt", [P, NT, BW])
        edge = sb("edge", [P, 2, HALF], bf16)
        unused = sb("unused", [P, HALF], bf16)
        top = sb("top", [P, BT, HEADS, 2])
        src_fifth = sb("src_fifth", [P, NT, HEADS])
        dst_all = sb("dst_all", [P, NT, HEADS])
        col = sb("col", [P, 2, BT, HEADS])
        cols_next = sb("cols_next", [P, 3, BT, HEADS])
        cols_now = sb("cols_now", [P, 3, BT, HEADS])
        rden = sb("rden", [P, BT, HEADS])
        bias = sb("bias", [P, D])
        psE = ctx.enter_context(nc.psum_tensor(tag + "psE", [P, 2, 1024], f32))
        psO = ctx.enter_context(nc.psum_tensor(tag + "psO", [P, 2, 512], f32))
        psX = ctx.enter_context(nc.psum_tensor(tag + "psX", [P, 1024], f32))
        o_sb = sb("o_sb", [P, BW])

        cnt_loaded = [sem(f"cnt_loaded{k}") for k in range(BT)]
        edge_loaded = [sem(f"edge_loaded{k}") for k in range(2)]
        bias_loaded, setup, turn, max_done, col_steps, cols_moved = (sem(n) for n in ("bias_loaded", "setup", "turn", "max_done", "col_steps", "cols_moved"))
        logit_ready, turned, exp_ready, prob_ready, prob_used, out_steps = (
            sem(n) for n in ("logit_ready", "turned", "exp_ready", "prob_ready", "prob_used", "out_steps"))
        o_kept, o_turned, relu_ready, shifted, pool_ready = (sem(n) for n in ("o_kept", "o_turned", "relu_ready", "shifted", "pool_ready"))
        MAXIMA = BT * HEADS * 2
        COLUMNS_GROUP = 19
        max_units = [g * BT + t for g in range(COLUMNS_GROUP) for t in ((1, 2, 4) if g in (5, 12) else (2, 4))]
        assert len(max_units) == MAXIMA

        def over_blocks(eng, body):
            with eng.Fori(0, NB - 1) as j:
                body(j, True)
            body(NB - 1, False)

        with nc.Block() as block:
            @block.sync
            def _(sp):
                sp.dma_start(bias[:], bcast_rows(a["L0_gnn_bias"][layer], P)).then_inc(bias_loaded, 16)

                def load_edges(j, q):
                    for f in range(2):
                        held(sp, turn, max_done, j * MAXIMA + 2 * HEADS * q + HEADS * f - HEADS)
                        sp.dma_start(edge[:, f, :], edge_rows[bass.ds(j * BW + q * P, P), f * HALF:(f + 1) * HALF]).then_inc(edge_loaded[f], 16)

                def load_counts(j, k):
                    held(sp, turn, prob_ready, (j - 1) * UNITS + (k + 1) * BT * HEADS)
                    sp.dma_start(cnt[:, k * BT:(k + 1) * BT, :],
                                 counts_rows[k * BW:(k + 1) * BW, bass.ds(j * BW, BW)].rearrange("(t p) c -> p t c", p=P)
                                 ).then_inc(cnt_loaded[k], 16)

                for q in range(BT):
                    load_edges(0, q)
                with sp.Fori(0, NB - 1) as j:
                    load_edges(j + 1, 0)
                    for k in range(NB):
                        if k + 1 < BT:
                            load_edges(j + 1, k + 1)
                        load_counts(j + 1, k)

            @block.vector
            def _(dve):
                shift_over = shift[:].unsqueeze(1).to_broadcast([P, NT, HEADS])
                nc.vector.tensor_tensor(src_fifth[:], att[:, :, 0:HEADS], shift_over, ALU.add).then_inc(setup, 1)
                dve.wait_ge(setup, 1)
                nc.vector.tensor_scalar(src_fifth[:], src_fifth[:], SLOPE, None, ALU.mult)
                nc.vector.tensor_tensor(dst_all[:], att[:, :, HEADS:2 * HEADS], shift_over, ALU.subtract).then_inc(setup, 1)
                dve.wait_ge(setup, 2)

                def maximum(j, n):
                    q, rest = divmod(n, 2 * HEADS)
                    f, h = divmod(rest, HEADS)
                    if h == 0:
                        held(dve, turn, edge_loaded[f], j * (16 * BT) + 16 * q + 16)
                    if n or not isinstance(j, int):
                        held(dve, turn, max_done, j * MAXIMA + n)
                    half = slice(f * HALF, (f + 1) * HALF)
                    nc.vector.tensor_tensor_reduce(out=unused[:], in0=edge[:, f, :], in1=src_row[:, h, half], scale=1.0, scalar=0.0,
                                                   op0=ALU.mult, op1=ALU.max, accum_out=top[:, q, h, f:f + 1]).then_inc(max_done, 1)

                def columns(j):
                    dve.wait_ge(max_done, j * MAXIMA + MAXIMA)
                    step = Chain(dve, col_steps, j * 6)
                    dst = dst_all[:, bass.ds(j * BT, BT), :]
                    step(nc.vector.tensor_tensor(col[:, 0], top[:, :, :, 0], top[:, :, :, 1], ALU.max))
                    step(nc.vector.scalar_tensor_tensor(col[:, 0], col[:, 0], 1.0 / (1.0 - SLOPE), dst, ALU.mult, ALU.add))
                    step(nc.vector.scalar_tensor_tensor(col[:, 1], col[:, 0], SLOPE, col[:, 0], ALU.mult, ALU.max))
                    step(nc.vector.tensor_tensor(cols_next[:, 0], dst, col[:, 1], ALU.subtract))
                    step(nc.vector.scalar_tensor_tensor(cols_next[:, 1], dst, SLOPE, col[:, 1], ALU.mult, ALU.subtract))
                    step(nc.vector.tensor_tensor(cols_next[:, 2], cols_next[:, 0], cols_next[:, 1], ALU.subtract))
                    assert step.n == 6

                def make_logit(j, g, q, cols):
                    c, h = divmod(g, HEADS)
                    nc.vector.tensor_scalar(logit[:, g % 2, q, :], src_row[:, h, c * BW:(c + 1) * BW], cols[:, 0, q, h:h + 1], cols[:, 1, q, h:h + 1],
                                            ALU.add, ALU.max).then_inc(logit_ready, 1)

                for n in range(MAXIMA):
                    maximum(0, n)
                columns(0)
                nc.vector.tensor_copy(cols_now[:], cols_next[:]).then_inc(cols_moved, 1)
                dve.wait_ge(cols_moved, 1)
                for q in DVE_TILES:
                    make_logit(0, 0, q, cols_now)

                def body(j, more):
                    for g in range(GROUPS):
                        c, h = divmod(g, HEADS)
                        if more and g == COLUMNS_GROUP:
                            columns(j + 1)
                        for t in range(BT):
                            u = g * BT + t
                            for q in DVE_TILES[t:t + 1]:
                                if g + 1 < GROUPS:
                                    make_logit(j, g + 1, q, cols_now)
                                elif more:
                                    make_logit(j + 1, 0, q, cols_next)
                            if more and u in max_units:
                                maximum(j + 1, max_units.index(u))
                            if t == 0 and h == 0:
                                dve.wait_ge(cnt_loaded[c], 16 * j + 16)
                            dve.wait_ge(exp_ready, j * UNITS + u + 3)
                            p = prob[:, u % P_BUFS, :]
                            nc.vector.scalar_tensor_tensor(p, p, BIG, cnt[:, c * BT + t, :], ALU.min, ALU.mult).then_inc(prob_ready, 1)
                    if more:
                        nc.vector.tensor_copy(cols_now[:], cols_next[:]).then_inc(cols_moved, 1)
                        dve.wait_ge(cols_moved, j + 2)
                    dve.wait_ge(o_turned, j + 1)
                    step = Chain(dve, out_steps, j * 5)
                    o = psX[:, 0:BW].rearrange("p (q h c) -> p q h c", h=HEADS, c=VW)
                    yb = y[:, bass.ds(j * BT, BT), :]
                    step(nc.vector.tensor_scalar(rden[:], o[:, :, :, DH], 1e-16, None, ALU.add))
                    step(nc.vector.reciprocal(rden[:], rden[:]))
                    for h in range(HEADS):
                        last = nc.vector.tensor_tensor(yb[:, :, h * DH:(h + 1) * DH], o[:, :, h, 0:DH],
                                                       rden[:, :, h:h + 1].to_broadcast([P, BT, DH]), ALU.mult)
                    step(last)
                    step(nc.vector.tensor_tensor(yb, yb, bias[:].unsqueeze(1).to_broadcast([P, BT, D]), ALU.add))
                    step(nc.vector.tensor_scalar(yb, yb, 0.0, None, ALU.max))

                dve.wait_ge(bias_loaded, 16)
                over_blocks(dve, body)

            @block.gpsimd
            def _(pool):
                def make_logit(g, cols):
                    c, h = divmod(g, HEADS)
                    for q in POOL_TILES:
                        nc.gpsimd.tensor_scalar(logit[:, g % 2, q, :], src_row[:, h, c * BW:(c + 1) * BW], cols[:, 0, q, h:h + 1], cols[:, 1, q, h:h + 1],
                                                ALU.add, ALU.max).then_inc(pool_ready, 1)

                pool.wait_ge(cols_moved, 1)
                pool.sem_inc(turn, 1)
                make_logit(0, cols_now)

                def body(j, more):
                    held(pool, turn, cols_moved, j + 1)
                    for g in range(GROUPS):
                        if g:
                            held(pool, turn, turned, j * UNITS + g * BT)
                        if g + 1 < GROUPS:
                            make_logit(g + 1, cols_now)
                        elif more:
                            held(pool, turn, col_steps, (j + 2) * 6)
                            make_logit(0, cols_next)

                over_blocks(pool, body)

            @block.scalar
            def _(act):
                act.sem_inc(exp_ready, 2)
                act.sem_inc(o_kept, 1)
                for k in range(NB):
                    act.dma_start(cnt[:, k * BT:(k + 1) * BT, :], counts_rows[k * BW:(k + 1) * BW, 0:BW].rearrange("(t p) c -> p t c", p=P)
                                  ).then_inc(cnt_loaded[k], 16)
                act.wait_ge(setup, 2)

                def logit_relu(g, q, cols):
                    c, h = divmod(g, HEADS)
                    nc.scalar.activation(logit[:, g % 2, q, :], src_row[:, h, c * BW:(c + 1) * BW], ACT.Relu, bias=cols[:, 2, q, h:h + 1]).then_inc(relu_ready, 1)

                def logit_shift(n, g, q, cols):
                    h = g % HEADS
                    act.wait_ge(relu_ready, n)
                    nc.scalar.activation(logit[:, g % 2, q, :], logit[:, g % 2, q, :], ACT.Identity, bias=cols[:, 1, q, h:h + 1]).then_inc(shifted, 1)

                act.wait_ge(cols_moved, 1)
                for q in ACT_TILES:
                    logit_relu(0, q, cols_now)
                for k, q in enumerate(ACT_TILES):
                    logit_shift(k + 1, 0, q, cols_now)

                def body(j, more):
                    held(act, turn, cols_moved, j + 1)
                    for u in range(UNITS):
                        g, t = divmod(u, BT)
                        c, h = divmod(g, HEADS)
                        act.wait_ge(turned, j * UNITS + u + 1)
                        if g + 1 < GROUPS or more:
                            ng, cols = ((g + 1, cols_now) if g + 1 < GROUPS else (0, cols_next))
                            if t == 0 and g + 1 == GROUPS:
                                held(act, turn, col_steps, (j + 2) * 6)
                            if t < 2:
                                logit_relu(ng, ACT_TILES[t], cols)
                            elif t < 4:
                                logit_shift((j * GROUPS + g + 1) * len(ACT_TILES) + t - 1, ng, ACT_TILES[t - 2], cols)
                        act.wait_ge(prob_used, j * UNITS + u + 1)
                        nc.scalar.activation(prob[:, u % P_BUFS, :], psE[:, u % 2, 0:BW], ACT.Exp, bias=src_fifth[:, c * BT + t, h:h + 1]).then_inc(exp_ready, 1)

                    act.wait_ge(prob_used, j * UNITS + UNITS + P_BUFS)
                    nc.scalar.activation(o_sb[:].rearrange("p (f c) -> p f c", f=2), psO[:, :, 0:HW], ACT.Copy).then_inc(o_kept, 1)

                over_blocks(act, body)

            @block.tensor
            def _(pe):
                pe.sem_inc(prob_used, P_BUFS)
                LAG = 4

                def body(j, more):
                    for u in range(UNITS + LAG):
                        if u < UNITS:
                            g, t = divmod(u, BT)
                            if t == 0:
                                n = j * GROUPS + g + 1
                                pe.wait_ge(logit_ready, n * len(DVE_TILES))
                                pe.wait_ge(shifted, n * len(ACT_TILES))
                                pe.wait_ge(pool_ready, n * len(POOL_TILES))
                            pe.wait_ge(exp_ready, j * UNITS + u + 1)
                            for q in range(BT):
                                last = nc.tensor.transpose(psE[:, u % 2, q * P:(q + 1) * P], logit[:, g % 2, q, t * P:(t + 1) * P], ident[:])
                            last.then_inc(turned, 1)
                        if u >= LAG:
                            v = u - LAG
                            g, t = divmod(v, BT)
                            c, h = divmod(g, HEADS)
                            s = c * BT + t
                            if v == 0:
                                pe.wait_ge(o_kept, j + 1)
                            pe.wait_ge(prob_ready, j * UNITS + v + 1)
                            for f in range(2):
                                last = nc.tensor.matmul(psO[h * VW:(h + 1) * VW, f, 0:HW], hx[:, s, h, :], prob[:, v % P_BUFS, f * HW:(f + 1) * HW],
                                                        start=(s == 0), stop=(s == NT - 1), skip_group_check=True, tile_position=(0, h * VW))
                            last.then_inc(prob_used, 1)
                    pe.wait_ge(o_kept, j + 2)
                    for q in range(BT):
                        last = nc.tensor.transpose(psX[:, q * P:(q + 1) * P], o_sb[:, q * P:(q + 1) * P], ident[:])
                    last.then_inc(o_turned, 1)

                over_blocks(pe, body)


def layer_norm(nc, tag, x, y):
    ctx = ExitStack()
    with ctx:
        ctx.enter_context(nc.cleanup_on_exit())
        sb = lambda n, s, d=f32: ctx.enter_context(nc.sbuf_tensor(tag + n, s, d))
        sem = lambda n: nc.alloc_semaphore(tag + n)
        mean, var = sb("mean", [P, NT]), sb("var", [P, NT])
        steps, var_ready, std_ready = (sem(n) for n in ("steps", "var_ready", "std_ready"))
        with nc.Block() as block:
            @block.vector
            def _(dve):
                step = Chain(dve, steps)
                over = lambda t: t[:].unsqueeze(2).to_broadcast([P, NT, D])
                step(nc.vector.tensor_tensor(x[:], x[:], y[:], ALU.add))
                step(nc.vector.reduce_sum(mean[:], x[:], axis=AX.X))
                step(nc.vector.tensor_scalar(mean[:], mean[:], 1.0 / D, None, ALU.mult))
                step(nc.vector.tensor_tensor(x[:], x[:], over(mean), ALU.subtract))
                step(nc.vector.tensor_tensor(y[:], x[:], x[:], ALU.mult))
                step(nc.vector.reduce_sum(var[:], y[:], axis=AX.X))
                nc.vector.tensor_scalar(var[:], var[:], 1.0 / D, LN_EPS, ALU.mult, ALU.add).then_inc(var_ready, 1)
                dve.wait_ge(std_ready, 1)
                step(nc.vector.reciprocal(var[:], var[:]))
                step(nc.vector.tensor_tensor(x[:], x[:], over(var), ALU.mult))

            @block.scalar
            def _(act):
                act.wait_ge(var_ready, 1)
                nc.scalar.activation(var[:], var[:], ACT.Sqrt).then_inc(std_ready, 1)


def gin_pool(nc, a, x, xT, counts_rows):
    ctx = ExitStack()
    with ctx:
        ctx.enter_context(nc.cleanup_on_exit())
        sb = lambda n, s, d=f32: ctx.enter_context(nc.sbuf_tensor("gin" + n, s, d))
        sem = lambda n: nc.alloc_semaphore("gin" + n)
        cnt = sb("cnt", [P, NT, BW])
        eps = sb("eps", [D, 1])
        ps = ctx.enter_context(nc.psum_tensor("ginps", [D, 2, 2, 512], f32))
        cnt_loaded = [sem(f"cnt_loaded{k}") for k in range(BT)]
        eps_loaded, eps_made, used, kept = (sem(n) for n in ("eps_loaded", "eps_made", "used", "kept"))
        with nc.Block() as block:
            @block.sync
            def _(sp):
                sp.dma_start(eps[:], bcast_rows(a["L1_gnn_eps"], D)).then_inc(eps_loaded, 16)
                with sp.Fori(0, NB) as j:
                    for k in range(BT):
                        sp.wait_ge(used, j * BT + k + 1)
                        sp.dma_start(cnt[:, k * BT:(k + 1) * BT, :],
                                     counts_rows[k * BW:(k + 1) * BW, bass.ds(j * BW, BW)].rearrange("(t p) c -> p t c", p=P)
                                     ).then_inc(cnt_loaded[k], 16)

            @block.tensor
            def _(pe):
                pe.sem_inc(used, BT)
                with pe.Fori(0, NB) as j:
                    pe.wait_ge(kept, j + 1)
                    for s in range(NT):
                        if s % BT == 0:
                            pe.wait_ge(cnt_loaded[s // BT], 16 * j + 16)
                        for f in range(2):
                            last = nc.tensor.matmul(ps[:, 0, f, 0:HW], x[:, s, :], cnt[:, s, f * HW:(f + 1) * HW], start=(s == 0), stop=(s == NT - 1))
                        if s % BT == BT - 1:
                            last.then_inc(used, 1)

            @block.vector
            def _(dve):
                dve.sem_inc(kept, 1)
                dve.wait_ge(eps_loaded, 16)
                nc.vector.tensor_scalar(eps[:], eps[:], 1.0, None, ALU.add).then_inc(eps_made, 1)
                dve.wait_ge(eps_made, 1)
                with dve.Fori(0, NB) as j:
                    dve.wait_ge(used, j * BT + 2 * BT)
                    block_T = xT[:, bass.ds(j * BW, BW)].rearrange("p (f c) -> p f c", f=2)
                    nc.vector.scalar_tensor_tensor(block_T, block_T, eps[:, 0:1], ps[:, 0, :, 0:HW], ALU.mult, ALU.add).then_inc(kept, 1)


def mlp_norm(nc, a, layer, ident, xT, y):
    ctx = ExitStack()
    with ctx:
        ctx.enter_context(nc.cleanup_on_exit())
        sb = lambda n, s, d=f32: ctx.enter_context(nc.sbuf_tensor(layer + n, s, d))
        sem = lambda n: nc.alloc_semaphore(layer + n)
        w = sb("w", [D, 2, D])
        vec = sb("vec", [D, 4])
        z1, z2 = sb("z1", [D, NP]), sb("z2", [D, NP])
        stat = sb("stat", [D, 4])
        ps = [ctx.enter_context(nc.psum_tensor(f"{layer}ps{k}", [D, 2, 512], f32)) for k in range(2)]
        psY = ctx.enter_context(nc.psum_tensor(layer + "psY", [P, 2, 512], f32))
        loaded, steps, var_ready, std_ready, scaled, turned, kept = (sem(n) for n in ("loaded", "steps", "var_ready", "std_ready", "scaled", "turned", "kept"))
        multiplied = [sem(f"multiplied{k}") for k in range(2)]
        acted = [sem(f"acted{k}") for k in range(2)]
        normed = sem("normed")
        chunks = [(c, min(512, NP - c)) for c in range(0, NP, 512)]
        groups = [(t, min(4, NT - t)) for t in range(0, NT, 4)]
        with nc.Block() as block:
            @block.sync
            def _(sp):
                for k in range(2):
                    sp.dma_start(w[:, k, :], a[f"{layer}_W{k + 1}"]).then_inc(loaded, 16)
                for k, name in enumerate(("b1", "b2", "gamma", "beta")):
                    sp.dma_start(vec[:, k:k + 1], a[f"{layer}_{name}"].unsqueeze(1)).then_inc(loaded, 16)

            @block.tensor
            def _(pe):
                pe.wait_ge(loaded, 96)
                for k, src in ((0, xT), (1, z1)):
                    for n, (c, m) in enumerate(chunks):
                        if k == 1:
                            pe.wait_ge(acted[0], n + 1)
                        if n >= 2:
                            pe.wait_ge(acted[k], n - 1)
                        nc.tensor.matmul(ps[k][:, n % 2, 0:m], w[:, k, :], src[:, c:c + m], start=True, stop=True).then_inc(multiplied[k], 1)
                pe.wait_ge(normed, 1)
                for n, (t, k) in enumerate(groups):
                    if n >= 2:
                        pe.wait_ge(kept, n - 1)
                    for j in range(k):
                        last = nc.tensor.transpose(psY[:, n % 2, j * D:(j + 1) * D], z1[:, (t + j) * P:(t + j + 1) * P], ident[0:D, 0:D])
                    last.then_inc(turned, 1)

            @block.scalar
            def _(act):
                act.wait_ge(loaded, 96)
                for k, dst, func in ((0, z1, ACT.Relu), (1, z2, ACT.Identity)):
                    for n, (c, m) in enumerate(chunks):
                        act.wait_ge(multiplied[k], n + 1)
                        nc.scalar.activation(dst[:, c:c + m], ps[k][:, n % 2, 0:m], func, bias=vec[:, k:k + 1]).then_inc(acted[k], 1)
                act.wait_ge(var_ready, 1)
                nc.scalar.activation(stat[:, 2:3], stat[:, 1:2], ACT.Sqrt).then_inc(std_ready, 1)
                act.wait_ge(scaled, 1)
                nc.scalar.activation(z1[:], z2[:], ACT.Relu, bias=vec[:, 3:4], scale=stat[:, 3:4]).then_inc(normed, 1)

            @block.vector
            def _(dve):
                step = Chain(dve, steps)
                dve.wait_ge(acted[1], len(chunks))
                step(nc.vector.reduce_sum(stat[:, 0:1], z2[:, 0:N], axis=AX.X))
                step(nc.vector.tensor_scalar(stat[:, 0:1], stat[:, 0:1], 1.0 / N, None, ALU.mult))
                step(nc.vector.tensor_scalar(z2[:], z2[:], stat[:, 0:1], None, ALU.subtract))
                step(nc.vector.tensor_tensor(z1[:, 0:N], z2[:, 0:N], z2[:, 0:N], ALU.mult))
                step(nc.vector.reduce_sum(stat[:, 1:2], z1[:, 0:N], axis=AX.X))
                nc.vector.tensor_scalar(stat[:, 1:2], stat[:, 1:2], 1.0 / N, BN_EPS, ALU.mult, ALU.add).then_inc(var_ready, 1)
                dve.wait_ge(std_ready, 1)
                step(nc.vector.reciprocal(stat[:, 2:3], stat[:, 2:3]))
                nc.vector.tensor_tensor(stat[:, 3:4], stat[:, 2:3], vec[:, 2:3], ALU.mult).then_inc(scaled, 1)
                for n, (t, k) in enumerate(groups):
                    dve.wait_ge(turned, n + 1)
                    nc.vector.tensor_copy(y[:, t:t + k, :].rearrange("p t d -> p (t d)"), psY[:, n % 2, 0:k * D]).then_inc(kept, 1)


def value_project(nc, a, x, ident, xT, hx):
    def project(ctx, block, sem, sb):
        wv = sb("wv", [D, D])
        w_loaded, steps = sem("w_loaded"), sem("steps")

        @block.sync
        def _(sp):
            sp.dma_start(wv[:], a["L2_gnn_vW"]).then_inc(w_loaded, 16)

        def start(dve):
            nc.vector.memset(hx[:, :, :, DH + 1:VW], 0.0).then_inc(steps, 1)
            dve.wait_ge(steps, 1)
            nc.vector.memset(hx[:, :, :, DH:DH + 1], 1.0)

        def group(ps, t, k):
            for j in range(k):
                last = nc.vector.tensor_copy(hx[:, t + j, :, 0:DH], ps[:, j, :].rearrange("p (h c) -> p h c", c=DH))
            return last

        return wv[:], D, lambda pe: pe.wait_ge(w_loaded, 16), Keep(start, group, lambda dve: None)

    transpose_and_project(nc, "vp", x, ident, xT, project)


def dot_attend(nc, a, x, ident, xT, hx, counts_rows, y):
    value_project(nc, a, x, ident, xT, hx)
    ctx = ExitStack()
    with ctx:
        ctx.enter_context(nc.cleanup_on_exit())
        sb = lambda n, s, d=f32: ctx.enter_context(nc.sbuf_tensor("dot" + n, s, d))
        sem = lambda n: nc.alloc_semaphore("dot" + n)
        RING = 3
        wq, wk = sb("wq", [D, HEADS, VW]), sb("wk", [D, HEADS, VW])
        kT = sb("kT", [P, NP])
        qb = sb("qb", [P, BW])
        raw = sb("raw", [P, RING, BT, BW])
        cnt = sb("cnt", [P, 2, BW])
        work = sb("work", [P, W_BUFS, BW])
        o_sb = sb("o_sb", [P, BW])
        rden = sb("rden", [P, BT, HEADS])
        psS = ctx.enter_context(nc.psum_tensor("dotpsS", [P, 2, 2, 512], f32))
        psO = ctx.enter_context(nc.psum_tensor("dotpsO", [P, 2, 512], f32))
        psC = ctx.enter_context(nc.psum_tensor("dotpsC", [P, 2, 512], f32))
        raw_loaded = [sem(f"raw_loaded{k}") for k in range(RING)]
        w_cleared, w_loaded, k_ready, k_kept = (sem(n) for n in ("w_cleared", "w_loaded", "k_ready", "k_kept"))
        q_ready, q_kept, c_turned, c_kept = (sem(n) for n in ("q_ready", "q_kept", "c_turned", "c_kept"))
        s_ready, clipped, exp_ready, prob_ready, prob_used = (sem(n) for n in ("s_ready", "clipped", "exp_ready", "prob_ready", "prob_used"))
        o_kept, o_turned, out_steps, turn = (sem(n) for n in ("o_kept", "o_turned", "out_steps", "turn"))
        kchunks = [(c, min(512, NP - c)) for c in range(0, NP, 512)]
        flatC = psC[:, :, :].rearrange("p a c -> p (a c)")
        with nc.Block() as block:
            @block.sync
            def _(sp):
                sp.wait_ge(w_cleared, 1)
                for w, name in ((wq, "L2_gnn_qW"), (wk, "L2_gnn_kW")):
                    sp.dma_start(w[:, :, 0:DH], a[name].rearrange("k (h c) -> k h c", c=DH)).then_inc(w_loaded, 16)
                for j in range(NB):
                    for k in range(BT):
                        n = j * BT + k
                        if n >= RING:
                            sp.wait_ge(c_turned, (n - RING + 1) * BT)
                        sp.dma_start(raw[:, n % RING, :, :],
                                     counts_rows[j * BW:(j + 1) * BW, k * BW:(k + 1) * BW].rearrange("(t p) c -> p t c", p=P)
                                     ).then_inc(raw_loaded[n % RING], 16)

            @block.tensor
            def _(pe):
                pe.wait_ge(w_loaded, 32)
                for n, (c, m) in enumerate(kchunks):
                    if n >= 2:
                        pe.wait_ge(k_kept, n - 1)
                    nc.tensor.matmul(psS[:, 0, n % 2, 0:m], wk[:].rearrange("p h c -> p (h c)"), xT[:, c:c + m], start=True, stop=True).then_inc(k_ready, 1)
                pe.wait_ge(k_kept, len(kchunks))
                for j in range(NB):
                    if j:
                        pe.wait_ge(out_steps, 5 * j)
                    for f in range(2):
                        last = nc.tensor.matmul(psC[:, f, 0:HW], wq[:].rearrange("p h c -> p (h c)"), xT[:, j * BW + f * HW:j * BW + (f + 1) * HW], start=True, stop=True)
                    last.then_inc(q_ready, 1)
                    pe.wait_ge(q_kept, j + 1)

                    def turn_counts(s):
                        t = j * NT + s
                        n = t // BT
                        pe.wait_ge(raw_loaded[n % RING], 16 * (n // RING + 1))
                        if s:
                            pe.wait_ge(c_kept, t)
                        for q in range(BT):
                            last = nc.tensor.transpose(flatC[:, q * P:(q + 1) * P], raw[:, n % RING, q, (s % BT) * P:(s % BT + 1) * P], ident[:])
                        last.then_inc(c_turned, 1)

                    turn_counts(0)
                    LAG = 3
                    for m in range(UNITS + LAG):
                        if m < UNITS:
                            s, h = divmod(m, HEADS)
                            n = j * UNITS + m
                            if n >= 2:
                                pe.wait_ge(clipped, n - 1)
                            for f in range(2):
                                last = nc.tensor.matmul(psS[:, m % 2, f, 0:HW], kT[h * VW:(h + 1) * VW, s * P:(s + 1) * P],
                                                        qb[h * VW:(h + 1) * VW, f * HW:(f + 1) * HW], start=True, stop=True, tile_position=(h * VW, 0))
                            last.then_inc(s_ready, 1)
                            if h == HEADS - 1 and s + 1 < NT:
                                turn_counts(s + 1)
                        if m >= LAG:
                            k = m - LAG
                            s, h = divmod(k, HEADS)
                            pe.wait_ge(prob_ready, j * UNITS + k + 1)
                            for f in range(2):
                                last = nc.tensor.matmul(psO[h * VW:(h + 1) * VW, f, 0:HW], hx[:, s, h, :], work[:, k % W_BUFS, f * HW:(f + 1) * HW],
                                                        start=(s == 0), stop=(s == NT - 1), skip_group_check=True, tile_position=(0, h * VW))
                            last.then_inc(prob_used, 1)
                    pe.wait_ge(o_kept, j + 1)
                    for q in range(BT):
                        last = nc.tensor.transpose(flatC[:, q * P:(q + 1) * P], o_sb[:, q * P:(q + 1) * P], ident[:])
                    last.then_inc(o_turned, 1)

            @block.scalar
            def _(act):
                for n, (c, m) in enumerate(kchunks):
                    act.wait_ge(k_ready, n + 1)
                    nc.scalar.activation(kT[:, c:c + m], psS[:, 0, n % 2, 0:m], ACT.Copy).then_inc(k_kept, 1)
                for j in range(NB):
                    act.wait_ge(q_ready, j + 1)
                    nc.scalar.activation(qb[:].rearrange("p (f c) -> p f c", f=2), psC[:, :, 0:HW], ACT.Copy).then_inc(q_kept, 1)
                    for m in range(UNITS):
                        s, h = divmod(m, HEADS)
                        n = j * UNITS + m
                        if h == 0:
                            t = j * NT + s
                            act.wait_ge(c_turned, t + 1)
                            if t >= 2:
                                act.wait_ge(prob_ready, (t - 1) * HEADS)
                            nc.scalar.activation(cnt[:, t % 2, :], flatC[:, 0:BW], ACT.Copy).then_inc(c_kept, 1)
                        act.wait_ge(clipped, n + 1)
                        w = work[:, m % W_BUFS, :]
                        nc.scalar.activation(w, w, ACT.Exp).then_inc(exp_ready, 1)
                    act.wait_ge(prob_used, (j + 1) * UNITS)
                    nc.scalar.activation(o_sb[:].rearrange("p (f c) -> p f c", f=2), psO[:, :, 0:HW], ACT.Copy).then_inc(o_kept, 1)

            @block.vector
            def _(dve):
                nc.vector.memset(wq[:], 0.0)
                nc.vector.memset(wk[:], 0.0).then_inc(w_cleared, 1)
                dve.wait_ge(w_cleared, 1)
                LAG = 1
                for j in range(NB):
                    for m in range(UNITS + LAG):
                        if m < UNITS:
                            n = j * UNITS + m
                            dve.wait_ge(s_ready, n + 1)
                            free = n - W_BUFS + 1 if m >= W_BUFS else j * UNITS
                            if free > 0:
                                dve.wait_ge(prob_used, free)
                            nc.vector.tensor_scalar(work[:, m % W_BUFS, :].rearrange("p (f c) -> p f c", f=2), psS[:, m % 2, :, 0:HW],
                                                    -10.0, 10.0, ALU.max, ALU.min).then_inc(clipped, 1)
                        if m >= LAG:
                            k = m - LAG
                            s = k // HEADS
                            t = j * NT + s
                            dve.wait_ge(exp_ready, j * UNITS + k + 1)
                            w = work[:, k % W_BUFS, :]
                            nc.vector.tensor_tensor(w, w, cnt[:, t % 2, :], ALU.mult).then_inc(prob_ready, 1)
                    dve.wait_ge(o_turned, j + 1)
                    step = Chain(dve, out_steps, j * 5)
                    o = flatC[:, 0:BW].rearrange("p (q h c) -> p q h c", h=HEADS, c=VW)
                    yb = y[:, j * BT:(j + 1) * BT, :]
                    step(nc.vector.tensor_scalar(rden[:], o[:, :, :, DH], 1e-8, None, ALU.add))
                    step(nc.vector.reciprocal(rden[:], rden[:]))
                    for h in range(HEADS):
                        last = nc.vector.tensor_tensor(yb[:, :, h * DH:(h + 1) * DH], o[:, :, h, 0:DH],
                                                       rden[:, :, h:h + 1].to_broadcast([P, BT, DH]), ALU.mult)
                    step(last)
                    step(nc.vector.tensor_tensor(yb, yb, x[:, j * BT:(j + 1) * BT, :], ALU.add))
                    dve.sem_inc(out_steps, 1)


def edge_messages(nc, a, x, ident, tables, xtab, aggr):
    ctx = ExitStack()
    with ctx:
        ctx.enter_context(nc.cleanup_on_exit())
        sb = lambda n, s, d=f32: ctx.enter_context(nc.sbuf_tensor("em" + n, s, d))
        sem = lambda n: nc.alloc_semaphore("em" + n)
        CH = [(0, 4), (4, 4), (8, 4), (12, 1)]
        NC = len(CH)
        dst_f = sb("dst_f", [P, ET])
        src_i = sb("src_i", [P, ET], i32)
        dst_slot = sb("dst_slot", [P, ET], i32)
        xe = sb("xe", [P, NT, D])
        be = sb("be", [P, D])
        zeros = sb("zeros", [P, NT + 1, D])
        we = sb("we", [P, 4, D])
        feat = sb("feat", [P, 2, G, ED])
        featT = sb("featT", [P, 2, P])
        src_st = sb("src_st", [P, 2, G], i32)
        dst_stage = sb("dst_stage", [P, 2, G], i32)
        key_st = sb("key_st", [P, 2, G])
        xg = sb("xg", [P, 2, G, D])
        msg = sb("msg", [P, 2, 4, D])
        same = sb("same", [P, 2, 4, P])
        sums = sb("sums", [P, 2, G, D])
        ps_f = ctx.enter_context(nc.psum_tensor("emps_f", [P, 2, 512], f32))
        ps_k = ctx.enter_context(nc.psum_tensor("emps_k", [P, 2, 512], f32))
        ps_m = ctx.enter_context(nc.psum_tensor("emps_m", [P, 2, 512], f32))
        ps_s = ctx.enter_context(nc.psum_tensor("emps_s", [P, 2, 512], f32))
        be_loaded, xe_made, x_stored, we_cleared, we_loaded, z_set, z_stored = (
            sem(n) for n in ("be_loaded", "xe_made", "x_stored", "we_cleared", "we_loaded", "z_set", "z_stored"))
        feat_loaded = [sem(f"feat_loaded{h}") for h in range(2)]
        gathered = [sem(f"gathered{h}") for h in range(2)]
        added = [sem(f"added{k}") for k in range(KA)]
        feat_turned, feat_kept, key_turned, same_ready, pre_ready, pre_read, msg_ready, sum_ready, sum_kept, turn = (
            sem(n) for n in ("feat_turned", "feat_kept", "key_turned", "same_ready", "pre_ready", "pre_read", "msg_ready", "sum_ready", "sum_kept", "turn"))
        tables_loaded = sem("tables_loaded")
        raw_ready, src_staged, dst_staged, key_staged = (sem(n) for n in ("raw_ready", "src_staged", "dst_staged", "key_staged"))
        per = [len(range(k, 2 * G, KA)) for k in range(KA)]
        FULL = EREST // G
        PART = EREST - FULL * G

        LASTI = NG // 2 - 1
        FULL_TURNS = EREST // G // 2
        assert FULL_TURNS * 2 == EREST // G

        def landed(i, half, j, k):
            return i * per[k] + len(range(k, half * G + j, KA))

        def before_last(i, half, k):
            return 16 * (i * per[k] + (len(range(k, G, KA)) - per[k] if half == 0 else 0))

        with nc.Block() as block:
            @block.sync
            def _(sp):
                sp.dma_start(be[:], bcast_rows(a["L3_gnn_be"], P)).then_inc(be_loaded, 16)
                for name, t in (("dst_f", dst_f), ("src_i", src_i), ("dst_slot", dst_slot)):
                    sp.dma_start(t[:], tables[name][:, :]).then_inc(tables_loaded, 16)
                sp.wait_ge(we_cleared, 1)
                for g in range(4):
                    sp.dma_start(we[g * ED:(g + 1) * ED, g, :], a["L3_gnn_We"]).then_inc(we_loaded, 16)
                sp.wait_ge(z_set, 1)
                for k in range(KA):
                    sp.dma_start(aggr[k][:, :].rearrange("(t p) d -> p t d", p=P), zeros[:]).then_inc(z_stored, 16)
                sp.wait_ge(xe_made, 1)
                sp.dma_start(xtab[:, :].rearrange("(t p) d -> p t d", p=P), xe[:]).then_inc(x_stored, 16)
                flat = a["edge_attr_32"].rearrange("e k -> (e k)")
                most = flat[0:(P - 1) * ET * ED].rearrange("(p f) -> p f", f=ET * ED)
                rest = flat[(P - 1) * ET * ED:E * ED].rearrange("(p f) -> p f", p=1)

                def load(i, half, last_group, n):
                    sp.wait_ge(feat_turned, i * (2 * NC) + (half + 1) * NC)
                    dst = feat[:, half, :, :].rearrange("p t k -> p (t k)")
                    for lo, hi in ((0, 112), (112, P - 1)):
                        sp.dma_start(dst[lo:hi, :], most[lo:hi, bass.ds((2 * i + half) * (G * ED), G * ED)]).then_inc(feat_loaded[half], 16)
                    sp.dma_start(dst[P - 1:P, 0:n * ED], rest[:, bass.ds(last_group * (G * ED), n * ED)]).then_inc(feat_loaded[half], 16)

                with sp.Fori(0, FULL_TURNS) as i:
                    for half in range(2):
                        load(i, half, 2 * i + half, G)
                for i in range(FULL_TURNS, NG // 2):
                    for half in range(2):
                        g = 2 * i + half
                        n = min(G, EREST - g * G)
                        load(i, half, g if n > 0 else 0, n if n > 0 else G)

            @block.gpsimd
            def _(pool):
                def gather(i, half, j, staging=src_st):
                    nc.gpsimd.indirect_dma_start(xg[:, half, j, :], None, xtab[:, :],
                                                 bass.IndirectOffsetOnAxis(ap=src_st[:, half, j:j + 1], axis=0)).then_inc(gathered[half], 16)

                def body(i, last=False):
                    for half in range(2):
                        g = 2 * i + half
                        ahead = not (last and half == 1)
                        if ahead:
                            held(pool, turn, src_staged, g + 2)
                            held(pool, turn, raw_ready, 4 * g)
                        held(pool, turn, dst_staged, g + 1)
                        for c, (lo, n) in enumerate(CH):
                            for j in range(lo, lo + n):
                                if ahead:
                                    gather(i, 1 - half, j)
                                if j == lo:
                                    held(pool, turn, sum_kept, NC * g + c + 1)
                                k = (half * G + j) % KA
                                held(pool, turn, added[k], 16 * landed(i, half, j, k))
                                nc.gpsimd.indirect_dma_start(aggr[k][:, :], bass.IndirectOffsetOnAxis(ap=dst_stage[:, half, j:j + 1], axis=0),
                                                             sums[:, half, j, :], None, compute_op=ALU.add).then_inc(added[k], 16)

                pool.wait_ge(x_stored, 16)
                pool.wait_ge(z_stored, 16 * KA)
                pool.wait_ge(src_staged, 1)
                for j in range(G):
                    gather(0, 0, j)
                body(0)
                with pool.Fori(1, LASTI) as i:
                    body(i)
                body(LASTI, last=True)
                for k in range(KA):
                    pool.wait_ge(added[k], 16 * per[k] * (NG // 2))

            @block.scalar
            def _(act):
                def body(i):
                    for half in range(2):
                        for c, (lo, n) in enumerate(CH):
                            u, v = c % 2, 2 * NC * i + half * NC + c
                            act.wait_ge(feat_turned, v + 2 * NC + 1)
                            wait(act, pre_ready, v - 1)
                            nc.scalar.activation(featT[0:n * ED, u, :], ps_f[0:n * ED, u, 0:P], ACT.Copy).then_inc(feat_kept, 1)
                            act.wait_ge(raw_ready, v + 1)
                            nc.scalar.activation(msg[:, u, 0:n, :], msg[:, u, 0:n, :], ACT.Relu).then_inc(msg_ready, 1)
                            if c == 0:
                                for k in range(KA):
                                    wait(act, added[k], before_last(i, half, k))
                            act.wait_ge(sum_ready, v + 1)
                            nc.scalar.activation(sums[:, half, lo:lo + n, :].rearrange("p t d -> p (t d)"), ps_s[:, u, 0:n * D], ACT.Copy).then_inc(sum_kept, 1)

                turns(act, NG // 2, body)

            @block.vector
            def _(dve):
                dve.sem_inc(feat_turned, 2 * NC)
                nc.vector.memset(zeros[:], 0.0).then_inc(z_set, 1)
                nc.vector.memset(we[:], 0.0).then_inc(we_cleared, 1)
                dve.wait_ge(be_loaded, 16)
                nc.vector.tensor_tensor(xe[:], x[:], be[:].unsqueeze(1).to_broadcast([P, NT, D]), ALU.add).then_inc(xe_made, 1)
                dve.wait_ge(tables_loaded, 48)
                for half in range(2):
                    nc.vector.tensor_copy(src_st[:, half, :], src_i[:, half * G:(half + 1) * G]).then_inc(src_staged, 1)

                def body(i, last=False):
                    for half in range(2):
                        g = 2 * i + half
                        group = bass.ds(g * G, G)
                        held(dve, turn, key_turned, NC * (g - 1) if not isinstance(g, int) or g > 1 else 0)
                        nc.vector.tensor_copy(key_st[:, half, :], dst_f[:, group]).then_inc(key_staged, 1)
                        for k in range(KA):
                            held(dve, turn, added[k], before_last(i, half, k))
                        nc.vector.tensor_copy(dst_stage[:, half, :], dst_slot[:, group]).then_inc(dst_staged, 1)
                        dve.wait_ge(key_staged, g + 1)
                        for c, (lo, n) in enumerate(CH):
                            u, v = c % 2, 2 * NC * i + half * NC + c
                            dve.wait_ge(key_turned, v + 1)
                            wait(dve, sum_ready, v - 1)
                            nc.vector.tensor_tensor(same[:, u, 0:n, :], ps_k[:, u, 0:n * P].rearrange("p (t c) -> p t c", c=P),
                                                    key_st[:, half, lo:lo + n].unsqueeze(2).to_broadcast([P, n, P]), ALU.is_equal).then_inc(same_ready, 1)
                            if c == 0:
                                dve.wait_ge(gathered[half], (16 * G) * i + 16 * G)
                            dve.wait_ge(pre_ready, v + 1)
                            nc.vector.tensor_tensor(msg[:, u, 0:n, :], ps_m[:, u, 0:n * D].rearrange("p (t d) -> p t d", d=D),
                                                    xg[:, half, lo:lo + n, :], ALU.add).then_inc(raw_ready, 1)
                        if not last:
                            nc.vector.tensor_copy(src_st[:, half, :], src_i[:, bass.ds((g + 2) * G, G)]).then_inc(src_staged, 1)

                body(0)
                with dve.Fori(1, LASTI) as i:
                    body(i)
                body(LASTI, last=True)

            @block.tensor
            def _(pe):
                pe.wait_ge(we_loaded, 64)

                def body(i):
                    for half in range(2):
                        g = 2 * i + half
                        for c, (lo, n) in enumerate(CH):
                            u, v = c % 2, 2 * NC * i + half * NC + c
                            if c == 0:
                                pe.wait_ge(feat_loaded[half], 48 * i + 48)
                                pe.wait_ge(key_staged, g + 1)
                            wait(pe, feat_kept, v - 1)
                            nc.tensor.transpose(ps_f[0:n * ED, u, 0:P], feat[:, half, lo:lo + n, :].rearrange("p t k -> p (t k)"), ident[:]).then_inc(feat_turned, 1)
                            wait(pe, same_ready, v - 1)
                            for j in range(n):
                                last = nc.tensor.transpose(ps_k[:, u, j * P:(j + 1) * P], key_st[:, half, lo + j:lo + j + 1].to_broadcast([P, P]), ident[:])
                            last.then_inc(key_turned, 1)
                            pe.wait_ge(feat_kept, v + 1)
                            wait(pe, raw_ready, v - 1)
                            nc.tensor.matmul(ps_m[:, u, 0:n * D], featT[0:n * ED, u, :], we[0:n * ED, 0:n, :].rearrange("p t d -> p (t d)"),
                                             start=True, stop=True).then_inc(pre_ready, 1)
                            pe.wait_ge(same_ready, v + 1)
                            pe.wait_ge(msg_ready, v + 1)
                            wait(pe, sum_kept, v - 1)
                            for j in range(n):
                                last = nc.tensor.matmul(ps_s[:, u, j * D:(j + 1) * D], same[:, u, j, :], msg[:, u, j, :], start=True, stop=True)
                            last.then_inc(sum_ready, 1)

                turns(pe, NG // 2, body)


def gather_sums(nc, x, y, ident, xT, aggr):
    ctx = ExitStack()
    with ctx:
        ctx.enter_context(nc.cleanup_on_exit())
        part = ctx.enter_context(nc.sbuf_tensor("part", [P, KA, NT, D], f32))
        loaded, steps = (nc.alloc_semaphore(n) for n in ("parts_loaded", "part_steps"))
        with nc.Block() as block:
            @block.sync
            def _(sp):
                for k in range(KA):
                    sp.dma_start(part[:, k, :, :], aggr[k][0:NP, :].rearrange("(t p) d -> p t d", p=P)).then_inc(loaded, 16)

            @block.vector
            def _(dve):
                dve.wait_ge(loaded, 16 * KA)
                step = Chain(dve, steps)
                step(nc.vector.tensor_tensor(y[:], x[:], part[:, 0], ALU.add))
                for k in range(1, KA):
                    step(nc.vector.tensor_tensor(y[:], y[:], part[:, k], ALU.add))
    transpose_and_project(nc, "gs", y, ident, xT)


def store(nc, x, out):
    with nc.semaphore("stored") as stored, nc.Block() as block:
        @block.sync
        def _(sp):
            sp.dma_start(out[0:NFULL * P, :].rearrange("(t p) d -> p t d", p=P), x[:, 0:NFULL, :]).then_inc(stored, 16)
            sp.dma_start(out[NFULL * P:N, :], x[0:NREST, NFULL, :]).then_inc(stored, 16)
            sp.wait_ge(stored, 32)


_INS = ['x', 'src', 'dst', 'edge_attr_32', 'L0_gnn_W', 'L0_gnn_att_src', 'L0_gnn_att_dst', 'L0_gnn_bias',
        'L1_gnn_W1', 'L1_gnn_b1', 'L1_gnn_W2', 'L1_gnn_b2', 'L1_gnn_gamma', 'L1_gnn_beta', 'L1_gnn_eps',
        'L2_gnn_qW', 'L2_gnn_kW', 'L2_gnn_vW', 'L3_gnn_We', 'L3_gnn_be', 'L3_gnn_W1', 'L3_gnn_b1',
        'L3_gnn_W2', 'L3_gnn_b2', 'L3_gnn_gamma', 'L3_gnn_beta']


def kernel(**inputs):
    import numpy as _np
    import concourse.bacc as _bacc
    from concourse import mybir as _mybir
    from concourse.bass_utils import run_bass_kernel_spmd as _run

    nc = _bacc.Bacc("TRN2", target_bir_lowering=False, num_devices=1)
    arrays, args = {}, {}
    for name in _INS:
        a = _np.ascontiguousarray(inputs[name])
        arrays[f"in_{name}_dram"] = a
        args[name] = nc.dram_tensor(f"in_{name}_dram", a.shape, _mybir.dt.from_np(a.dtype), kind="ExternalInput").ap()
    out = nc.dram_tensor("out_dram", (N, D), _mybir.dt.float32, kind="ExternalOutput").ap()
    program(nc, args, out)
    r = _run(nc, [arrays], core_ids=[0])
    return r.results[0]["out_dram"]
```

```python
import concourse.bass as bass
from concourse import mybir
from contextlib import ExitStack

N, D, E, ED, HEADS, LAYERS = 3125, 96, 103125, 32, 4, 3
DH = D // HEADS
P = 128
NT = -(-N // P)
NP = NT * P
NFULL = N // P
NREST = N - NFULL * P
ET = -(-E // P)
EREST = E - (P - 1) * ET
G = 13
NG = ET // G
ZERO_STEPS = NP // P
BT = 5
NB = NT // BT
BW = BT * P
HW = BW // 2
VW = 32
VC = DH + 1
UNITS = NT * HEADS
W_BUFS = 6
CHUNKS = [(0, 4), (4, 3), (7, 3), (10, 3)]
NC = len(CHUNKS)
SET_SUMS = [max(n for _, n in CHUNKS[w::2]) for w in range(2)]
SET_TILES = [sum(n for _, n in CHUNKS[w::2]) for w in range(2)]
KA = sum(SET_SUMS)
LN_EPS = BN_EPS = 1e-5
SLOPE = 0.2
BIG = 1e30

f32, bf16, i32 = mybir.dt.float32, mybir.dt.bfloat16, mybir.dt.int32
ALU = mybir.AluOpType
ACT = mybir.ActivationFunctionType
AX = mybir.AxisListType


def bcast_rows(ap, n):
    return ap.unsqueeze(0).to_broadcast([n, ap.shape[0]])


class Chain:

    def __init__(self, eng, sem, base=0):
        self.eng, self.sem, self.base, self.n = eng, sem, base, 0

    def __call__(self, instruction):
        instruction.then_inc(self.sem, 1)
        self.n += 1
        self.eng.wait_ge(self.sem, self.base + self.n)


def wait(eng, sem, value):
    if not isinstance(value, int) or value > 0:
        eng.wait_ge(sem, value)


def held(eng, turn, sem, value):
    if not isinstance(value, int) or value > 0:
        eng.wait_ge(sem, value)
        eng.sem_inc(turn, 1)


def turns(eng, n, body):
    body(0)
    with eng.Fori(1, n) as i:
        body(i)


def program(nc, a, out):
    ctx = ExitStack()
    with ctx:
        sb = lambda n, s, d=f32: ctx.enter_context(nc.sbuf_tensor(n, s, d))

        counts = [nc.dram_tensor(f"counts{w}", [NP * NP + P, 1], f32) for w in range(2)]
        xtab = nc.dram_tensor("xtab", [NP, D], f32)
        aggr = [nc.dram_tensor(f"aggr{k}", [NP + P, D], f32) for k in range(KA)]
        edge_rows = nc.dram_tensor("edge_rows", [NP, NP], bf16)
        halves_rows = [c[0:NP * NP, :].rearrange("(r c) o -> r (c o)", c=NP) for c in counts]
        counts_rows = halves_rows[0]

        tables = {"dst_f": nc.dram_tensor("dst_f_kept", [P, ET], f32), "src_i": nc.dram_tensor("src_i_kept", [P, ET], i32),
                  "dst_slot": nc.dram_tensor("dst_slot_kept", [P, ET], i32)}

        x = sb("x", [P, NT, D])
        ident = sb("ident", [P, P])
        y = sb("y", [P, NT, D])
        with ExitStack() as c2:
            sb2 = lambda n, s, d=f32: c2.enter_context(nc.sbuf_tensor(n, s, d))
            hx = sb2("hx", [P, NT, HEADS, VW])
            att = sb2("att", [P, NT, 2 * HEADS])
            shift = sb2("shift", [P, HEADS])
            src_row = sb2("src_row", [P, HEADS, NP])

            wext = sb2("wext", [D, D + 2 * HEADS])
            arow = sb2("arow", [D, 2, D])

            def project(layer, cur):
                with ExitStack() as c3:
                    xT = c3.enter_context(nc.sbuf_tensor(f"xT{layer}", [D, NP], f32))
                    gat_project(nc, a, layer, cur, ident, xT, hx, wext, arow, att, shift)
                    source_rows(nc, f"sr{layer}", xT, wext, shift, src_row)

            with ExitStack() as c4:
                c4.enter_context(nc.cleanup_on_exit())
                zeros = c4.enter_context(nc.sbuf_tensor("zeros", [P, NP], f32))
                src_i, dst_i = (c4.enter_context(nc.sbuf_tensor(n, [P, ET], i32)) for n in ("src_i", "dst_i"))
                zeroed, sums_zeroed = nc.alloc_semaphore("zeroed"), nc.alloc_semaphore("sums_zeroed")
                start(nc, a, x, ident, src_i, dst_i, wext, arow, counts, aggr, zeros, zeroed, sums_zeroed)
                project(0, x)
                build_counts(nc, ident, src_i, dst_i, counts, tables, zeroed, sums_zeroed)
            make_edge_rows(nc, ident, halves_rows, edge_rows)

            for layer in range(LAYERS):
                if layer:
                    project(layer, y)
                gat_attend(nc, a, layer, ident, hx, att, shift, src_row, counts_rows, edge_rows, y)
        layer_norm(nc, "n0", x, y)

        xT = sb("xT", [D, NP])
        transpose_and_project(nc, "t1", x, ident, xT)
        gin_pool(nc, a, x, xT, counts_rows)
        mlp_norm(nc, a, "L1_gnn", ident, xT, y)
        layer_norm(nc, "n1", x, y)
        with ExitStack() as c2:
            hx = c2.enter_context(nc.sbuf_tensor("hx2", [P, NT, HEADS, VW], f32))
            dot_attend(nc, a, x, ident, xT, hx, counts_rows, y)
        layer_norm(nc, "n2", x, y)
        edge_messages(nc, a, x, ident, tables, xtab, aggr)
        gather_sums(nc, x, y, ident, xT, aggr)
        mlp_norm(nc, a, "L3_gnn", ident, xT, y)
        layer_norm(nc, "n3", x, y)
        store(nc, x, out)


def load_gat_weights(sp, a, layer, wext, arow, loaded):
    sp.dma_start(wext[:, 0:D], a["L0_gnn_W"][layer]).then_inc(loaded, 16)
    for k, name in enumerate(("L0_gnn_att_src", "L0_gnn_att_dst")):
        sp.dma_start(arow[:, k, :], bcast_rows(a[name][layer].rearrange("h c -> (h c)"), D)).then_inc(loaded, 16)


def start(nc, a, x, ident, src_i, dst_i, wext, arow, counts, aggr, zeros, zeroed, sums_zeroed):
    ctx = ExitStack()
    with ctx:
        ctx.enter_context(nc.cleanup_on_exit())
        zeros_set, padded, x_padded, loaded, const_made = (nc.alloc_semaphore("st" + n) for n in ("zeros_set", "padded", "x_padded", "loaded", "const_made"))
        with nc.Block() as block:
            @block.sync
            def _(sp):
                load_gat_weights(sp, a, 0, wext, arow, loaded)
                sp.wait_ge(x_padded, 1)
                sp.dma_start(x[:, 0:NFULL, :], a["x"][0:NFULL * P, :].rearrange("(t p) d -> p t d", p=P)).then_inc(loaded, 16)
                sp.dma_start(x[0:NREST, NFULL, :], a["x"][NFULL * P:N, :]).then_inc(loaded, 16)
                sp.wait_ge(padded, 2)
                for ap, t in ((a["src"], src_i), (a["dst"], dst_i)):
                    for lo, hi in ((0, 112), (112, P - 1)):
                        sp.dma_start(t[lo:hi, :], ap[lo * ET:hi * ET].rearrange("(p t) -> p t", t=ET)).then_inc(loaded, 16)
                    sp.dma_start(t[P - 1:P, 0:EREST], ap[(P - 1) * ET:E].rearrange("(p t) -> p t", p=1)).then_inc(loaded, 16)
                sp.wait_ge(zeros_set, 1)
                for part in counts:
                    v = part[0:NP * NP, :].rearrange("(p j f) o -> j p (f o)", p=P, f=NP)
                    for j in range(ZERO_STEPS):
                        sp.dma_start(v[j], zeros[:]).then_inc(zeroed, 16)
                    sp.dma_start(part[NP * NP:NP * NP + P, :], zeros[:, 0:1]).then_inc(zeroed, 16)
                for part in aggr:
                    sp.dma_start(part[:, :].rearrange("(p t) d -> p (t d)", p=P), zeros[:, 0:(NT + 1) * D]).then_inc(sums_zeroed, 16)
                sp.wait_ge(loaded, 16 * 11)

            @block.gpsimd
            def _(pool):
                nc.gpsimd.memset(ident[:], 0.0).then_inc(const_made, 1)
                pool.wait_ge(const_made, 1)
                nc.gpsimd.affine_select(out=ident[:], in_=ident[:], compare_op=ALU.not_equal, fill=1.0, base=0, pattern=[[-1, P]], channel_multiplier=1)

            @block.vector
            def _(dve):
                nc.vector.memset(x[:, NFULL, :], 0.0).then_inc(x_padded, 1)
                for t in (src_i, dst_i):
                    nc.vector.memset(t[96:P, :], NP - 1).then_inc(padded, 1)
                nc.vector.memset(zeros[:], 0.0).then_inc(zeros_set, 1)


def build_counts(nc, ident, src_i, dst_i, counts, tables, zeroed, sums_zeroed):
    ctx = ExitStack()
    with ctx:
        ctx.enter_context(nc.cleanup_on_exit())
        sb = lambda n, s, d=f32: ctx.enter_context(nc.sbuf_tensor(n, s, d))
        sem = lambda n: nc.alloc_semaphore(n)
        dst_f = sb("dst_f", [P, ET])
        dst_slot = sb("dst_slot", [P, ET], i32)
        cell = sb("cell", [P, ET])
        keys = sb("keys", [P, 2, 2, G])
        cell_slot = sb("cell_slot", [P, 2, G], i32)
        cell_add = sb("cell_add", [P, 2, G])
        nlow = sb("nlow", [P, G])
        first = sb("first", [P, G])
        moved = sb("moved", [P, G])
        spare_i = sb("spare_i", [P, 2], i32)
        spare = sb("spare", [P, 2])
        earlier = sb("earlier", [P, P], bf16)
        same = sb("same", [P, G, P], bf16)
        rows = [ctx.enter_context(nc.psum_tensor(f"rows{w}", [P, 4 * 512], f32)) for w in range(2)]

        const_made, cells_made, keys_set, slots_ready = (sem(n) for n in ("const_made", "cells_made", "keys_set", "slots_ready"))
        rows_ready = [sem(f"rows_ready{w}") for w in range(2)]
        rows_free = [sem(f"rows_free{w}") for w in range(2)]
        converted, dve_steps, turn = (sem(n) for n in ("converted", "dve_steps", "turn"))
        added = [sem(f"added{w}") for w in range(2)]
        tables_kept = sem("tables_kept")
        STEPS = 13

        with nc.Block() as block:
            @block.sync
            def _(sp):
                sp.wait_ge(dve_steps, STEPS * NG)
                for name, t in (("dst_f", dst_f), ("src_i", src_i), ("dst_slot", dst_slot)):
                    sp.dma_start(tables[name][:, :], t[:]).then_inc(tables_kept, 16)
                sp.wait_ge(tables_kept, 48)
                sp.wait_ge(sums_zeroed, 16 * KA)

            @block.scalar
            def _(act):
                act.wait_ge(cells_made, 1)

                def copy_keys(g, half):
                    nc.scalar.activation(keys[:, half, 0, :], cell[:, bass.ds(g * G, G)], ACT.Copy)
                    nc.scalar.activation(keys[:, half, 1, :], dst_f[:, bass.ds(g * G, G)], ACT.Copy).then_inc(keys_set, 1)

                for half in range(2):
                    copy_keys(half, half)
                with act.Fori(1, NG // 2) as i:
                    for half in range(2):
                        act.wait_ge(rows_ready[1], 2 * i + half - 1)
                        act.sem_inc(turn, 1)
                        copy_keys(2 * i + half, half)

            @block.gpsimd
            def _(pool):
                nc.gpsimd.memset(earlier[:], 1.0).then_inc(const_made, 1)
                pool.wait_ge(const_made, 1)
                nc.gpsimd.affine_select(out=earlier[:], in_=earlier[:], compare_op=ALU.is_gt, fill=0.0, base=0, pattern=[[-1, P]], channel_multiplier=1)
                nc.gpsimd.iota(spare_i[:, 0:1], pattern=[[0, 1]], base=NP * NP, channel_multiplier=1)
                nc.gpsimd.iota(spare_i[:, 1:2], pattern=[[0, 1]], base=NP, channel_multiplier=1).then_inc(const_made, 1)
                pool.wait_ge(zeroed, 16 * len(counts) * (ZERO_STEPS + 1))

                def body(i):
                    for u in range(2 * G):
                        half, j = divmod(u, G)
                        if j == 0:
                            held(pool, turn, slots_ready, 2 * i + half + 1)
                        held(pool, turn, added[u % 2], i * (16 * G) + 16 * (u // 2))
                        nc.gpsimd.indirect_dma_start(counts[u % 2][:, :], bass.IndirectOffsetOnAxis(ap=cell_slot[:, half, j:j + 1], axis=0),
                                                     cell_add[:, half, j:j + 1], None, compute_op=ALU.add).then_inc(added[u % 2], 16)

                turns(pool, NG // 2, body)
                for w in range(2):
                    pool.wait_ge(added[w], 16 * (ET // 2))

            @block.vector
            def _(dve):
                for w in range(2):
                    dve.sem_inc(rows_free[w], 1)
                dve.wait_ge(const_made, 2)
                nc.vector.tensor_copy(spare[:], spare_i[:])
                nc.vector.tensor_copy(dst_f[:], dst_i[:])
                nc.vector.tensor_copy(cell[:], src_i[:]).then_inc(converted, 1)
                dve.wait_ge(converted, 1)
                nc.vector.scalar_tensor_tensor(cell[:], cell[:], float(NP), dst_f[:], ALU.mult, ALU.add).then_inc(cells_made, 1)
                dve.wait_ge(cells_made, 1)

                def body(i):
                    for half in range(2):
                        g = 2 * i + half
                        group = bass.ds(g * G, G)
                        step = Chain(dve, dve_steps, i * (2 * STEPS) + half * STEPS)
                        for w, table in ((0, cell), (1, dst_f)):
                            dve.wait_ge(rows_ready[w], g + 1)
                            nc.vector.tensor_tensor(same[:], rows[w][:, 0:G * P].rearrange("p (t c) -> p t c", c=P),
                                                    table[:, group].unsqueeze(2).to_broadcast([P, G, P]), ALU.is_equal).then_inc(rows_free[w], 1)
                            dve.wait_ge(rows_free[w], g + 2)
                            if w == 0:
                                for part in range(2):
                                    wait(dve, added[part], i * (16 * G) - 16 * ((1 - half) * (G + part) // 2))
                                step(nc.vector.reduce_sum(cell_add[:, half, :], same[:], axis=AX.X))
                            step(nc.vector.tensor_tensor(same[:], same[:], earlier[:].unsqueeze(1).to_broadcast([P, G, P]), ALU.mult))
                            step(nc.vector.reduce_sum(nlow[:], same[:], axis=AX.X))
                            step(nc.vector.tensor_scalar(first[:], nlow[:], 0.0, None, ALU.is_equal))
                            step(nc.vector.tensor_scalar(moved[:], table[:, group], spare[:, w:w + 1], None, ALU.subtract))
                            step(nc.vector.tensor_tensor(moved[:], moved[:], first[:], ALU.mult))
                            slot = cell_slot[:, half, :] if w == 0 else dst_slot[:, group]
                            step(nc.vector.tensor_scalar(slot, moved[:], spare[:, w:w + 1], None, ALU.add))
                            if w == 0:
                                dve.sem_inc(slots_ready, 1)
                        assert step.n == STEPS

                turns(dve, NG // 2, body)

            @block.tensor
            def _(pe):
                pe.wait_ge(const_made, 2)
                with pe.Fori(0, NG // 2) as i:
                    for half in range(2):
                        g = 2 * i + half
                        pe.wait_ge(keys_set, g + 1)
                        for w in range(2):
                            pe.wait_ge(rows_free[w], g + 1)
                            for j in range(G):
                                last = nc.tensor.transpose(rows[w][:, j * P:(j + 1) * P],
                                                           keys[:, half, w, j:j + 1].to_broadcast([P, P]), ident[:])
                            last.then_inc(rows_ready[w], 1)


def transpose_and_project(nc, tag, cur, ident, xT, project=None):
    ctx = ExitStack()
    with ctx:
        ctx.enter_context(nc.cleanup_on_exit())
        sb = lambda n, s, d=f32: ctx.enter_context(nc.sbuf_tensor(tag + n, s, d))
        sem = lambda n: nc.alloc_semaphore(tag + n)
        groups = [(t, min(4, NT - t)) for t in range(0, NT, 4)]
        psT = ctx.enter_context(nc.psum_tensor(tag + "psT", [D, 2, 512], f32))
        psH = ctx.enter_context(nc.psum_tensor(tag + "psH", [P, 2, 512], f32))
        turned, evacuated, projected, kept = (sem(n) for n in ("turned", "evacuated", "projected", "kept"))
        with nc.Block() as block:
            more = project(ctx, block, sem, sb) if project else None

            @block.tensor
            def _(pe):
                for n, (t, k) in enumerate(groups):
                    if n >= 2:
                        pe.wait_ge(evacuated, n - 1)
                    for j in range(k):
                        last = nc.tensor.transpose(psT[:, n % 2, j * P:(j + 1) * P], cur[:, t + j, :], ident[:])
                    last.then_inc(turned, 1)
                if more:
                    weights, width, ready, keep = more
                    ready(pe)
                    pe.wait_ge(evacuated, len(groups))
                    for n, (t, k) in enumerate(groups):
                        if n >= 2:
                            pe.wait_ge(kept, n - 1)
                        for j in range(k):
                            last = nc.tensor.matmul(psH[:, n % 2, j * width:(j + 1) * width], xT[:, (t + j) * P:(t + j + 1) * P],
                                                    weights, start=True, stop=True)
                        last.then_inc(projected, 1)

            @block.scalar
            def _(act):
                for n, (t, k) in enumerate(groups):
                    act.wait_ge(turned, n + 1)
                    nc.scalar.activation(xT[:, t * P:(t + k) * P], psT[:, n % 2, 0:k * P], ACT.Copy).then_inc(evacuated, 1)

            if more:
                @block.vector
                def _(dve):
                    weights, width, ready, keep = more
                    keep.start(dve)
                    for n, (t, k) in enumerate(groups):
                        dve.wait_ge(projected, n + 1)
                        keep.group(psH[:, n % 2, 0:k * width].rearrange("p (t w) -> p t w", w=width), t, k).then_inc(kept, 1)
                    dve.wait_ge(kept, len(groups))
                    keep.end(dve)


class Keep:
    def __init__(self, start, group, end):
        self.start, self.group, self.end = start, group, end


def gat_project(nc, a, layer, cur, ident, xT, hx, wext, arow, att, shift):
    WE = D + 2 * HEADS

    def project(ctx, block, sem, sb):
        prod = sb("prod", [D, 2, D])
        neg = sb("neg", [P, HEADS])
        w_loaded, steps, weights_made, neg_made, shifted = (sem(n) for n in ("w_loaded", "steps", "weights_made", "neg_made", "shifted"))

        if layer:
            @block.sync
            def _(sp):
                load_gat_weights(sp, a, layer, wext, arow, w_loaded)

        @block.gpsimd
        def _(pool):
            pool.wait_ge(neg_made, 1)
            nc.gpsimd.partition_all_reduce(shift[:], neg[:], P, bass.bass_isa.ReduceOp.max).then_inc(shifted, 1)
            pool.wait_ge(shifted, 1)

        def start(dve):
            if layer:
                dve.wait_ge(w_loaded, 48)
            step = Chain(dve, steps)
            for k in range(2):
                step(nc.vector.tensor_tensor(prod[:, k, :], wext[:, 0:D], arow[:, k, :], ALU.mult))
                nc.vector.reduce_sum(wext[:, D + k * HEADS:D + (k + 1) * HEADS], prod[:, k, :].rearrange("p (h c) -> p h c", c=DH),
                                     axis=AX.X).then_inc(weights_made, 1)
            nc.vector.memset(hx[:, :, :, VC:VW], 0.0)
            step(nc.vector.memset(hx[:, :, :, DH:VC], 1.0))

        def group(ps, t, k):
            for j in range(k):
                nc.vector.tensor_copy(hx[:, t + j, :, 0:DH], ps[:, j, 0:D].rearrange("p (h c) -> p h c", c=DH))
            return nc.vector.tensor_copy(att[:, t:t + k, :], ps[:, :, D:WE])

        def end(dve):
            nc.vector.tensor_reduce(neg[:], att[:, :, 0:HEADS].rearrange("p t h -> p h t"), AX.X, ALU.min).then_inc(steps, 1)
            dve.wait_ge(steps, 4)
            nc.vector.tensor_scalar(neg[:], neg[:], -1.0, None, ALU.mult).then_inc(neg_made, 1)

        return wext[:], WE, lambda pe: pe.wait_ge(weights_made, 2), Keep(start, group, end)

    transpose_and_project(nc, f"gp{layer}", cur, ident, xT, project)


def make_edge_rows(nc, ident, halves_rows, edge_rows):
    ctx = ExitStack()
    with ctx:
        ctx.enter_context(nc.cleanup_on_exit())
        sb = lambda n, s, d=f32: ctx.enter_context(nc.sbuf_tensor("er" + n, s, d))
        sem = lambda n: nc.alloc_semaphore("er" + n)
        RING = 3
        cnt = sb("cnt", [P, RING, NP])
        more = sb("more", [P, RING, NP])
        sign = sb("sign", [P, NT, BW], bf16)
        ps = ctx.enter_context(nc.psum_tensor("erps", [P, 3, 1024], f32))
        cnt_loaded = [sem(f"cnt_loaded{k}") for k in range(RING)]
        sum_stored = [sem(f"sum_stored{k}") for k in range(RING)]
        summed, turned, signed, stored = (sem(n) for n in ("summed", "turned", "signed", "stored"))
        with nc.Block() as block:
            @block.sync
            def _(sp):
                for i in range(NT):
                    if i >= RING:
                        sp.wait_ge(turned, NB * (i - RING + 1))
                        sp.wait_ge(sum_stored[i % RING], 16 * (i // RING))
                    for part, t in zip(halves_rows, (cnt, more)):
                        sp.dma_start(t[:, i % RING], part[i * P:(i + 1) * P, :]).then_inc(cnt_loaded[i % RING], 16)

            @block.tensor
            def _(pe):
                for i in range(NT):
                    pe.wait_ge(summed, i + 1)
                    for k in range(NB):
                        u = i * NB + k
                        if u >= 3:
                            pe.wait_ge(signed, u - 2)
                        for q in range(BT):
                            last = nc.tensor.transpose(ps[:, u % 3, q * P:(q + 1) * P], cnt[:, i % RING, (k * BT + q) * P:(k * BT + q + 1) * P], ident[:])
                        last.then_inc(turned, 1)

            @block.vector
            def _(dve):
                def add_parts(i):
                    dve.wait_ge(cnt_loaded[i % RING], 32 * (i // RING + 1))
                    nc.vector.tensor_tensor(cnt[:, i % RING], cnt[:, i % RING], more[:, i % RING], ALU.add).then_inc(summed, 1)

                add_parts(0)
                for i in range(NT):
                    if i + 1 < NT:
                        add_parts(i + 1)
                    strip, piece = divmod(i, BT)
                    if piece == 0 and strip:
                        dve.wait_ge(stored, 16 * strip)
                    for k in range(NB):
                        dve.wait_ge(turned, i * NB + k + 1)
                        nc.vector.tensor_scalar(sign[:, k * BT:(k + 1) * BT, piece * P:(piece + 1) * P],
                                                ps[:, (i * NB + k) % 3, 0:BW].rearrange("p (q c) -> p q c", c=P), 1.0, None, ALU.min).then_inc(signed, 1)

            @block.scalar
            def _(act):
                for i in range(NT):
                    act.wait_ge(summed, i + 1)
                    act.dma_start(halves_rows[0][i * P:(i + 1) * P, :], cnt[:, i % RING]).then_inc(sum_stored[i % RING], 16)
                    strip, piece = divmod(i, BT)
                    if piece == BT - 1:
                        act.wait_ge(signed, NB * (i + 1))
                        act.dma_start(edge_rows[:, strip * BW:(strip + 1) * BW].rearrange("(t p) c -> p t c", p=P), sign[:]).then_inc(stored, 16)
                act.wait_ge(stored, 16 * NB)
                for k in range(RING):
                    act.wait_ge(sum_stored[k], 16 * len(range(k, NT, RING)))


def source_rows(nc, tag, xT, wext, shift, src_row):
    ctx = ExitStack()
    with ctx:
        ctx.enter_context(nc.cleanup_on_exit())
        sem = lambda n: nc.alloc_semaphore(tag + n)
        ps = ctx.enter_context(nc.psum_tensor(tag + "ps", [P, 4, 512], f32))
        scaled = ctx.enter_context(nc.sbuf_tensor(tag + "scaled", [P, HEADS], f32))
        row_ready, row_kept, shift_scaled = sem("row_ready"), sem("row_kept"), sem("shift_scaled")
        chunks = [(h, c, min(512, NP - c)) for h in range(HEADS) for c in range(0, NP, 512)]
        with nc.Block() as block:
            @block.tensor
            def _(pe):
                for n, (h, c, m) in enumerate(chunks):
                    if n >= 4:
                        pe.wait_ge(row_kept, n - 3)
                    nc.tensor.matmul(ps[:, n % 4, 0:m], wext[:, D + h:D + h + 1].to_broadcast([D, P]), xT[:, c:c + m], start=True, stop=True).then_inc(row_ready, 1)

            @block.scalar
            def _(act):
                nc.scalar.activation(scaled[:], shift[:], ACT.Copy, scale=1.0 - SLOPE).then_inc(shift_scaled, 1)
                act.wait_ge(shift_scaled, 1)
                for n, (h, c, m) in enumerate(chunks):
                    act.wait_ge(row_ready, n + 1)
                    nc.scalar.activation(src_row[:, h, c:c + m], ps[:, n % 4, 0:m], ACT.Identity, bias=scaled[:, h:h + 1], scale=1.0 - SLOPE).then_inc(row_kept, 1)


def gat_attend(nc, a, layer, ident, hx, att, shift, src_row, counts_rows, edge_rows, y):
    ctx = ExitStack()
    tag = f"ga{layer}"
    with ctx:
        ctx.enter_context(nc.cleanup_on_exit())
        sb = lambda n, s, d=f32: ctx.enter_context(nc.sbuf_tensor(tag + n, s, d))
        sem = lambda n: nc.alloc_semaphore(tag + n)
        GROUPS = HEADS * NB
        DVE_TILES, ACT_TILES, POOL_TILES = (0,), (1, 2), (3, 4)
        P_BUFS = 5
        HALF = NP // 2
        logit = sb("logit", [P, 2, BT, BW])
        prob = sb("prob", [P, P_BUFS, BW])
        cnt = sb("cnt", [P, NT, BW])
        edge = sb("edge", [P, 2, HALF], bf16)
        unused = sb("unused", [P, HALF], bf16)
        top = sb("top", [P, BT, HEADS, 2])
        src_fifth = sb("src_fifth", [P, NT, HEADS])
        dst_all = sb("dst_all", [P, NT, HEADS])
        col = sb("col", [P, 2, BT, HEADS])
        cols_next = sb("cols_next", [P, 3, BT, HEADS])
        cols_now = sb("cols_now", [P, 3, BT, HEADS])
        rden = sb("rden", [P, BT, HEADS])
        bias = sb("bias", [P, D])
        psE = ctx.enter_context(nc.psum_tensor(tag + "psE", [P, 3, 1024], f32))
        psO = ctx.enter_context(nc.psum_tensor(tag + "psO", [P, 2, 512], f32))
        psX = psE[:, 2, :]
        o_sb = sb("o_sb", [P, BW])

        cnt_loaded = [sem(f"cnt_loaded{k}") for k in range(BT)]
        edge_loaded = [sem(f"edge_loaded{k}") for k in range(2)]
        bias_loaded, setup, turn, max_done, col_steps, cols_moved = (sem(n) for n in ("bias_loaded", "setup", "turn", "max_done", "col_steps", "cols_moved"))
        logit_ready, turned, exp_ready, prob_ready, prob_used, out_steps = (
            sem(n) for n in ("logit_ready", "turned", "exp_ready", "prob_ready", "prob_used", "out_steps"))
        o_kept, o_turned, relu_ready, shifted, pool_ready = (sem(n) for n in ("o_kept", "o_turned", "relu_ready", "shifted", "pool_ready"))
        MAXIMA = BT * HEADS * 2
        COLUMNS_GROUP = 19
        max_units = [g * BT + t for g in range(COLUMNS_GROUP) for t in ((1, 2, 4) if g in (5, 12) else (2, 4))]
        assert len(max_units) == MAXIMA

        def over_blocks(eng, body):
            with eng.Fori(0, NB - 1) as j:
                body(j, True)
            body(NB - 1, False)

        with nc.Block() as block:
            @block.sync
            def _(sp):
                sp.dma_start(bias[:], bcast_rows(a["L0_gnn_bias"][layer], P)).then_inc(bias_loaded, 16)

                def load_edges(j, q):
                    for f in range(2):
                        held(sp, turn, max_done, j * MAXIMA + 2 * HEADS * q + HEADS * f - HEADS)
                        sp.dma_start(edge[:, f, :], edge_rows[bass.ds(j * BW + q * P, P), f * HALF:(f + 1) * HALF]).then_inc(edge_loaded[f], 16)

                def load_counts(j, k):
                    held(sp, turn, prob_ready, (j - 1) * UNITS + (k + 1) * BT * HEADS)
                    sp.dma_start(cnt[:, k * BT:(k + 1) * BT, :],
                                 counts_rows[k * BW:(k + 1) * BW, bass.ds(j * BW, BW)].rearrange("(t p) c -> p t c", p=P)
                                 ).then_inc(cnt_loaded[k], 16)

                for q in range(BT):
                    load_edges(0, q)
                with sp.Fori(0, NB - 1) as j:
                    load_edges(j + 1, 0)
                    for k in range(NB):
                        if k + 1 < BT:
                            load_edges(j + 1, k + 1)
                        load_counts(j + 1, k)

            @block.vector
            def _(dve):
                shift_over = shift[:].unsqueeze(1).to_broadcast([P, NT, HEADS])
                nc.vector.tensor_tensor(src_fifth[:], att[:, :, 0:HEADS], shift_over, ALU.add).then_inc(setup, 1)
                dve.wait_ge(setup, 1)
                nc.vector.tensor_scalar(src_fifth[:], src_fifth[:], SLOPE, None, ALU.mult)
                nc.vector.tensor_tensor(dst_all[:], att[:, :, HEADS:2 * HEADS], shift_over, ALU.subtract).then_inc(setup, 1)
                dve.wait_ge(setup, 2)

                def maximum(j, n):
                    q, rest = divmod(n, 2 * HEADS)
                    f, h = divmod(rest, HEADS)
                    if h == 0:
                        held(dve, turn, edge_loaded[f], j * (16 * BT) + 16 * q + 16)
                    if n or not isinstance(j, int):
                        held(dve, turn, max_done, j * MAXIMA + n)
                    half = slice(f * HALF, min((f + 1) * HALF, NP if q == BT - 1 else N))
                    width = half.stop - half.start
                    nc.vector.tensor_tensor_reduce(out=unused[:, 0:width], in0=edge[:, f, 0:width], in1=src_row[:, h, half], scale=1.0, scalar=0.0,
                                                   op0=ALU.mult, op1=ALU.max, accum_out=top[:, q, h, f:f + 1]).then_inc(max_done, 1)

                def columns(j):
                    dve.wait_ge(max_done, j * MAXIMA + MAXIMA)
                    step = Chain(dve, col_steps, j * 6)
                    dst = dst_all[:, bass.ds(j * BT, BT), :]
                    step(nc.vector.tensor_tensor(col[:, 0], top[:, :, :, 0], top[:, :, :, 1], ALU.max))
                    step(nc.vector.scalar_tensor_tensor(col[:, 0], col[:, 0], 1.0 / (1.0 - SLOPE), dst, ALU.mult, ALU.add))
                    step(nc.vector.scalar_tensor_tensor(col[:, 1], col[:, 0], SLOPE, col[:, 0], ALU.mult, ALU.max))
                    step(nc.vector.tensor_tensor(cols_next[:, 0], dst, col[:, 1], ALU.subtract))
                    step(nc.vector.scalar_tensor_tensor(cols_next[:, 1], dst, SLOPE, col[:, 1], ALU.mult, ALU.subtract))
                    step(nc.vector.tensor_tensor(cols_next[:, 2], cols_next[:, 0], cols_next[:, 1], ALU.subtract))
                    assert step.n == 6

                def make_logit(j, g, q, cols):
                    c, h = divmod(g, HEADS)
                    nc.vector.tensor_scalar(logit[:, g % 2, q, :], src_row[:, h, c * BW:(c + 1) * BW], cols[:, 0, q, h:h + 1], cols[:, 1, q, h:h + 1],
                                            ALU.add, ALU.max).then_inc(logit_ready, 1)

                for n in range(MAXIMA):
                    maximum(0, n)
                columns(0)
                nc.vector.tensor_copy(cols_now[:], cols_next[:]).then_inc(cols_moved, 1)
                dve.wait_ge(cols_moved, 1)
                for q in DVE_TILES:
                    make_logit(0, 0, q, cols_now)

                def body(j, more):
                    for g in range(GROUPS):
                        c, h = divmod(g, HEADS)
                        if more and g == COLUMNS_GROUP:
                            columns(j + 1)
                        for t in range(BT):
                            u = g * BT + t
                            for q in DVE_TILES[t:t + 1]:
                                if g + 1 < GROUPS:
                                    make_logit(j, g + 1, q, cols_now)
                                elif more:
                                    make_logit(j + 1, 0, q, cols_next)
                            if more and u in max_units:
                                maximum(j + 1, max_units.index(u))
                            if t == 0 and h == 0:
                                dve.wait_ge(cnt_loaded[c], 16 * j + 16)
                            dve.wait_ge(exp_ready, j * UNITS + u + 3)
                            p = prob[:, u % P_BUFS, :]
                            nc.vector.scalar_tensor_tensor(p, p, BIG, cnt[:, c * BT + t, :], ALU.min, ALU.mult).then_inc(prob_ready, 1)
                    if more:
                        nc.vector.tensor_copy(cols_now[:], cols_next[:]).then_inc(cols_moved, 1)
                        dve.wait_ge(cols_moved, j + 2)
                    dve.wait_ge(o_turned, j + 1)
                    step = Chain(dve, out_steps, j * 5 + 5)
                    o = psX[:, 0:BW].rearrange("p (q h c) -> p q h c", h=HEADS, c=VW)
                    yb = y[:, bass.ds(j * BT, BT), :]
                    step(nc.vector.tensor_scalar(rden[:], o[:, :, :, DH], 1e-16, None, ALU.add))
                    step(nc.vector.reciprocal(rden[:], rden[:]))
                    for h in range(HEADS):
                        last = nc.vector.tensor_tensor(yb[:, :, h * DH:(h + 1) * DH], o[:, :, h, 0:DH],
                                                       rden[:, :, h:h + 1].to_broadcast([P, BT, DH]), ALU.mult)
                    step(last)
                    step(nc.vector.tensor_tensor(yb, yb, bias[:].unsqueeze(1).to_broadcast([P, BT, D]), ALU.add))
                    step(nc.vector.tensor_scalar(yb, yb, 0.0, None, ALU.max))

                dve.wait_ge(bias_loaded, 16)
                dve.sem_inc(out_steps, 5)
                over_blocks(dve, body)

            @block.gpsimd
            def _(pool):
                def make_logit(g, cols):
                    c, h = divmod(g, HEADS)
                    for q in POOL_TILES:
                        nc.gpsimd.tensor_scalar(logit[:, g % 2, q, :], src_row[:, h, c * BW:(c + 1) * BW], cols[:, 0, q, h:h + 1], cols[:, 1, q, h:h + 1],
                                                ALU.add, ALU.max).then_inc(pool_ready, 1)

                pool.wait_ge(cols_moved, 1)
                pool.sem_inc(turn, 1)
                make_logit(0, cols_now)

                def body(j, more):
                    held(pool, turn, cols_moved, j + 1)
                    for g in range(GROUPS):
                        if g:
                            held(pool, turn, turned, j * UNITS + g * BT)
                        if g + 1 < GROUPS:
                            make_logit(g + 1, cols_now)
                        elif more:
                            held(pool, turn, col_steps, (j + 2) * 6)
                            make_logit(0, cols_next)

                over_blocks(pool, body)

            @block.scalar
            def _(act):
                act.sem_inc(exp_ready, 2)
                act.sem_inc(o_kept, 1)
                for k in range(NB):
                    act.wait_ge(max_done, 2 * HEADS * k + HEADS)
                    act.dma_start(cnt[:, k * BT:(k + 1) * BT, :], counts_rows[k * BW:(k + 1) * BW, 0:BW].rearrange("(t p) c -> p t c", p=P)
                                  ).then_inc(cnt_loaded[k], 16)
                act.wait_ge(setup, 2)

                def logit_relu(g, q, cols):
                    c, h = divmod(g, HEADS)
                    nc.scalar.activation(logit[:, g % 2, q, :], src_row[:, h, c * BW:(c + 1) * BW], ACT.Relu, bias=cols[:, 2, q, h:h + 1]).then_inc(relu_ready, 1)

                def logit_shift(n, g, q, cols):
                    h = g % HEADS
                    act.wait_ge(relu_ready, n)
                    nc.scalar.activation(logit[:, g % 2, q, :], logit[:, g % 2, q, :], ACT.Identity, bias=cols[:, 1, q, h:h + 1]).then_inc(shifted, 1)

                act.wait_ge(cols_moved, 1)
                for q in ACT_TILES:
                    logit_relu(0, q, cols_now)
                for k, q in enumerate(ACT_TILES):
                    logit_shift(k + 1, 0, q, cols_now)

                def body(j, more):
                    held(act, turn, cols_moved, j + 1)
                    for u in range(UNITS):
                        g, t = divmod(u, BT)
                        c, h = divmod(g, HEADS)
                        act.wait_ge(turned, j * UNITS + u + 1)
                        if g + 1 < GROUPS or more:
                            ng, cols = ((g + 1, cols_now) if g + 1 < GROUPS else (0, cols_next))
                            if t == 0 and g + 1 == GROUPS:
                                held(act, turn, col_steps, (j + 2) * 6)
                            if t < 2:
                                logit_relu(ng, ACT_TILES[t], cols)
                            elif t < 4:
                                logit_shift((j * GROUPS + g + 1) * len(ACT_TILES) + t - 1, ng, ACT_TILES[t - 2], cols)
                        act.wait_ge(prob_used, j * UNITS + u + 1)
                        nc.scalar.activation(prob[:, u % P_BUFS, :], psE[:, u % 3, 0:BW], ACT.Exp, bias=src_fifth[:, c * BT + t, h:h + 1]).then_inc(exp_ready, 1)

                    act.wait_ge(prob_used, j * UNITS + UNITS + P_BUFS)
                    nc.scalar.activation(o_sb[:].rearrange("p (f c) -> p f c", f=2), psO[:, :, 0:HW], ACT.Copy).then_inc(o_kept, 1)

                over_blocks(act, body)

            @block.tensor
            def _(pe):
                pe.sem_inc(prob_used, P_BUFS)
                LAG = 4

                def body(j, more):
                    for u in range(UNITS + LAG):
                        if u < UNITS:
                            g, t = divmod(u, BT)
                            if t == 0:
                                n = j * GROUPS + g + 1
                                pe.wait_ge(logit_ready, n * len(DVE_TILES))
                                pe.wait_ge(shifted, n * len(ACT_TILES))
                                pe.wait_ge(pool_ready, n * len(POOL_TILES))
                            pe.wait_ge(exp_ready, j * UNITS + max(u, 2))
                            if u == 2:
                                pe.wait_ge(out_steps, 5 * j + 3)
                            for q in range(BT):
                                last = nc.tensor.transpose(psE[:, u % 3, q * P:(q + 1) * P], logit[:, g % 2, q, t * P:(t + 1) * P], ident[:])
                            last.then_inc(turned, 1)
                        if u >= LAG:
                            v = u - LAG
                            g, t = divmod(v, BT)
                            c, h = divmod(g, HEADS)
                            s = c * BT + t
                            if v == 0:
                                pe.wait_ge(o_kept, j + 1)
                            pe.wait_ge(prob_ready, j * UNITS + v + 1)
                            for f in range(2):
                                last = nc.tensor.matmul(psO[h * VW:(h + 1) * VW, f, 0:HW], hx[:, s, h, :], prob[:, v % P_BUFS, f * HW:(f + 1) * HW],
                                                        start=(s == 0), stop=(s == NT - 1), skip_group_check=True, tile_position=(0, h * VW))
                            last.then_inc(prob_used, 1)
                    pe.wait_ge(o_kept, j + 2)
                    for q in range(BT):
                        last = nc.tensor.transpose(psX[:, q * P:(q + 1) * P], o_sb[:, q * P:(q + 1) * P], ident[:])
                    last.then_inc(o_turned, 1)

                over_blocks(pe, body)


def layer_norm(nc, tag, x, y):
    ctx = ExitStack()
    with ctx:
        ctx.enter_context(nc.cleanup_on_exit())
        sb = lambda n, s, d=f32: ctx.enter_context(nc.sbuf_tensor(tag + n, s, d))
        sem = lambda n: nc.alloc_semaphore(tag + n)
        mean, var = sb("mean", [P, NT]), sb("var", [P, NT])
        steps, var_ready, std_ready = (sem(n) for n in ("steps", "var_ready", "std_ready"))
        with nc.Block() as block:
            @block.vector
            def _(dve):
                step = Chain(dve, steps)
                over = lambda t: t[:].unsqueeze(2).to_broadcast([P, NT, D])
                step(nc.vector.tensor_tensor(x[:], x[:], y[:], ALU.add))
                step(nc.vector.reduce_sum(mean[:], x[:], axis=AX.X))
                step(nc.vector.tensor_scalar(mean[:], mean[:], 1.0 / D, None, ALU.mult))
                step(nc.vector.tensor_tensor(x[:], x[:], over(mean), ALU.subtract))
                step(nc.vector.tensor_tensor(y[:], x[:], x[:], ALU.mult))
                step(nc.vector.reduce_sum(var[:], y[:], axis=AX.X))
                nc.vector.tensor_scalar(var[:], var[:], 1.0 / D, LN_EPS, ALU.mult, ALU.add).then_inc(var_ready, 1)
                dve.wait_ge(std_ready, 1)
                step(nc.vector.reciprocal(var[:], var[:]))
                step(nc.vector.tensor_tensor(x[:], x[:], over(var), ALU.mult))

            @block.scalar
            def _(act):
                act.wait_ge(var_ready, 1)
                nc.scalar.activation(var[:], var[:], ACT.Sqrt).then_inc(std_ready, 1)


def gin_pool(nc, a, x, xT, counts_rows):
    ctx = ExitStack()
    with ctx:
        ctx.enter_context(nc.cleanup_on_exit())
        sb = lambda n, s, d=f32: ctx.enter_context(nc.sbuf_tensor("gin" + n, s, d))
        sem = lambda n: nc.alloc_semaphore("gin" + n)
        cnt = sb("cnt", [P, NT, BW])
        eps = sb("eps", [D, 1])
        ps = ctx.enter_context(nc.psum_tensor("ginps", [D, 2, 2, 512], f32))
        cnt_loaded = [sem(f"cnt_loaded{k}") for k in range(BT)]
        eps_loaded, eps_made, used, kept = (sem(n) for n in ("eps_loaded", "eps_made", "used", "kept"))
        with nc.Block() as block:
            @block.sync
            def _(sp):
                sp.dma_start(eps[:], bcast_rows(a["L1_gnn_eps"], D)).then_inc(eps_loaded, 16)
                with sp.Fori(0, NB) as j:
                    for k in range(BT):
                        sp.wait_ge(used, j * BT + k + 1)
                        sp.dma_start(cnt[:, k * BT:(k + 1) * BT, :],
                                     counts_rows[k * BW:(k + 1) * BW, bass.ds(j * BW, BW)].rearrange("(t p) c -> p t c", p=P)
                                     ).then_inc(cnt_loaded[k], 16)

            @block.tensor
            def _(pe):
                pe.sem_inc(used, BT)
                with pe.Fori(0, NB) as j:
                    pe.wait_ge(kept, j + 1)
                    for s in range(NT):
                        if s % BT == 0:
                            pe.wait_ge(cnt_loaded[s // BT], 16 * j + 16)
                        for f in range(2):
                            last = nc.tensor.matmul(ps[:, 0, f, 0:HW], x[:, s, :], cnt[:, s, f * HW:(f + 1) * HW], start=(s == 0), stop=(s == NT - 1))
                        if s % BT == BT - 1:
                            last.then_inc(used, 1)

            @block.vector
            def _(dve):
                dve.sem_inc(kept, 1)
                dve.wait_ge(eps_loaded, 16)
                nc.vector.tensor_scalar(eps[:], eps[:], 1.0, None, ALU.add).then_inc(eps_made, 1)
                dve.wait_ge(eps_made, 1)
                with dve.Fori(0, NB) as j:
                    dve.wait_ge(used, j * BT + 2 * BT)
                    block_T = xT[:, bass.ds(j * BW, BW)].rearrange("p (f c) -> p f c", f=2)
                    nc.vector.scalar_tensor_tensor(block_T, block_T, eps[:, 0:1], ps[:, 0, :, 0:HW], ALU.mult, ALU.add).then_inc(kept, 1)


def mlp_norm(nc, a, layer, ident, xT, y):
    ctx = ExitStack()
    with ctx:
        ctx.enter_context(nc.cleanup_on_exit())
        sb = lambda n, s, d=f32: ctx.enter_context(nc.sbuf_tensor(layer + n, s, d))
        sem = lambda n: nc.alloc_semaphore(layer + n)
        w = sb("w", [D, 2, D])
        vec = sb("vec", [D, 4])
        z1, z2 = sb("z1", [D, NP]), sb("z2", [D, NP])
        stat = sb("stat", [D, 4])
        ps = [ctx.enter_context(nc.psum_tensor(f"{layer}ps{k}", [D, 2, 512], f32)) for k in range(2)]
        psY = ctx.enter_context(nc.psum_tensor(layer + "psY", [P, 2, 512], f32))
        loaded, steps, var_ready, std_ready, scaled, turned, kept = (sem(n) for n in ("loaded", "steps", "var_ready", "std_ready", "scaled", "turned", "kept"))
        multiplied = [sem(f"multiplied{k}") for k in range(2)]
        acted = [sem(f"acted{k}") for k in range(2)]
        normed = sem("normed")
        chunks = [(c, min(512, NP - c)) for c in range(0, NP, 512)]
        groups = [(t, min(4, NT - t)) for t in range(0, NT, 4)]
        with nc.Block() as block:
            @block.sync
            def _(sp):
                for k in range(2):
                    sp.dma_start(w[:, k, :], a[f"{layer}_W{k + 1}"]).then_inc(loaded, 16)
                for k, name in enumerate(("b1", "b2", "gamma", "beta")):
                    sp.dma_start(vec[:, k:k + 1], a[f"{layer}_{name}"].unsqueeze(1)).then_inc(loaded, 16)

            @block.tensor
            def _(pe):
                pe.wait_ge(loaded, 96)
                for k, src in ((0, xT), (1, z1)):
                    for n, (c, m) in enumerate(chunks):
                        if k == 1:
                            pe.wait_ge(acted[0], n + 1)
                        if n >= 2:
                            pe.wait_ge(acted[k], n - 1)
                        nc.tensor.matmul(ps[k][:, n % 2, 0:m], w[:, k, :], src[:, c:c + m], start=True, stop=True).then_inc(multiplied[k], 1)
                pe.wait_ge(normed, 1)
                for n, (t, k) in enumerate(groups):
                    if n >= 2:
                        pe.wait_ge(kept, n - 1)
                    for j in range(k):
                        last = nc.tensor.transpose(psY[:, n % 2, j * D:(j + 1) * D], z1[:, (t + j) * P:(t + j + 1) * P], ident[0:D, 0:D])
                    last.then_inc(turned, 1)

            @block.scalar
            def _(act):
                act.wait_ge(loaded, 96)
                for k, dst, func in ((0, z1, ACT.Relu), (1, z2, ACT.Identity)):
                    for n, (c, m) in enumerate(chunks):
                        act.wait_ge(multiplied[k], n + 1)
                        nc.scalar.activation(dst[:, c:c + m], ps[k][:, n % 2, 0:m], func, bias=vec[:, k:k + 1]).then_inc(acted[k], 1)
                act.wait_ge(var_ready, 1)
                nc.scalar.activation(stat[:, 2:3], stat[:, 1:2], ACT.Sqrt).then_inc(std_ready, 1)
                act.wait_ge(scaled, 1)
                nc.scalar.activation(z1[:], z2[:], ACT.Relu, bias=vec[:, 3:4], scale=stat[:, 3:4]).then_inc(normed, 1)

            @block.vector
            def _(dve):
                step = Chain(dve, steps)
                dve.wait_ge(acted[1], len(chunks))
                step(nc.vector.reduce_sum(stat[:, 0:1], z2[:, 0:N], axis=AX.X))
                step(nc.vector.tensor_scalar(stat[:, 0:1], stat[:, 0:1], 1.0 / N, None, ALU.mult))
                step(nc.vector.tensor_scalar(z2[:], z2[:], stat[:, 0:1], None, ALU.subtract))
                step(nc.vector.tensor_tensor(z1[:, 0:N], z2[:, 0:N], z2[:, 0:N], ALU.mult))
                step(nc.vector.reduce_sum(stat[:, 1:2], z1[:, 0:N], axis=AX.X))
                nc.vector.tensor_scalar(stat[:, 1:2], stat[:, 1:2], 1.0 / N, BN_EPS, ALU.mult, ALU.add).then_inc(var_ready, 1)
                dve.wait_ge(std_ready, 1)
                step(nc.vector.reciprocal(stat[:, 2:3], stat[:, 2:3]))
                nc.vector.tensor_tensor(stat[:, 3:4], stat[:, 2:3], vec[:, 2:3], ALU.mult).then_inc(scaled, 1)
                for n, (t, k) in enumerate(groups):
                    dve.wait_ge(turned, n + 1)
                    nc.vector.tensor_copy(y[:, t:t + k, :].rearrange("p t d -> p (t d)"), psY[:, n % 2, 0:k * D]).then_inc(kept, 1)


def value_project(nc, a, x, ident, xT, hx):
    def project(ctx, block, sem, sb):
        wv = sb("wv", [D, D])
        w_loaded, steps = sem("w_loaded"), sem("steps")

        @block.sync
        def _(sp):
            sp.dma_start(wv[:], a["L2_gnn_vW"]).then_inc(w_loaded, 16)

        def start(dve):
            nc.vector.memset(hx[:, :, :, DH + 1:VW], 0.0).then_inc(steps, 1)
            dve.wait_ge(steps, 1)
            nc.vector.memset(hx[:, :, :, DH:DH + 1], 1.0)

        def group(ps, t, k):
            for j in range(k):
                last = nc.vector.tensor_copy(hx[:, t + j, :, 0:DH], ps[:, j, :].rearrange("p (h c) -> p h c", c=DH))
            return last

        return wv[:], D, lambda pe: pe.wait_ge(w_loaded, 16), Keep(start, group, lambda dve: None)

    transpose_and_project(nc, "vp", x, ident, xT, project)


FOUR = {"k": (0, 0, 1, 1), "q": (0, 1, 0, 1)}
TWO = {"k": (0, 2), "q": (2, 0)}


def split_heads(nc, a, xT, parts4, parts2):
    ctx = ExitStack()
    with ctx:
        ctx.enter_context(nc.cleanup_on_exit())
        sb = lambda n, s, d=f32: ctx.enter_context(nc.sbuf_tensor("sp" + n, s, d))
        sem = lambda n: nc.alloc_semaphore("sp" + n)
        QT = P // 4
        RING = 3
        weights = sb("weights", [D, 2, HEADS, 4, QT])
        rest = sb("rest", [P, RING, BW])
        second = sb("second", [P, 2, BW], bf16)
        ps = ctx.enter_context(nc.psum_tensor("spps", [P, 4, 1024], f32))
        w_cleared, w_loaded, projected, first_kept, rest_ready, parts_kept, third_kept = (
            sem(n) for n in ("w_cleared", "w_loaded", "projected", "first_kept", "rest_ready", "parts_kept", "third_kept"))
        jobs = [(w, h, c) for w in "kq" for h in range(HEADS) for c in range(NB)]
        halves = lambda t: t.rearrange("p (f c) -> p f c", f=2)

        def place(n):
            w, h, c = jobs[n]
            base = (h % 2) * 2 * QT
            quarter = lambda part: slice(base + TWO[w].index(part) * QT, base + TWO[w].index(part) * QT + QT)
            return w, h, slice(c * BW, (c + 1) * BW), quarter(0), quarter(2)

        with nc.Block() as block:
            @block.sync
            def _(sp):
                sp.wait_ge(w_cleared, 1)
                for k, name in enumerate(("L2_gnn_kW", "L2_gnn_qW")):
                    for r in range(4):
                        sp.dma_start(weights[:, k, :, r, 0:DH], a[name].rearrange("k (h c) -> k h c", c=DH)).then_inc(w_loaded, 16)

            @block.tensor
            def _(pe):
                pe.wait_ge(w_loaded, 128)
                for n, (w, h, c) in enumerate(jobs):
                    if n >= 4:
                        pe.wait_ge(rest_ready, n - 3)
                    for f in range(2):
                        last = nc.tensor.matmul(ps[:, n % 4, f * 512:f * 512 + HW], weights[:, "kq".index(w), h, :, :].rearrange("k r c -> k (r c)"),
                                                xT[:, c * BW + f * HW:c * BW + (f + 1) * HW], start=True, stop=True)
                    last.then_inc(projected, 1)

            @block.scalar
            def _(act):
                for n in range(len(jobs) + 1):
                    if n < len(jobs):
                        w, h, cols, _, _ = place(n)
                        act.wait_ge(projected, n + 1)
                        nc.scalar.activation(halves(parts4[w][:, h, cols]), ps[:, n % 4, :].rearrange("p (f c) -> p f c", f=2)[:, :, 0:HW],
                                             ACT.Copy).then_inc(first_kept, 1)
                    if n:
                        m = n - 1
                        w, h, cols, _, third = place(m)
                        act.wait_ge(rest_ready, m + 1)
                        if m >= 2:
                            act.wait_ge(third_kept, m - 1)
                        nc.scalar.activation(second[third, m % 2, :], rest[third, m % RING, :], ACT.Copy)
                        runs = ((64, 128),) if w == "k" else ((32, 64), (96, 128))
                        for lo, hi in runs:
                            last = nc.scalar.activation(parts4[w][lo:hi, h, cols], rest[lo:hi, m % RING, :], ACT.Copy)
                        last.then_inc(parts_kept, 1)

            @block.vector
            def _(dve):
                nc.vector.memset(weights[:], 0.0).then_inc(w_cleared, 1)
                for n in range(len(jobs) + 1):
                    if n < len(jobs):
                        w, h, cols, first, _ = place(n)
                        dve.wait_ge(first_kept, n + 1)
                        if n >= RING:
                            dve.wait_ge(parts_kept, n - RING + 1)
                            dve.wait_ge(third_kept, n - RING + 1)
                        nc.vector.tensor_copy(parts2[w][first, h // 2, cols], parts4[w][first, h, cols])
                        nc.vector.tensor_tensor(halves(rest[:, n % RING, :]), ps[:, n % 4, :].rearrange("p (f c) -> p f c", f=2)[:, :, 0:HW],
                                                halves(parts4[w][:, h, cols]), ALU.subtract).then_inc(rest_ready, 1)
                    if n:
                        m = n - 1
                        w, h, cols, _, third = place(m)
                        dve.wait_ge(parts_kept, m + 1)
                        dve.wait_ge(rest_ready, m + 1)
                        nc.vector.tensor_tensor(parts2[w][third, h // 2, cols], rest[third, m % RING, :], second[third, m % 2, :], ALU.subtract).then_inc(third_kept, 1)


def dot_attend(nc, a, x, ident, xT, hx, counts_rows, y):
    value_project(nc, a, x, ident, xT, hx)
    ctx = ExitStack()
    with ctx:
        sb = lambda n, s, d=f32: ctx.enter_context(nc.sbuf_tensor("dot" + n, s, d))
        parts4 = {w: sb(w + "_four", [P, HEADS, NP], bf16) for w in "kq"}
        parts2 = {w: sb(w + "_two", [P, HEADS // 2, NP], bf16) for w in "kq"}
        split_heads(nc, a, xT, parts4, parts2)
        ctx.enter_context(nc.cleanup_on_exit())
        sem = lambda n: nc.alloc_semaphore("dot" + n)
        RING = 3
        raw = sb("raw", [P, RING, BT, BW])
        cnt = sb("cnt", [P, 2, BW])
        work = sb("work", [P, W_BUFS, BW])
        o_sb = sb("o_sb", [P, BW])
        rden = sb("rden", [P, BT, HEADS])
        psS = ctx.enter_context(nc.psum_tensor("dotpsS", [P, 2, 2, 512], f32))
        psO = ctx.enter_context(nc.psum_tensor("dotpsO", [P, 2, 512], f32))
        psC = ctx.enter_context(nc.psum_tensor("dotpsC", [P, 2, 512], f32))
        raw_loaded = [sem(f"raw_loaded{k}") for k in range(RING)]
        c_turned, c_kept = sem("c_turned"), sem("c_kept")
        s_ready, clipped, exp_ready, prob_ready, prob_used = (sem(n) for n in ("s_ready", "clipped", "exp_ready", "prob_ready", "prob_used"))
        o_kept, o_turned, out_steps = (sem(n) for n in ("o_kept", "o_turned", "out_steps"))
        flatC = psC[:, :, :].rearrange("p a c -> p (a c)")
        with nc.Block() as block:
            @block.sync
            def _(sp):
                for j in range(NB):
                    for k in range(BT):
                        n = j * BT + k
                        if n >= RING:
                            sp.wait_ge(c_turned, (n - RING + 1) * BT)
                        sp.dma_start(raw[:, n % RING, :, :],
                                     counts_rows[j * BW:(j + 1) * BW, k * BW:(k + 1) * BW].rearrange("(t p) c -> p t c", p=P)
                                     ).then_inc(raw_loaded[n % RING], 16)

            @block.tensor
            def _(pe):
                for j in range(NB):
                    if j:
                        pe.wait_ge(out_steps, 5 * j)

                    def turn_counts(s):
                        t = j * NT + s
                        n = t // BT
                        pe.wait_ge(raw_loaded[n % RING], 16 * (n // RING + 1))
                        if s:
                            pe.wait_ge(c_kept, t)
                        for q in range(BT):
                            last = nc.tensor.transpose(flatC[:, q * P:(q + 1) * P], raw[:, n % RING, q, (s % BT) * P:(s % BT + 1) * P], ident[:])
                        last.then_inc(c_turned, 1)

                    turn_counts(0)
                    LAG = 3
                    for m in range(UNITS + LAG):
                        if m < UNITS:
                            s, h = divmod(m, HEADS)
                            n = j * UNITS + m
                            if n >= 2:
                                pe.wait_ge(clipped, n - 1)
                            two = slice((h % 2) * 64, (h % 2) * 64 + 64)
                            for f in range(2):
                                rows = slice(j * BW + f * HW, j * BW + (f + 1) * HW)
                                nc.tensor.matmul(psS[:, m % 2, f, 0:HW], parts4["k"][:, h, s * P:(s + 1) * P], parts4["q"][:, h, rows], start=True, stop=False)
                            for f in range(2):
                                rows = slice(j * BW + f * HW, j * BW + (f + 1) * HW)
                                last = nc.tensor.matmul(psS[:, m % 2, f, 0:HW], parts2["k"][two, h // 2, s * P:(s + 1) * P], parts2["q"][two, h // 2, rows],
                                                        start=False, stop=True, tile_position=(two.start, 0))
                            last.then_inc(s_ready, 1)
                            if h == HEADS - 1 and s + 1 < NT:
                                turn_counts(s + 1)
                        if m >= LAG:
                            k = m - LAG
                            s, h = divmod(k, HEADS)
                            pe.wait_ge(prob_ready, j * UNITS + k + 1)
                            for f in range(2):
                                last = nc.tensor.matmul(psO[h * VW:(h + 1) * VW, f, 0:HW], hx[:, s, h, :], work[:, k % W_BUFS, f * HW:(f + 1) * HW],
                                                        start=(s == 0), stop=(s == NT - 1), skip_group_check=True, tile_position=(0, h * VW))
                            last.then_inc(prob_used, 1)
                    pe.wait_ge(o_kept, j + 1)
                    for q in range(BT):
                        last = nc.tensor.transpose(flatC[:, q * P:(q + 1) * P], o_sb[:, q * P:(q + 1) * P], ident[:])
                    last.then_inc(o_turned, 1)

            @block.scalar
            def _(act):
                for j in range(NB):
                    for m in range(UNITS):
                        s, h = divmod(m, HEADS)
                        n = j * UNITS + m
                        if h == 0:
                            t = j * NT + s
                            act.wait_ge(c_turned, t + 1)
                            if t >= 2:
                                act.wait_ge(prob_ready, (t - 1) * HEADS)
                            nc.scalar.activation(cnt[:, t % 2, :], flatC[:, 0:BW], ACT.Copy).then_inc(c_kept, 1)
                        act.wait_ge(clipped, n + 1)
                        w = work[:, m % W_BUFS, :]
                        nc.scalar.activation(w, w, ACT.Exp).then_inc(exp_ready, 1)
                    act.wait_ge(prob_used, (j + 1) * UNITS)
                    nc.scalar.activation(o_sb[:].rearrange("p (f c) -> p f c", f=2), psO[:, :, 0:HW], ACT.Copy).then_inc(o_kept, 1)

            @block.vector
            def _(dve):
                LAG = 1
                for j in range(NB):
                    for m in range(UNITS + LAG):
                        if m < UNITS:
                            n = j * UNITS + m
                            dve.wait_ge(s_ready, n + 1)
                            free = n - W_BUFS + 1 if m >= W_BUFS else j * UNITS
                            if free > 0:
                                dve.wait_ge(prob_used, free)
                            nc.vector.tensor_scalar(work[:, m % W_BUFS, :].rearrange("p (f c) -> p f c", f=2), psS[:, m % 2, :, 0:HW],
                                                    -10.0, 10.0, ALU.max, ALU.min).then_inc(clipped, 1)
                        if m >= LAG:
                            k = m - LAG
                            s = k // HEADS
                            t = j * NT + s
                            dve.wait_ge(exp_ready, j * UNITS + k + 1)
                            w = work[:, k % W_BUFS, :]
                            nc.vector.tensor_tensor(w, w, cnt[:, t % 2, :], ALU.mult).then_inc(prob_ready, 1)
                    dve.wait_ge(o_turned, j + 1)
                    step = Chain(dve, out_steps, j * 5)
                    o = flatC[:, 0:BW].rearrange("p (q h c) -> p q h c", h=HEADS, c=VW)
                    yb = y[:, j * BT:(j + 1) * BT, :]
                    step(nc.vector.tensor_scalar(rden[:], o[:, :, :, DH], 1e-8, None, ALU.add))
                    step(nc.vector.reciprocal(rden[:], rden[:]))
                    for h in range(HEADS):
                        last = nc.vector.tensor_tensor(yb[:, :, h * DH:(h + 1) * DH], o[:, :, h, 0:DH],
                                                       rden[:, :, h:h + 1].to_broadcast([P, BT, DH]), ALU.mult)
                    step(last)
                    step(nc.vector.tensor_tensor(yb, yb, x[:, j * BT:(j + 1) * BT, :], ALU.add))
                    dve.sem_inc(out_steps, 1)


def edge_messages(nc, a, x, ident, tables, xtab, aggr):
    ctx = ExitStack()
    with ctx:
        ctx.enter_context(nc.cleanup_on_exit())
        sb = lambda n, s, d=f32: ctx.enter_context(nc.sbuf_tensor("em" + n, s, d))
        sem = lambda n: nc.alloc_semaphore("em" + n)
        dst_f = sb("dst_f", [P, ET])
        src_i = sb("src_i", [P, ET], i32)
        dst_slot = sb("dst_slot", [P, ET], i32)
        xe = sb("xe", [P, NT, D])
        be = sb("be", [P, D])
        we = sb("we", [P, 4, D])
        feat = sb("feat", [P, 2, G, ED])
        featT = sb("featT", [P, 2, P])
        src_st = sb("src_st", [P, 2, G], i32)
        dst_stage = sb("dst_stage", [P, 2, G], i32)
        key_st = sb("key_st", [P, 2, G])
        xg = sb("xg", [P, 2, G, D])
        msg = sb("msg", [P, 2, 4, D])
        same = sb("same", [P, 2, 4, P])
        sums = sb("sums", [P, 2, G, D])
        ps_f = ctx.enter_context(nc.psum_tensor("emps_f", [P, 2, 512], f32))
        ps_k = ctx.enter_context(nc.psum_tensor("emps_k", [P, 2, 512], f32))
        ps_m = ctx.enter_context(nc.psum_tensor("emps_m", [P, 2, 512], f32))
        ps_s = ctx.enter_context(nc.psum_tensor("emps_s", [P, 2, 512], f32))
        be_loaded, xe_made, x_stored, we_cleared, we_loaded = (sem(n) for n in ("be_loaded", "xe_made", "x_stored", "we_cleared", "we_loaded"))
        feat_loaded = [sem(f"feat_loaded{h}") for h in range(2)]
        gathered = [[sem(f"gathered{h}_{c}") for c in range(NC)] for h in range(2)]
        added = [sem(f"added{w}") for w in range(2)]
        feat_turned, feat_kept, key_turned, same_ready, pre_ready, msg_ready, sum_ready, sum_kept, turn = (
            sem(n) for n in ("feat_turned", "feat_kept", "key_turned", "same_ready", "pre_ready", "msg_ready", "sum_ready", "sum_kept", "turn"))
        tables_loaded = sem("tables_loaded")
        raw_ready, src_staged, dst_staged, key_staged = (sem(n) for n in ("raw_ready", "src_staged", "dst_staged", "key_staged"))
        LASTI = NG // 2 - 1
        FULL_TURNS = EREST // G // 2
        assert FULL_TURNS * 2 == EREST // G

        def landed(i, half, c):
            w = c % 2
            return i * (32 * SET_TILES[w]) + 16 * (half * SET_TILES[w] + sum(n for _, n in CHUNKS[w:c:2]))

        def before_last(i, half, w):
            return i * (32 * SET_TILES[w]) - (1 - half) * 16 * SET_TILES[w]

        with nc.Block() as block:
            @block.sync
            def _(sp):
                sp.dma_start(be[:], bcast_rows(a["L3_gnn_be"], P)).then_inc(be_loaded, 16)
                for name, t in (("dst_f", dst_f), ("src_i", src_i), ("dst_slot", dst_slot)):
                    sp.dma_start(t[:], tables[name][:, :]).then_inc(tables_loaded, 16)
                sp.wait_ge(we_cleared, 1)
                for g in range(4):
                    sp.dma_start(we[g * ED:(g + 1) * ED, g, :], a["L3_gnn_We"]).then_inc(we_loaded, 16)
                flat = a["edge_attr_32"].rearrange("e k -> (e k)")
                most = flat[0:(P - 1) * ET * ED].rearrange("(p f) -> p f", f=ET * ED)
                rest = flat[(P - 1) * ET * ED:E * ED].rearrange("(p f) -> p f", p=1)

                def load(i, half, last_group, n):
                    sp.wait_ge(feat_turned, i * (2 * NC) + (half + 1) * NC)
                    dst = feat[:, half, :, :].rearrange("p t k -> p (t k)")
                    for lo, hi in ((0, 112), (112, P - 1)):
                        sp.dma_start(dst[lo:hi, :], most[lo:hi, bass.ds((2 * i + half) * (G * ED), G * ED)]).then_inc(feat_loaded[half], 16)
                    sp.dma_start(dst[P - 1:P, 0:n * ED], rest[:, bass.ds(last_group * (G * ED), n * ED)]).then_inc(feat_loaded[half], 16)

                with sp.Fori(0, FULL_TURNS) as i:
                    for half in range(2):
                        load(i, half, 2 * i + half, G)
                for i in range(FULL_TURNS, NG // 2):
                    for half in range(2):
                        g = 2 * i + half
                        n = min(G, EREST - g * G)
                        load(i, half, g if n > 0 else 0, n if n > 0 else G)

            @block.gpsimd
            def _(pool):
                def gather(half, c, j):
                    nc.gpsimd.indirect_dma_start(xg[:, half, j, :], None, xtab[:, :],
                                                 bass.IndirectOffsetOnAxis(ap=src_st[:, half, j:j + 1], axis=0)).then_inc(gathered[half][c], 16)

                def body(i, last=False):
                    for half in range(2):
                        g = 2 * i + half
                        ahead = not (last and half == 1)
                        if ahead:
                            held(pool, turn, src_staged, g + 2)
                            held(pool, turn, raw_ready, 4 * g)
                        held(pool, turn, dst_staged, g + 1)
                        for c, (lo, n) in enumerate(CHUNKS):
                            for j in range(lo, lo + n):
                                if ahead:
                                    gather(1 - half, c, j)
                                if j == lo:
                                    held(pool, turn, sum_kept, NC * g + c + 1)
                                    held(pool, turn, added[c % 2], landed(i, half, c))
                                k = (c % 2) * SET_SUMS[0] + j - lo
                                nc.gpsimd.indirect_dma_start(aggr[k][:, :], bass.IndirectOffsetOnAxis(ap=dst_stage[:, half, j:j + 1], axis=0),
                                                             sums[:, half, j, :], None, compute_op=ALU.add).then_inc(added[c % 2], 16)

                pool.wait_ge(x_stored, 16)
                pool.wait_ge(src_staged, 1)
                for c, (lo, n) in enumerate(CHUNKS):
                    for j in range(lo, lo + n):
                        gather(0, c, j)
                body(0)
                with pool.Fori(1, LASTI) as i:
                    body(i)
                body(LASTI, last=True)
                for w in range(2):
                    pool.wait_ge(added[w], 16 * SET_TILES[w] * NG)

            @block.scalar
            def _(act):
                act.wait_ge(xe_made, 1)
                act.dma_start(xtab[:, :].rearrange("(t p) d -> p t d", p=P), xe[:]).then_inc(x_stored, 16)

                def body(i):
                    for half in range(2):
                        for c, (lo, n) in enumerate(CHUNKS):
                            u, v = c % 2, 2 * NC * i + half * NC + c
                            act.wait_ge(feat_turned, v + 2 * NC + 1)
                            wait(act, pre_ready, v - 1)
                            nc.scalar.activation(featT[0:n * ED, u, :], ps_f[0:n * ED, u, 0:P], ACT.Copy).then_inc(feat_kept, 1)
                            act.wait_ge(raw_ready, v + 1)
                            nc.scalar.activation(msg[:, u, 0:n, :], msg[:, u, 0:n, :], ACT.Relu).then_inc(msg_ready, 1)
                            if c == 0:
                                for w in range(2):
                                    wait(act, added[w], before_last(i, half, w))
                            act.wait_ge(sum_ready, v + 1)
                            nc.scalar.activation(sums[:, half, lo:lo + n, :].rearrange("p t d -> p (t d)"), ps_s[:, u, 0:n * D], ACT.Copy).then_inc(sum_kept, 1)

                turns(act, NG // 2, body)

            @block.vector
            def _(dve):
                dve.sem_inc(feat_turned, 2 * NC)
                nc.vector.memset(we[:], 0.0).then_inc(we_cleared, 1)
                dve.wait_ge(be_loaded, 16)
                nc.vector.tensor_tensor(xe[:], x[:], be[:].unsqueeze(1).to_broadcast([P, NT, D]), ALU.add).then_inc(xe_made, 1)
                dve.wait_ge(tables_loaded, 48)
                for half in range(2):
                    nc.vector.tensor_copy(src_st[:, half, :], src_i[:, half * G:(half + 1) * G]).then_inc(src_staged, 1)

                def body(i, last=False):
                    for half in range(2):
                        g = 2 * i + half
                        group = bass.ds(g * G, G)
                        held(dve, turn, key_turned, NC * (g - 1) if not isinstance(g, int) or g > 1 else 0)
                        nc.vector.tensor_copy(key_st[:, half, :], dst_f[:, group]).then_inc(key_staged, 1)
                        for w in range(2):
                            held(dve, turn, added[w], before_last(i, half, w))
                        nc.vector.tensor_copy(dst_stage[:, half, :], dst_slot[:, group]).then_inc(dst_staged, 1)
                        dve.wait_ge(key_staged, g + 1)
                        for c, (lo, n) in enumerate(CHUNKS):
                            u, v = c % 2, 2 * NC * i + half * NC + c
                            dve.wait_ge(key_turned, v + 1)
                            wait(dve, sum_ready, v - 1)
                            nc.vector.tensor_tensor(same[:, u, 0:n, :], ps_k[:, u, 0:n * P].rearrange("p (t c) -> p t c", c=P),
                                                    key_st[:, half, lo:lo + n].unsqueeze(2).to_broadcast([P, n, P]), ALU.is_equal).then_inc(same_ready, 1)
                            dve.wait_ge(gathered[half][c], 16 * n * i + 16 * n)
                            dve.wait_ge(pre_ready, v + 1)
                            nc.vector.tensor_tensor(msg[:, u, 0:n, :], ps_m[:, u, 0:n * D].rearrange("p (t d) -> p t d", d=D),
                                                    xg[:, half, lo:lo + n, :], ALU.add).then_inc(raw_ready, 1)
                        if not last:
                            nc.vector.tensor_copy(src_st[:, half, :], src_i[:, bass.ds((g + 2) * G, G)]).then_inc(src_staged, 1)

                body(0)
                with dve.Fori(1, LASTI) as i:
                    body(i)
                body(LASTI, last=True)

            @block.tensor
            def _(pe):
                pe.wait_ge(we_loaded, 64)

                def body(i):
                    for half in range(2):
                        g = 2 * i + half
                        for c, (lo, n) in enumerate(CHUNKS):
                            u, v = c % 2, 2 * NC * i + half * NC + c
                            if c == 0:
                                pe.wait_ge(feat_loaded[half], 48 * i + 48)
                                pe.wait_ge(key_staged, g + 1)
                            wait(pe, feat_kept, v - 1)
                            nc.tensor.transpose(ps_f[0:n * ED, u, 0:P], feat[:, half, lo:lo + n, :].rearrange("p t k -> p (t k)"), ident[:]).then_inc(feat_turned, 1)
                            wait(pe, same_ready, v - 1)
                            for j in range(n):
                                last = nc.tensor.transpose(ps_k[:, u, j * P:(j + 1) * P], key_st[:, half, lo + j:lo + j + 1].to_broadcast([P, P]), ident[:])
                            last.then_inc(key_turned, 1)
                            pe.wait_ge(feat_kept, v + 1)
                            wait(pe, raw_ready, v - 1)
                            nc.tensor.matmul(ps_m[:, u, 0:n * D], featT[0:n * ED, u, :], we[0:n * ED, 0:n, :].rearrange("p t d -> p (t d)"),
                                             start=True, stop=True).then_inc(pre_ready, 1)
                            pe.wait_ge(same_ready, v + 1)
                            pe.wait_ge(msg_ready, v + 1)
                            wait(pe, sum_kept, v - 1)
                            for j in range(n):
                                last = nc.tensor.matmul(ps_s[:, u, j * D:(j + 1) * D], same[:, u, j, :], msg[:, u, j, :], start=True, stop=True)
                            last.then_inc(sum_ready, 1)

                turns(pe, NG // 2, body)


def gather_sums(nc, x, y, ident, xT, aggr):
    ctx = ExitStack()
    with ctx:
        ctx.enter_context(nc.cleanup_on_exit())
        part = ctx.enter_context(nc.sbuf_tensor("part", [P, KA, NT, D], f32))
        loaded, steps = [nc.alloc_semaphore(f"part_loaded{k}") for k in range(KA)], nc.alloc_semaphore("part_steps")
        with nc.Block() as block:
            @block.sync
            def _(sp):
                for k in range(KA):
                    sp.dma_start(part[:, k, :, :], aggr[k][0:NP, :].rearrange("(t p) d -> p t d", p=P)).then_inc(loaded[k], 16)

            @block.vector
            def _(dve):
                step = Chain(dve, steps)
                for k in range(KA):
                    dve.wait_ge(loaded[k], 16)
                    step(nc.vector.tensor_tensor(y[:], y[:] if k else x[:], part[:, k], ALU.add))
    transpose_and_project(nc, "gs", y, ident, xT)


def store(nc, x, out):
    with nc.semaphore("stored") as stored, nc.Block() as block:
        @block.sync
        def _(sp):
            sp.dma_start(out[0:NFULL * P, :].rearrange("(t p) d -> p t d", p=P), x[:, 0:NFULL, :]).then_inc(stored, 16)
            sp.dma_start(out[NFULL * P:N, :], x[0:NREST, NFULL, :]).then_inc(stored, 16)
            sp.wait_ge(stored, 32)


_INS = ['x', 'src', 'dst', 'edge_attr_32', 'L0_gnn_W', 'L0_gnn_att_src', 'L0_gnn_att_dst', 'L0_gnn_bias',
        'L1_gnn_W1', 'L1_gnn_b1', 'L1_gnn_W2', 'L1_gnn_b2', 'L1_gnn_gamma', 'L1_gnn_beta', 'L1_gnn_eps',
        'L2_gnn_qW', 'L2_gnn_kW', 'L2_gnn_vW', 'L3_gnn_We', 'L3_gnn_be', 'L3_gnn_W1', 'L3_gnn_b1',
        'L3_gnn_W2', 'L3_gnn_b2', 'L3_gnn_gamma', 'L3_gnn_beta']


def kernel(**inputs):
    import numpy as _np
    import concourse.bacc as _bacc
    from concourse import mybir as _mybir
    from concourse.bass_utils import run_bass_kernel_spmd as _run

    nc = _bacc.Bacc("TRN2", target_bir_lowering=False, num_devices=1)
    arrays, args = {}, {}
    for name in _INS:
        a = _np.ascontiguousarray(inputs[name])
        arrays[f"in_{name}_dram"] = a
        args[name] = nc.dram_tensor(f"in_{name}_dram", a.shape, _mybir.dt.from_np(a.dtype), kind="ExternalInput").ap()
    out = nc.dram_tensor("out_dram", (N, D), _mybir.dt.float32, kind="ExternalOutput").ap()
    program(nc, args, out)
    r = _run(nc, [arrays], core_ids=[0])
    return r.results[0]["out_dram"]
```
